# Optimizing a Trainium2 kernel written in Bass

```python
import numpy as np
import jax
import jax.numpy as jnp

def _softmax(x, axis=-1):
    return jax.nn.softmax(x, axis=axis)
def _gelu(x):
    return jax.nn.gelu(x, approximate=True)
def _silu(x):
    return jax.nn.silu(x)
def _sigmoid(x):
    return jax.nn.sigmoid(x)
def _layernorm(x, axis=-1, eps=1e-5):
    m = jnp.mean(x, axis=axis, keepdims=True)
    v = jnp.var(x, axis=axis, keepdims=True)
    return (x - m) / jnp.sqrt(v + eps)
def _scatter_add(tgt, idx, src, axis=0):
    return tgt.at[idx].add(src)
def _segment_sum(src, seg, n):
    return jax.ops.segment_sum(src, seg, n)

kernel_name = 'mk_dlrm_tower_d1_rec_e3d1f9'

def setup_inputs(seed: int = 0):
    np.random.seed(seed)
    _w = jnp.asarray
    def _rec_inputs():
        import jax
        import jax.numpy as jnp
        _tk = jax.random.key(seed)
        ids = jnp.stack([jax.random.randint(jax.random.fold_in(_tk, 200 + f), (1024,), 0, v, jnp.int32) for f, v in enumerate([100000, 10000, 10000, 1000000])], axis=1)
        tbl_0 = 0.05 * jax.random.normal(jax.random.fold_in(_tk, 500 + 0), (100000, 4), jnp.float32)
        tbl_1 = 0.05 * jax.random.normal(jax.random.fold_in(_tk, 500 + 1), (10000, 4), jnp.float32)
        tbl_2 = 0.05 * jax.random.normal(jax.random.fold_in(_tk, 500 + 2), (10000, 4), jnp.float32)
        tbl_3 = 0.05 * jax.random.normal(jax.random.fold_in(_tk, 500 + 3), (1000000, 4), jnp.float32)
        _rk = jax.random.fold_in(_tk, 7)
        r_x = 7.22013e-05 + 1.00017 * jax.random.normal(jax.random.fold_in(_rk, 101), (1024, 2048), jnp.float32)
        W_top1 = 0.0197642 * jax.random.normal(jax.random.fold_in(_tk, 801), (2560, 512), jnp.float32)
        W_top2 = 0.0441942 * jax.random.normal(jax.random.fold_in(_tk, 802), (512, 256), jnp.float32)
        W_top3 = 0.0625 * jax.random.normal(jax.random.fold_in(_tk, 803), (256, 1), jnp.float32)
        b_top1 = jnp.zeros((512,), jnp.float32)
        b_top2 = jnp.zeros((256,), jnp.float32)
        return r_x, ids, tbl_0, tbl_1, tbl_2, tbl_3, W_top1, b_top1, W_top2, b_top2, W_top3
    r_x, ids, tbl_0, tbl_1, tbl_2, tbl_3, W_top1, b_top1, W_top2, b_top2, W_top3 = _rec_inputs()
    def _L0_rec_setup():
        import jax, jax.numpy as jnp
        import numpy as np
        B, IN, HID, D, N, OUT = (4096, 2048, 2048, 512, 4, 512)
        H = 8
        HD = D // H

        def _ln(x, g, b):
            m = x.mean(-1, keepdims=True)
            v = ((x - m) ** 2).mean(-1, keepdims=True)
            return (x - m) / jnp.sqrt(v + 1e-05) * g + b
        key = jax.random.key(seed)
        ks = jax.random.split(key, 32)

        def nrm(k, shape, scale=0.02):
            return jax.random.normal(k, shape, jnp.float32) * scale
        inp = {}
        inp['x'] = jax.random.normal(ks[0], (B, IN), jnp.float32)
        inp['strength'] = jax.random.uniform(ks[1], (B, N, N), jnp.float32)
        for t, i in (('er', 2), ('ei', 4)):
            inp[t + '_W1'] = nrm(ks[i], (HID, IN))
            inp[t + '_b1'] = jnp.zeros((HID,), jnp.float32)
            inp[t + '_g1'] = jnp.ones((HID,), jnp.float32)
            inp[t + '_be1'] = jnp.zeros((HID,), jnp.float32)
            inp[t + '_W2'] = nrm(ks[i + 1], (N * D, HID))
            inp[t + '_b2'] = jnp.zeros((N * D,), jnp.float32)
        names = ['Wq_r', 'Wq_i', 'Wk_r', 'Wk_i', 'Wv_r', 'Wv_i', 'Wo_r', 'Wo_i']
        for j, nm in enumerate(names):
            inp[nm] = nrm(ks[6 + j], (D, D))
            inp['b' + nm[1:]] = jnp.zeros((D,), jnp.float32)
        inp['int_Wr'] = jnp.tile(jnp.eye(D, dtype=jnp.float32)[None], (N, 1, 1))
        inp['int_Wi'] = jnp.zeros((N, D, D), jnp.float32)
        inp['meas_Mr'] = nrm(ks[20], (OUT, D), 1.0 / np.sqrt(D))
        inp['meas_Mi'] = nrm(ks[21], (OUT, D), 1.0 / np.sqrt(D))
        inp['post_W'] = nrm(ks[22], (OUT, OUT))
        inp['post_b'] = jnp.zeros((OUT,), jnp.float32)
        inp['post_g'] = jnp.ones((OUT,), jnp.float32)
        inp['post_be'] = jnp.zeros((OUT,), jnp.float32)
        return inp
    _L0_rec_all = _L0_rec_setup()
    _L0_rec_in = {k: v for k, v in _L0_rec_all.items() if k in ('er_W1', 'er_b1', 'er_g1', 'er_be1', 'er_W2', 'er_b2', 'ei_W1', 'ei_b1', 'ei_g1', 'ei_be1', 'ei_W2', 'ei_b2', 'Wq_r', 'bq_r', 'Wq_i', 'bq_i', 'Wk_r', 'bk_r', 'Wk_i', 'bk_i', 'Wv_r', 'bv_r', 'Wv_i', 'bv_i', 'Wo_r', 'bo_r', 'Wo_i', 'bo_i', 'int_Wr', 'int_Wi', 'meas_Mr', 'meas_Mi', 'post_W', 'post_b', 'post_g', 'post_be', )}
    del _L0_rec_all

    return {
        "r_x": r_x,
        "ids": ids,
        "tbl_0": tbl_0,
        "tbl_1": tbl_1,
        "tbl_2": tbl_2,
        "tbl_3": tbl_3,
        "W_top1": W_top1,
        "b_top1": b_top1,
        "W_top2": W_top2,
        "b_top2": b_top2,
        "W_top3": W_top3,
        "L0_rec_er_W1": _L0_rec_in["er_W1"],
        "L0_rec_er_b1": _L0_rec_in["er_b1"],
        "L0_rec_er_g1": _L0_rec_in["er_g1"],
        "L0_rec_er_be1": _L0_rec_in["er_be1"],
        "L0_rec_er_W2": _L0_rec_in["er_W2"],
        "L0_rec_er_b2": _L0_rec_in["er_b2"],
        "L0_rec_ei_W1": _L0_rec_in["ei_W1"],
        "L0_rec_ei_b1": _L0_rec_in["ei_b1"],
        "L0_rec_ei_g1": _L0_rec_in["ei_g1"],
        "L0_rec_ei_be1": _L0_rec_in["ei_be1"],
        "L0_rec_ei_W2": _L0_rec_in["ei_W2"],
        "L0_rec_ei_b2": _L0_rec_in["ei_b2"],
        "L0_rec_Wq_r": _L0_rec_in["Wq_r"],
        "L0_rec_bq_r": _L0_rec_in["bq_r"],
        "L0_rec_Wq_i": _L0_rec_in["Wq_i"],
        "L0_rec_bq_i": _L0_rec_in["bq_i"],
        "L0_rec_Wk_r": _L0_rec_in["Wk_r"],
        "L0_rec_bk_r": _L0_rec_in["bk_r"],
        "L0_rec_Wk_i": _L0_rec_in["Wk_i"],
        "L0_rec_bk_i": _L0_rec_in["bk_i"],
        "L0_rec_Wv_r": _L0_rec_in["Wv_r"],
        "L0_rec_bv_r": _L0_rec_in["bv_r"],
        "L0_rec_Wv_i": _L0_rec_in["Wv_i"],
        "L0_rec_bv_i": _L0_rec_in["bv_i"],
        "L0_rec_Wo_r": _L0_rec_in["Wo_r"],
        "L0_rec_bo_r": _L0_rec_in["bo_r"],
        "L0_rec_Wo_i": _L0_rec_in["Wo_i"],
        "L0_rec_bo_i": _L0_rec_in["bo_i"],
        "L0_rec_int_Wr": _L0_rec_in["int_Wr"],
        "L0_rec_int_Wi": _L0_rec_in["int_Wi"],
        "L0_rec_meas_Mr": _L0_rec_in["meas_Mr"],
        "L0_rec_meas_Mi": _L0_rec_in["meas_Mi"],
        "L0_rec_post_W": _L0_rec_in["post_W"],
        "L0_rec_post_b": _L0_rec_in["post_b"],
        "L0_rec_post_g": _L0_rec_in["post_g"],
        "L0_rec_post_be": _L0_rec_in["post_be"],
    }

def reference(r_x, ids, tbl_0, tbl_1, tbl_2, tbl_3, W_top1, b_top1, W_top2, b_top2, W_top3, L0_rec_er_W1, L0_rec_er_b1, L0_rec_er_g1, L0_rec_er_be1, L0_rec_er_W2, L0_rec_er_b2, L0_rec_ei_W1, L0_rec_ei_b1, L0_rec_ei_g1, L0_rec_ei_be1, L0_rec_ei_W2, L0_rec_ei_b2, L0_rec_Wq_r, L0_rec_bq_r, L0_rec_Wq_i, L0_rec_bq_i, L0_rec_Wk_r, L0_rec_bk_r, L0_rec_Wk_i, L0_rec_bk_i, L0_rec_Wv_r, L0_rec_bv_r, L0_rec_Wv_i, L0_rec_bv_i, L0_rec_Wo_r, L0_rec_bo_r, L0_rec_Wo_i, L0_rec_bo_i, L0_rec_int_Wr, L0_rec_int_Wi, L0_rec_meas_Mr, L0_rec_meas_Mi, L0_rec_post_W, L0_rec_post_b, L0_rec_post_g, L0_rec_post_be):
    import jax
    import jax.numpy as jnp
    def _L0_rec_ref(x, strength, er_W1, er_b1, er_g1, er_be1, er_W2, er_b2, ei_W1, ei_b1, ei_g1, ei_be1, ei_W2, ei_b2, Wq_r, bq_r, Wq_i, bq_i, Wk_r, bk_r, Wk_i, bk_i, Wv_r, bv_r, Wv_i, bv_i, Wo_r, bo_r, Wo_i, bo_i, int_Wr, int_Wi, meas_Mr, meas_Mi, post_W, post_b, post_g, post_be):
        import jax, jax.numpy as jnp
        import numpy as np
        B, IN, HID, D, N, OUT = (4096, 2048, 2048, 512, 4, 512)
        H = 8
        HD = D // H

        def _ln(x, g, b):
            m = x.mean(-1, keepdims=True)
            v = ((x - m) ** 2).mean(-1, keepdims=True)
            return (x - m) / jnp.sqrt(v + 1e-05) * g + b
        Bsz = x.shape[0]

        def enc(W1, b1, g, be, W2, b2):
            h = jax.nn.gelu(_ln(x @ W1.T + b1, g, be), approximate=False)
            return (h @ W2.T + b2).reshape(Bsz, N, D)
        sr = enc(er_W1, er_b1, er_g1, er_be1, er_W2, er_b2)
        si = enc(ei_W1, ei_b1, ei_g1, ei_be1, ei_W2, ei_b2)

        def heads(t):
            return t.reshape(Bsz, N, H, HD).transpose(0, 2, 1, 3)
        qr = heads(sr @ Wq_r.T + bq_r)
        qi = heads(si @ Wq_i.T + bq_i)
        kr = heads(sr @ Wk_r.T + bk_r)
        ki = heads(si @ Wk_i.T + bk_i)
        vr = heads(sr @ Wv_r.T + bv_r)
        vi = heads(si @ Wv_i.T + bv_i)
        ar = jnp.einsum('bhnd,bhmd->bhnm', qr, kr) + jnp.einsum('bhnd,bhmd->bhnm', qi, ki)
        ai = jnp.einsum('bhnd,bhmd->bhnm', qi, kr) - jnp.einsum('bhnd,bhmd->bhnm', qr, ki)
        mag = jnp.sqrt(ar ** 2 + ai ** 2 + 1e-08) * HD ** (-0.5)
        w = jax.nn.softmax(mag, axis=-1)
        out_r = jnp.einsum('bhnm,bhmd->bhnd', w, vr).transpose(0, 2, 1, 3).reshape(Bsz, N, D)
        out_i = jnp.einsum('bhnm,bhmd->bhnd', w, vi).transpose(0, 2, 1, 3).reshape(Bsz, N, D)
        attn_r = out_r @ Wo_r.T + bo_r
        attn_i = out_i @ Wo_i.T + bo_i
        R = jnp.einsum('bnd,ned->bne', attn_r, int_Wr) - jnp.einsum('bnd,ned->bne', attn_i, int_Wi)
        I = jnp.einsum('bnd,ned->bne', attn_r, int_Wi) + jnp.einsum('bnd,ned->bne', attn_i, int_Wr)
        Ri, Ii = (R[:, :, None, :], I[:, :, None, :])
        Rj, Ij = (R[:, None, :, :], I[:, None, :, :])
        phase = jnp.arctan2(Ii * Rj - Ri * Ij, Ri * Rj + Ii * Ij)
        f = jnp.cos(phase) * strength[..., None]
        sup_r = jnp.einsum('bijd,bjd->bd', f, R)
        sup_i = jnp.einsum('bijd,bjd->bd', f, I)
        norm = jnp.sqrt(jnp.sum(sup_r ** 2 + sup_i ** 2, axis=-1, keepdims=True) + 1e-08)
        sup_r = sup_r / norm
        sup_i = sup_i / norm
        mr = sup_r @ meas_Mr.T - sup_i @ meas_Mi.T
        mi = sup_r @ meas_Mi.T + sup_i @ meas_Mr.T
        amp = jnp.sqrt(mr ** 2 + mi ** 2)
        out = jax.nn.gelu(_ln(amp @ post_W.T + post_b, post_g, post_be), approximate=False)
        return out

    e = jnp.stack([tbl_0[ids[:, 0]], tbl_1[ids[:, 1]], tbl_2[ids[:, 2]], tbl_3[ids[:, 3]]], axis=1)
    z = _L0_rec_ref(r_x, e, L0_rec_er_W1, L0_rec_er_b1, L0_rec_er_g1, L0_rec_er_be1, L0_rec_er_W2, L0_rec_er_b2, L0_rec_ei_W1, L0_rec_ei_b1, L0_rec_ei_g1, L0_rec_ei_be1, L0_rec_ei_W2, L0_rec_ei_b2, L0_rec_Wq_r, L0_rec_bq_r, L0_rec_Wq_i, L0_rec_bq_i, L0_rec_Wk_r, L0_rec_bk_r, L0_rec_Wk_i, L0_rec_bk_i, L0_rec_Wv_r, L0_rec_bv_r, L0_rec_Wv_i, L0_rec_bv_i, L0_rec_Wo_r, L0_rec_bo_r, L0_rec_Wo_i, L0_rec_bo_i, L0_rec_int_Wr, L0_rec_int_Wi, L0_rec_meas_Mr, L0_rec_meas_Mi, L0_rec_post_W, L0_rec_post_b, L0_rec_post_g, L0_rec_post_be)
    z = z.reshape(z.shape[0], -1)
    h = jnp.concatenate([z, r_x], axis=1)
    h = jnp.maximum(h @ W_top1 + b_top1, 0.0)
    h = jnp.maximum(h @ W_top2 + b_top2, 0.0)
    y = h @ W_top3
    return y


_drawn_inputs = setup_inputs


def setup_inputs(seed=0):
    import zlib

    import numpy as np

    out = dict(_drawn_inputs(seed))
    spreads = {'b_top1': (0.0, 0.1),
     'b_top2': (0.0, 0.1),
     'L0_rec_er_b1': (0.0, 0.8),
     'L0_rec_er_g1': (1.0, 0.6),
     'L0_rec_er_be1': (0.0, 0.8),
     'L0_rec_er_b2': (0.0, 0.8),
     'L0_rec_ei_b1': (0.0, 0.8),
     'L0_rec_ei_g1': (1.0, 0.6),
     'L0_rec_ei_be1': (0.0, 0.8),
     'L0_rec_ei_b2': (0.0, 0.8),
     'L0_rec_bq_r': (0.0, 0.8),
     'L0_rec_bq_i': (0.0, 0.8),
     'L0_rec_bk_r': (0.0, 0.8),
     'L0_rec_bk_i': (0.0, 0.8),
     'L0_rec_bv_r': (0.0, 0.1),
     'L0_rec_bv_i': (0.0, 0.1),
     'L0_rec_bo_r': (0.0, 0.1),
     'L0_rec_bo_i': (0.0, 0.1),
     'L0_rec_int_Wi': (0.0, 0.1),
     'L0_rec_post_b': (0.0, 0.1),
     'L0_rec_post_g': (1.0, 0.2),
     'L0_rec_post_be': (0.0, 0.1)}
    factors = {'L0_rec_Wq_r': 8.0, 'L0_rec_Wq_i': 8.0, 'L0_rec_Wk_r': 8.0, 'L0_rec_Wk_i': 8.0}
    for name, (base, spread) in spreads.items():
        noise = np.random.default_rng([zlib.crc32(name.encode()), seed]).standard_normal(out[name].shape)
        drawn = base * np.exp(spread * noise) if base else spread * noise
        out[name] = jnp.asarray(drawn.astype(out[name].dtype))
    for name, factor in factors.items():
        out[name] = (out[name] * factor).astype(out[name].dtype)
    return out
```

```python
from contextlib import ExitStack

import concourse.bass as bass
import numpy as np
from concourse import mybir

ALU = mybir.AluOpType
ACT = mybir.ActivationFunctionType
AX_X = mybir.AxisListType.X
F32 = mybir.dt.float32
F32R = mybir.dt.float32r
U32 = mybir.dt.uint32

P = 128
B = 1024
HB = 512
HALVES = B // HB
BT = B // P
K = 2048
FT = K // P
D = 512
DT = D // P
N = 4
H = 8
HD = D // H
HP = H // 2
LN_EPS = 1e-5
MAG_EPS = 1e-8
VEC_B1, VEC_G, VEC_BE, VEC_B2 = 0, 2, 4, 6


def mm3(nc, out, w, x, start, stop, **more):
    (w_hi, w_lo), (x_hi, x_lo) = w, x
    nc.tensor.matmul(out, w_hi, x_hi, start=start, stop=False, **more)
    nc.tensor.matmul(out, w_hi, x_lo, start=False, stop=False, **more)
    return nc.tensor.matmul(out, w_lo, x_hi, start=False, stop=stop, **more)


def low_part(engine, lo, full, hi):
    return engine.tensor_tensor(lo, full, hi.bitcast(F32), ALU.subtract)


def encoder_stage(nc, xT, w_enc, enc_vec, b_top1, s_dram, t_dram):
    CK = 8
    CHUNKS = FT // CK
    L1_R, TOP, L1_I, L2_R, L2_I = range(5)
    TILES = [FT, DT, FT, FT, FT]
    START = [sum(TILES[:g]) for g in range(5)]
    HT = sum(TILES)
    HC = HT * CHUNKS
    PAIRS = HC // 2
    ENC = {L1_R: 0, L1_I: 1, L2_R: 0, L2_I: 1}
    OUT_START = {TOP: 0, L2_R: DT, L2_I: DT + FT}
    OUT_TILES = DT + 2 * FT

    with ExitStack() as ctx:
        def sb(name, shape, dt):
            return ctx.enter_context(nc.sbuf_tensor(name, shape, dt))

        def sem(name):
            return ctx.enter_context(nc.semaphore(name))

        x_hi = sb("x_hi", [P, FT, HB], F32R)
        x_lo = sb("x_lo", [P, FT, HB], F32R)
        h_lo = sb("h_lo", [P, FT, HB], F32R)
        h_hi = sb("h_hi", [P, FT, HB], F32R)
        pre_r = nc.alloc_sbuf_tensor_at("pre_r", [P, FT, HB], F32, offset=nc.sbuf_base - FT * HB * 4)
        pre_i = sb("pre_i", [P, FT, HB], F32)
        w_raw = sb("w_raw", [P, 2, CK, P], F32)
        w_hi = sb("w_hi", [P, 2, CK, P], F32R)
        w_lo = sb("w_lo", [P, 2, CK, P], F32R)
        acc = sb("acc", [P, HB], F32)
        acc2 = sb("acc2", [P, HB], F32)
        rstd = sb("rstd", [P, HB], F32)
        norm = sb("norm", [P, 2, HB], F32)
        gelu = sb("gelu", [P, 2, HB], F32)
        s_out = sb("s_out", [P, 2, HB], F32)
        vec = sb("vec", [P, 8, FT], F32)
        vec_top = sb("vec_top", [P, DT], F32)
        ones = sb("ones", [P, P], F32)
        eps = sb("eps", [P, 1], F32)

        x_in = sem("x_in")
        vec_in = sem("vec_in")
        w_in = [sem("w_in_0"), sem("w_in_1")]
        consts_set = sem("consts_set")
        x_hi_made, x_lo_made = sem("x_hi_made"), sem("x_lo_made")
        w_hi_made, w_lo_made, w_used = sem("w_hi_made"), sem("w_lo_made"), sem("w_used")
        tile_out = sem("tile_out")
        cleared, summed = sem("cleared"), sem("summed")
        centred, squared, sq_summed = sem("centred"), sem("squared"), sem("sq_summed")
        stats_done, std_made, rstd_made = sem("stats_done"), sem("std_made"), sem("rstd_made")
        normed, gelu_made = sem("normed"), sem("gelu_made")
        hid_hi_made, hid_lo_made = sem("hid_hi_made"), sem("hid_lo_made")
        stored = [sem("stored_0"), sem("stored_1")]

        mm_ps = ctx.enter_context(nc.psum_tensor("enc_mm", [P, 2, HB], F32))
        st_ps = ctx.enter_context(nc.psum_tensor("enc_stats", [P, 2, HB], F32))
        moving = [(x_hi, x_lo), (x_hi, x_lo), (x_hi, x_lo), (h_hi, h_lo), (x_hi, x_lo)]
        pre = [pre_r, pre_i]
        hidden = [(h_hi, h_lo), (x_hi, x_lo)]
        BESIDE = [None, None, 0, 1, None]

        block = ctx.enter_context(nc.Block())

        @block.sync
        def _(sp):
            def load_x(h):
                for k in range(0, FT, 4):
                    sp.dma_start(pre_i[:, k:k + 4, :], xT[h, :, k:k + 4, :]).then_inc(x_in, 16)

            def load_pair(i, first, second):
                sp.wait_ge(w_lo_made, 2 * i)
                sp.dma_start(w_raw[:, 1], w_enc[first]).then_inc(w_in[1], 16)
                sp.wait_ge(w_lo_made, 2 * i + 1)
                sp.dma_start(w_raw[:, 0], w_enc[second]).then_inc(w_in[0], 16)

            sp.dma_start(vec[:], enc_vec).then_inc(vec_in, 16)
            sp.dma_start(vec_top[:], b_top1).then_inc(vec_in, 16)
            sp.dma_start(w_raw[:, 0], w_enc[0]).then_inc(w_in[0], 16)
            load_x(0)
            AHEAD = START[L2_I] * CHUNKS // 2 + 4
            with sp.Fori(0, AHEAD) as i:
                load_pair(i, 2 * i + 1, 2 * i + 2)
            sp.wait_ge(normed, 2 * FT)
            load_x(1)
            with sp.Fori(AHEAD, PAIRS - 1) as i:
                load_pair(i, 2 * i + 1, 2 * i + 2)
            load_pair(PAIRS - 1, HC - 1, 0)
            with sp.Fori(0, PAIRS - 1) as i:
                load_pair(i + PAIRS, 2 * i + 1, 2 * i + 2)
            load_pair(2 * PAIRS - 1, HC - 1, 0)

        @block.gpsimd
        def _(pool):
            nc.gpsimd.memset(ones[:], 1.0 / K).then_inc(consts_set, 1)
            nc.gpsimd.memset(eps[:], LN_EPS).then_inc(consts_set, 1)
            pool.wait_ge(w_hi_made, 1)
            low_part(nc.gpsimd, w_lo[:, 0], w_raw[:, 0], w_hi[:, 0]).then_inc(w_lo_made, 1)
            with pool.Fori(0, HALVES * PAIRS) as i:
                for slot in (1, 0):
                    pool.wait_ge(w_hi_made, 2 * i + (2 if slot else 3))
                    low_part(nc.gpsimd, w_lo[:, slot], w_raw[:, slot], w_hi[:, slot]).then_inc(w_lo_made, 1)

        @block.scalar
        def _(act):
            def high_of_chunk(c, slot, nth_in_slot):
                act.wait_ge(w_in[slot], 16 * nth_in_slot)
                act.wait_ge(w_used, c - 1)
                nc.scalar.copy(w_hi[:, slot], w_raw[:, slot]).then_inc(w_hi_made, 1)

            def square(h, e, k):
                nth = (2 * h + e) * FT + k
                act.wait_ge(centred, nth + 1)
                act.wait_ge(sq_summed, nth)
                nc.scalar.activation(norm[:, 0], pre[e][:, k, :], ACT.Square).then_inc(squared, 1)

            def gelu_tile(h, e, k, slot):
                nth = (2 * h + e) * FT + k
                act.wait_ge(normed, nth + 1)
                act.wait_ge(hid_lo_made, nth - slot)
                nc.scalar.activation(gelu[:, slot], norm[:, slot], ACT.Gelu,
                                     bias=vec[:, VEC_BE + e, bass.ds(k, 1)],
                                     scale=vec[:, VEC_G + e, bass.ds(k, 1)]).then_inc(gelu_made, 1)
                act.wait_ge(gelu_made, nth + 1)
                nc.scalar.copy(hidden[e][0][:, k, :], gelu[:, slot]).then_inc(hid_hi_made, 1)

            def tile_to_sbuf(h, g, f, slot):
                nth = h * HT + START[g] + f
                act.wait_ge(w_used, CHUNKS * (nth + 1))
                if g in (L1_R, L1_I):
                    nc.scalar.activation(pre[ENC[g]][:, f, :], mm_ps[:, slot], ACT.Identity,
                                         bias=vec[:, VEC_B1 + ENC[g], bass.ds(f, 1)]).then_inc(tile_out, 1)
                    return
                act.wait_ge(stored[slot], 8 * (h * OUT_TILES + OUT_START[g] + f - slot))
                bias = vec_top[:, bass.ds(f, 1)] if g == TOP else vec[:, VEC_B2 + ENC[g], bass.ds(f, 1)]
                nc.scalar.activation(s_out[:, slot], mm_ps[:, slot], ACT.Identity, bias=bias).then_inc(tile_out, 1)
                act.wait_ge(tile_out, nth + 1)
                to = t_dram[f] if g == TOP else s_dram[ENC[g], f]
                act.dma_start(to[:, bass.ds(h * HB, HB)], s_out[:, slot]).then_inc(stored[slot], 16)

            act.wait_ge(vec_in, 32)
            act.wait_ge(w_in[0], 16)
            nc.scalar.copy(w_hi[:, 0], w_raw[:, 0]).then_inc(w_hi_made, 1)
            with act.Fori(0, HALVES) as h:
                for k in range(FT):
                    act.wait_ge(x_in, h * 64 + 64)
                    act.wait_ge(w_used, h * HC)
                    nc.scalar.copy(x_hi[:, k, :], pre_i[:, k, :]).then_inc(x_hi_made, 1)
                for g in range(5):
                    e = BESIDE[g]
                    IT = TILES[g] // 2
                    for part in range(2):
                        if e is not None and part == 1:
                            act.wait_ge(stats_done, 4 * h + 2 * e + 2)
                            nc.scalar.activation(acc2[:], st_ps[:, 1], ACT.Sqrt, bias=eps[:]).then_inc(std_made, 1)
                        with act.Fori(part * IT // 2, (part + 1) * IT // 2) as it:
                            for j in range(2):
                                f = 2 * it + j
                                nth = h * HT + START[g] + f
                                for ch in range(CHUNKS):
                                    high_of_chunk(2 * nth + ch + 1, 1 - ch, nth + 1 + ch)
                                    k = 2 * f + ch - part * FT
                                    if e is not None and part == 0:
                                        square(h, e, k)
                                    if e is not None and part == 1:
                                        if j == 0 and ch == 0 and g == L2_R:
                                            act.wait_ge(w_used, h * HC + CHUNKS * START[L2_R])
                                        gelu_tile(h, e, k, ch)
                                tile_to_sbuf(h, g, f, j)
            for slot in range(2):
                act.wait_ge(stored[slot], 8 * HALVES * OUT_TILES)

        @block.vector
        def _(dve):
            dve.wait_ge(consts_set, 2)
            with dve.Fori(0, HALVES) as h:
                for k in range(FT):
                    dve.wait_ge(x_hi_made, h * FT + k + 1)
                    low_part(nc.vector, x_lo[:, k, :], pre_i[:, k, :], x_hi[:, k, :]).then_inc(x_lo_made, 1)
                for g in (L1_R, L1_I, L2_R):
                    e = BESIDE[g]
                    IT = TILES[g] // 2
                    if g == L1_R:
                        nc.vector.memset(acc[:], 0.0).then_inc(cleared, 1)
                    for part in range(2):
                        if e is not None and part == 0:
                            dve.wait_ge(stats_done, 4 * h + 2 * e + 1)
                            nc.vector.memset(acc[:], 0.0).then_inc(cleared, 1)
                            nc.vector.memset(acc2[:], 0.0).then_inc(cleared, 1)
                        if e is not None and part == 1:
                            dve.wait_ge(std_made, 2 * h + e + 1)
                            nc.vector.reciprocal(rstd[:], acc2[:]).then_inc(rstd_made, 1)
                        with dve.Fori(part * IT // 2, (part + 1) * IT // 2) as it:
                            for j in range(2):
                                f = 2 * it + j
                                for ch in range(CHUNKS):
                                    k = 2 * f + ch - part * FT
                                    if e is None:
                                        continue
                                    nth = (2 * h + e) * FT + k
                                    if part == 0:
                                        nc.vector.tensor_tensor(pre[e][:, k, :], pre[e][:, k, :], st_ps[:, 0],
                                                                ALU.subtract).then_inc(centred, 1)
                                        dve.wait_ge(cleared, 5 * h + 1 + 2 * e + 2)
                                        dve.wait_ge(squared, nth + 1)
                                        nc.vector.tensor_tensor(acc2[:], acc2[:], norm[:, 0],
                                                                ALU.add).then_inc(sq_summed, 1)
                                    else:
                                        dve.wait_ge(gelu_made, nth - ch)
                                        dve.wait_ge(rstd_made, 2 * h + e + 1)
                                        nc.vector.tensor_tensor(norm[:, ch], pre[e][:, k, :], rstd[:],
                                                                ALU.mult).then_inc(normed, 1)
                                        dve.wait_ge(hid_hi_made, nth + 1)
                                        low_part(nc.vector, hidden[e][1][:, k, :], gelu[:, ch],
                                                 hidden[e][0][:, k, :]).then_inc(hid_lo_made, 1)
                                if g != L2_R:
                                    dve.wait_ge(tile_out, h * HT + START[g] + f + 1)
                                    if g == L1_R:
                                        dve.wait_ge(cleared, 5 * h + 1)
                                    dve.wait_ge(summed, (2 * h + ENC[g]) * FT + f)
                                    nc.vector.tensor_tensor(acc[:], acc[:], pre[ENC[g]][:, f, :],
                                                            ALU.add).then_inc(summed, 1)

        @block.tensor
        def _(pe):
            pe.wait_ge(consts_set, 2)

            def product_tile(h, g, f, slot, first=False):
                nth = h * HT + START[g] + f
                for ch in range(CHUNKS):
                    if g in (L2_R, L2_I) and ch == 0:
                        pe.wait_ge(hid_lo_made, (2 * h + ENC[g] + 1) * FT)
                    pe.wait_ge(w_lo_made, CHUNKS * nth + ch + 1)
                    if ch == 0:
                        pe.wait_ge(tile_out, nth - slot)
                    for kk in range(CK):
                        k = ch * CK + kk
                        if first:
                            pe.wait_ge(x_lo_made, h * FT + k + 1)
                        mm = mm3(nc, mm_ps[:, slot], (w_hi[:, ch, kk, :], w_lo[:, ch, kk, :]),
                                 (moving[g][0][:, k, :], moving[g][1][:, k, :]), k == 0, k == FT - 1)
                    mm.then_inc(w_used, 1)

            with pe.Fori(0, HALVES) as h:
                for g in range(5):
                    e = BESIDE[g]
                    IT = TILES[g] // 2
                    for part in range(2):
                        if e is not None:
                            pe.wait_ge(sq_summed if part else summed, (2 * h + e + 1) * FT)
                            nc.tensor.matmul(st_ps[:, part], ones[:], (acc2 if part else acc)[:],
                                             start=True, stop=True).then_inc(stats_done, 1)
                        start = part * IT // 2
                        if g == L1_R and part == 0:
                            for j in range(2):
                                product_tile(h, g, j, j, first=True)
                            start = 1
                        with pe.Fori(start, (part + 1) * IT // 2) as it:
                            for j in range(2):
                                product_tile(h, g, 2 * it + j, j)


def attention_stage(nc, s_dram, w_qkv, b_qkv, o_dram):
    W3 = 3 * P
    SL = 2 * N
    BANKS = 4

    with ExitStack() as ctx:
        def sb(name, shape, dt):
            return ctx.enter_context(nc.sbuf_tensor(name, shape, dt))

        def sem(name):
            return ctx.enter_context(nc.semaphore(name))

        wq_hi = sb("wq_hi", [P, 2, DT, HP, W3], F32R)
        wq_lo = sb("wq_lo", [P, 2, DT, HP, W3], F32R)
        bias = sb("bias", [P, 2, HP, W3], F32R)
        ones = sb("ones_r", [P, P], F32R)
        s_raw = sb("s_raw", [P, 4, DT, P], F32)
        s_hi = sb("s_hi", [P, SL, DT, P], F32R)
        s_lo = sb("s_lo", [P, SL, DT, P], F32R)
        qk = sb("qk", [P, 2, N, 2, 2 * P], F32)
        v = sb("v", [P, HP, N, 2, P], F32)
        prod = sb("prod", [P, N, 2, P], F32)
        prod_x = sb("prod_x", [P, 2, N, 2, P], F32)
        sums = sb("sums", [P, 2, N, N, 2, 2], F32)
        wv = sb("wv", [P, 2, N, P], F32)
        out = sb("out_bd", [P, 2, N, 2, P], F32)
        ar = sb("ar", [P, N * N, 2], F32)
        ai = sb("ai", [P, N * N, 2], F32)
        mag = sb("mag", [P, N, N, 2], F32)
        top = sb("top", [P, N, 2], F32)
        ex = sb("ex", [P, N, N, 2], F32)
        tot = sb("tot", [P, N, 2], F32)
        wts = sb("wts", [P, 2, N, N, 2], F32)

        qkv_ps = ctx.enter_context(nc.psum_tensor("qkv_ps", [P, BANKS, 512], F32))

        consts_set = sem("att_consts_set")
        b_in, b_split, b_set = sem("b_in"), sem("b_split"), sem("b_set")
        wq_in = [sem("wq_in_0"), sem("wq_in_1")]
        wq_hi_made, wq_lo_made = sem("wq_hi_made"), sem("wq_lo_made")
        s_in = [sem(f"s_in_{i}") for i in range(4)]
        s_hi_made, s_lo_made = sem("s_hi_made"), sem("s_lo_made")
        qkv_done, qk_out, v_out = sem("qkv_done"), sem("qk_out"), sem("v_out")
        prod_made, prod_x_made = sem("prod_made"), sem("prod_x_made")
        qk_free, prod_x_free, wv_free = sem("qk_free"), sem("prod_x_free"), sem("wv_free")
        prod_summed, small = sem("prod_summed"), sem("small")
        sq_ready, mag_made, exp_ready, exp_made, wts_made = (
            sem("sq_ready"), sem("mag_made"), sem("exp_ready"), sem("exp_made"), sem("wts_made"))
        wv_made = sem("wv_made")
        o_stored = [sem("o_stored_0"), sem("o_stored_1")]


        PIECES = 6
        PN = 2 * DT * HP * W3 // PIECES
        BN = 2 * HP * W3
        HALF_B = BN // 2

        def flat(t):
            return t[:].rearrange("p a b c d -> p (a b c d)")

        def piece(t, i):
            return flat(t)[:, i * PN:(i + 1) * PN]

        def w_stage(i):
            return piece(qk, i % 2)

        b_raw = flat(v)[:, 0:BN]
        b_hi = flat(prod_x)[:, 0:HALF_B]
        bias_flat = bias[:].rearrange("p a b c -> p (a b c)")
        SMALLS = 8

        block = ctx.enter_context(nc.Block())

        @block.sync
        def _(sp):
            sp.dma_start(b_raw, b_qkv.partition_broadcast(P)).then_inc(b_in, 16)
            for i in range(PIECES):
                if i >= 2:
                    sp.wait_ge(wq_lo_made, i - 1)
                sp.dma_start(w_stage(i), w_qkv[:, i * PN:(i + 1) * PN]).then_inc(wq_in[i % 2], 16)

            def load_s(nth, bt, sl):
                if not isinstance(nth, int) or nth >= 4:
                    sp.wait_ge(s_lo_made, nth - 3)
                n, ri = sl // 2, sl % 2
                src = s_dram[ri, n * DT:(n + 1) * DT, :, bass.ds(bt * P, P)].rearrange("t p b -> p t b")
                sp.dma_start(s_raw[:, sl % 4], src).then_inc(s_in[sl % 4], 16)

            def store(bt, hp):
                sp.wait_ge(wv_free, (bt * HP + hp + 1) * SL + 2)
                sp.dma_start(o_dram[bt, :, :, :, hp * P:(hp + 1) * P], out[:, hp % 2]).then_inc(o_stored[hp % 2], 16)

            def tile(bt, following):
                for sl in range(4):
                    load_s((bt + 1) * SL + sl, following, sl)
                store(bt, 0)
                for sl in range(4, SL):
                    load_s((bt + 1) * SL + sl, following, sl)
                for hp in range(1, HP):
                    store(bt, hp)

            for sl in range(SL):
                load_s(sl, 0, sl)
            with sp.Fori(0, BT - 1) as bt:
                tile(bt, bt + 1)
            tile(BT - 1, 0)
            for slot in range(2):
                sp.wait_ge(o_stored[slot], 16 * BT * HP // 2)

        @block.scalar
        def _(act):
            act.wait_ge(b_in, 16)
            for half in range(2):
                part = slice(half * HALF_B, (half + 1) * HALF_B)
                if half:
                    act.wait_ge(b_split, 1)
                nc.scalar.copy(b_hi[0:64].bitcast(F32R), b_raw[0:64, part]).then_inc(b_set, 1)
                act.wait_ge(b_set, 2 * half + 1)
                act.wait_ge(consts_set, 2)
                nc.scalar.copy(bias_flat[0:1, part], b_hi[0:1]).then_inc(b_set, 1)
            for i in range(PIECES):
                act.wait_ge(wq_in[i % 2], 16 * (i // 2 + 1))
                nc.scalar.copy(piece(wq_hi, i), w_stage(i)).then_inc(wq_hi_made, 1)

            def high_of_s(sl, nth_in_slot):
                act.wait_ge(s_in[sl % 4], 16 * nth_in_slot)
                nc.scalar.copy(s_hi[:, sl], s_raw[:, sl % 4]).then_inc(s_hi_made, 1)

            def copies(u, hp, next_bt=None):
                act.wait_ge(qk_free, u + 1)
                for sl in range(SL):
                    act.wait_ge(qkv_done, u * SL + sl + 1)
                    n, ri = sl // 2, sl % 2
                    nc.scalar.copy(v[:, hp, n, ri, :], qkv_ps[:, sl % BANKS, 2 * P:W3]).then_inc(v_out, 1)
                    nc.scalar.copy(qk[:, hp % 2, n, ri, :], qkv_ps[:, sl % BANKS, 0:2 * P]).then_inc(qk_out, 1)
                    if next_bt is not None:
                        high_of_s(sl, next_bt * 2 + sl // 4 + 1)

            act.wait_ge(wq_lo_made, PIECES)
            act.wait_ge(b_split, 2)
            for sl in range(SL):
                high_of_s(sl, sl // 4 + 1)
            copies(0, 0)
            with act.Fori(0, BT) as bt:
                for hp in range(HP):
                    u = bt * HP + hp
                    copies(u + 1, (hp + 1) % HP, bt + 1 if hp == HP - 2 else None)
                    act.wait_ge(sq_ready, u + 1)
                    nc.scalar.activation(mag[:], mag[:], ACT.Sqrt, scale=1.0 / HD).then_inc(mag_made, 1)
                    act.wait_ge(exp_ready, u + 1)
                    nc.scalar.activation(ex[:], ex[:], ACT.Exp).then_inc(exp_made, 1)

        @block.gpsimd
        def _(pool):
            nc.gpsimd.memset(bias[:].bitcast(F32), 0.0).then_inc(consts_set, 1)
            nc.gpsimd.memset(ones[:].bitcast(F32), 1.0).then_inc(consts_set, 1)
            for i in range(0, PIECES, 2):
                pool.wait_ge(wq_hi_made, i + 1)
                low_part(nc.gpsimd, piece(wq_lo, i), w_stage(i), piece(wq_hi, i)).then_inc(wq_lo_made, 1)
                pool.wait_ge(wq_lo_made, i + 2)

            def low_of_s(nth, sl):
                pool.wait_ge(s_hi_made, nth + 1)
                low_part(nc.gpsimd, s_lo[:, sl], s_raw[:, sl % 4], s_hi[:, sl]).then_inc(s_lo_made, 1)

            def cross_products(u, hp):
                pool.wait_ge(qk_out, (u + 1) * SL)
                for n in range(N):
                    pool.wait_ge(prod_x_free, u * N + n + 1)
                    for ri in range(2):
                        q = qk[:, hp % 2, n, 1 - ri, 0:P].unsqueeze(1).broadcast_to([P, N, P])
                        k = qk[:, hp % 2, :, ri, P:2 * P]
                        ins = nc.gpsimd.tensor_tensor(prod_x[:, n % 2, :, ri, :], q, k, ALU.mult)
                        ins.then_inc(prod_x_made, 1)

            def weighted(u, hp):
                pool.wait_ge(wts_made, u + 1)
                pool.wait_ge(v_out, (u + 1) * SL)
                for n in range(N):
                    for ri in range(2):
                        pool.wait_ge(wv_free, u * SL + 2 * n + ri + 1)
                        vv = v[:, hp, :, ri, :].rearrange("p m (h d) -> p m h d", h=2)
                        w = wts[:, hp % 2, n].unsqueeze(3).broadcast_to([P, N, 2, HD])
                        o = wv[:, ri].rearrange("p m (h d) -> p m h d", h=2)
                        nc.gpsimd.tensor_tensor(o, vv, w, ALU.mult).then_inc(wv_made, 1)

            for sl in range(SL):
                low_of_s(sl, sl)
            with pool.Fori(0, BT) as bt:
                for hp in range(HP):
                    u = bt * HP + hp
                    cross_products(u, hp)
                    if hp == HP - 2:
                        for sl in range(SL):
                            low_of_s((bt + 1) * SL + sl, sl)
                    if hp:
                        weighted(u - 1, hp - 1)
                weighted(bt * HP + HP - 1, HP - 1)

        @block.vector
        def _(dve):
            for half in range(2):
                part = slice(half * HALF_B, (half + 1) * HALF_B)
                dve.wait_ge(b_set, 2 * half + 2)
                low_part(nc.vector, bias_flat[32:33, part], b_raw[32:33, part], b_hi[32:33]).then_inc(b_split, 1)
            for i in range(1, PIECES, 2):
                dve.wait_ge(wq_hi_made, i + 1)
                dve.wait_ge(wq_lo_made, i)
                low_part(nc.vector, piece(wq_lo, i), w_stage(i), piece(wq_hi, i)).then_inc(wq_lo_made, 1)
            dve.sem_inc(qk_free, 2)
            dve.sem_inc(prod_x_free, 2)
            dve.sem_inc(wv_free, 2)

            def scores(u, hp):
                dve.wait_ge(qk_out, (u + 1) * SL)
                for n in range(N):
                    q = qk[:, hp % 2, n, :, 0:P].unsqueeze(1).broadcast_to([P, N, 2, P])
                    dve.wait_ge(prod_summed, u * N + n)
                    nc.vector.tensor_tensor(prod[:], q, qk[:, hp % 2, :, :, P:2 * P], ALU.mult).then_inc(prod_made, 1)
                    dve.wait_ge(prod_x_made, 2 * (u * N + n + 1))
                    nc.vector.tensor_reduce(sums[:, 1, n].rearrange("p m r h -> p (m r h)"),
                                            prod_x[:, n % 2].rearrange("p m r (h d) -> p (m r h) d", h=2),
                                            AX_X, ALU.add).then_inc(prod_x_free, 1)
                    dve.wait_ge(prod_made, u * N + n + 1)
                    nc.vector.tensor_reduce(sums[:, 0, n].rearrange("p m r h -> p (m r h)"),
                                            prod[:].rearrange("p m r (h d) -> p (m r h) d", h=2),
                                            AX_X, ALU.add).then_inc(prod_summed, 1)
                dve.sem_inc(qk_free, 1)

            def chained(u, n, ins):
                ins.then_inc(small, 1)
                dve.wait_ge(small, u * SMALLS + n)

            def magnitude(u):
                s = sums[:].rearrange("p x n m r h -> p x (n m) r h")
                m2 = mag[:].rearrange("p n m h -> p (n m) h")
                dve.wait_ge(prod_summed, (u + 1) * N)
                dve.wait_ge(prod_x_free, (u + 1) * N + 2)
                chained(u, 1, nc.vector.tensor_tensor(ar[:], s[:, 0, :, 0], s[:, 0, :, 1], ALU.add))
                chained(u, 2, nc.vector.tensor_tensor(ai[:], s[:, 1, :, 0], s[:, 1, :, 1], ALU.subtract))
                chained(u, 3, nc.vector.tensor_tensor(ar[:], ar[:], ar[:], ALU.mult))
                chained(u, 4, nc.vector.tensor_tensor(ai[:], ai[:], ai[:], ALU.mult))
                chained(u, 5, nc.vector.tensor_tensor(m2, ar[:], ai[:], ALU.add))
                nc.vector.tensor_scalar(mag[:], mag[:], MAG_EPS, None, ALU.add).then_inc(sq_ready, 1)

            def less_top(u):
                dve.wait_ge(mag_made, u + 1)
                chained(u, 6, nc.vector.tensor_reduce(top[:], mag[:].rearrange("p n m h -> p n h m"), AX_X, ALU.max))
                nc.vector.tensor_tensor(ex[:], mag[:], top[:].unsqueeze(2).broadcast_to([P, N, N, 2]),
                                        ALU.subtract).then_inc(exp_ready, 1)

            def weights(u, hp):
                dve.wait_ge(exp_made, u + 1)
                chained(u, 7, nc.vector.tensor_reduce(tot[:], ex[:].rearrange("p n m h -> p n h m"), AX_X, ALU.add))
                chained(u, 8, nc.vector.reciprocal(tot[:], tot[:]))
                nc.vector.tensor_tensor(wts[:, hp % 2], ex[:], tot[:].unsqueeze(2).broadcast_to([P, N, N, 2]),
                                        ALU.mult).then_inc(wts_made, 1)

            def weighted_sums(bt, hp, half):
                u = bt * HP + hp
                if half == 0:
                    dve.wait_ge(o_stored[hp % 2], 16 * (bt * 2 + hp // 2))
                for i in range(half * N, half * N + N):
                    n, ri = i // 2, i % 2
                    dve.wait_ge(wv_made, u * SL + i + 1)
                    nc.vector.tensor_reduce(out[:, hp % 2, n, ri, :], wv[:, ri].rearrange("p m c -> p c m"),
                                            AX_X, ALU.add).then_inc(wv_free, 1)

            with dve.Fori(0, BT) as bt:
                for hp in range(HP):
                    u = bt * HP + hp
                    scores(u, hp)
                    magnitude(u)
                    if hp:
                        weighted_sums(bt, hp - 1, 0)
                    less_top(u)
                    if hp:
                        weighted_sums(bt, hp - 1, 1)
                    weights(u, hp)
                for half in range(2):
                    weighted_sums(bt, HP - 1, half)

        @block.tensor
        def _(pe):
            pe.wait_ge(wq_lo_made, PIECES)
            pe.wait_ge(b_split, 2)
            pe.wait_ge(consts_set, 2)

            def unit(u, hp, bt):
                for sl in range(SL):
                    n, ri = sl // 2, sl % 2
                    out_ps = qkv_ps[:, sl % BANKS, 0:W3]
                    if not (isinstance(u, int) and u == 0 and sl < BANKS):
                        pe.wait_ge(qk_out, u * SL + sl - BANKS + 1)
                    if hp == 0:
                        pe.wait_ge(s_lo_made, bt * SL + sl + 1)
                    nc.tensor.matmul(out_ps, ones[:], bias[:, ri, hp, :], start=True, stop=False)
                    for dt in range(DT):
                        mm = mm3(nc, out_ps, (s_hi[:, sl, dt, :], s_lo[:, sl, dt, :]),
                                 (wq_hi[:, ri, dt, hp, :], wq_lo[:, ri, dt, hp, :]), False, dt == DT - 1)
                    mm.then_inc(qkv_done, 1)

            unit(0, 0, 0)
            with pe.Fori(0, BT) as bt:
                for hp in range(HP):
                    unit(bt * HP + hp + 1, (hp + 1) % HP, bt + (hp + 1) // HP)


def mixing_stage(nc, o_dram, w_o, b_o, w_int, ident_dram, r_dram):
    T, NP = 2, 2
    STEPS = BT // T
    COLS = NP * T * P
    G = NP * T
    TR_BANKS, WO_BANKS, RI_BANKS = 2, 2, 4
    RI = 3

    with ExitStack() as ctx:
        def sb(name, shape, dt):
            return ctx.enter_context(nc.sbuf_tensor(name, shape, dt))

        def sem(name):
            return ctx.enter_context(nc.semaphore(name))

        wo_hi, wo_lo = sb("wo_hi", [P, 2, DT, D], F32R), sb("wo_lo", [P, 2, DT, D], F32R)
        wi_hi, wi_lo = sb("wi_hi", [P, NP, 2, DT, D], F32R), sb("wi_lo", [P, NP, 2, DT, D], F32R)
        w_raw = sb("mix_w_raw", [P, 2, D], F32)
        bo = sb("bo", [P, 2, DT], F32)
        ident = sb("mix_ident", [P, P], F32)
        o_raw = sb("o_raw", [P, T, NP, 2, D], F32)
        ot_hi, ot_lo = sb("ot_hi", [P, 2, DT, COLS], F32R), sb("ot_lo", [P, 2, DT, COLS], F32R)
        at_hi, at_lo = sb("at_hi", [P, 2, DT, COLS], F32R), sb("at_lo", [P, 2, DT, COLS], F32R)
        ri_out = sb("ri_out", [P, 2, 2, D], F32)

        tr_ps = ctx.enter_context(nc.psum_tensor("tr_ps", [P, TR_BANKS, COLS], F32))
        wo_ps = ctx.enter_context(nc.psum_tensor("wo_ps", [P, WO_BANKS, COLS], F32))
        ri_ps = ctx.enter_context(nc.psum_tensor("ri_ps", [P, RI_BANKS, D], F32))

        consts_in = sem("mix_consts_in")
        w_in = [sem("mix_w_in_0"), sem("mix_w_in_1")]
        w_hi_made, w_lo_made = sem("mix_w_hi_made"), sem("mix_w_lo_made")
        o_in, transposed, ot_hi_made, ot_lo_made = (
            sem("o_in"), sem("transposed"), sem("ot_hi_made"), sem("ot_lo_made"))
        wo_done, at_hi_made, at_lo_made = sem("wo_done"), sem("at_hi_made"), sem("at_lo_made")
        ri_done, r1_out, r_out, i_out = sem("ri_done"), sem("r1_out"), sem("r_out"), sem("i_out")
        r_stored = [sem("r_stored_0"), sem("r_stored_1")]

        WO_PIECES, WI_PIECES = 2 * DT, NP * 2 * DT

        def w_piece(i):
            if i < WO_PIECES:
                return [t[:].rearrange("p a b n -> p (a b) n")[:, i] for t in (wo_hi, wo_lo)]
            return [t[:].rearrange("p a b c n -> p (a b c) n")[:, (i - WO_PIECES) % WI_PIECES]
                    for t in (wi_hi, wi_lo)]

        def w_source(i):
            if i < WO_PIECES:
                return w_o[:, i]
            return w_int[:, i - WO_PIECES]

        FIRST = WO_PIECES + WI_PIECES
        TOTAL = FIRST + WI_PIECES

        block = ctx.enter_context(nc.Block())

        @block.sync
        def _(sp):
            sp.dma_start(ident[:], ident_dram).then_inc(consts_in, 16)
            sp.dma_start(bo[:], b_o).then_inc(consts_in, 16)

            def load_o(pair, step, nth):
                if not isinstance(nth, int):
                    sp.wait_ge(transposed, nth * 2 * DT)
                for t in range(T):
                    sp.dma_start(o_raw[:, t], o_dram[step * T + t, :, pair * NP:(pair + 1) * NP]).then_inc(o_in, 16)

            def load_w(i):
                if i >= 2:
                    sp.wait_ge(w_lo_made, i - 1)
                sp.dma_start(w_raw[:, i % 2], w_source(i)).then_inc(w_in[i % 2], 16)

            load_o(0, 0, 0)
            for i in range(FIRST):
                load_w(i)
            with sp.Fori(1, STEPS) as step:
                load_o(0, step, step)
            sp.wait_ge(transposed, STEPS * 2 * DT)
            load_o(1, 0, STEPS)
            for i in range(FIRST, TOTAL):
                load_w(i)
            with sp.Fori(1, STEPS) as step:
                load_o(1, step, step + STEPS)
            for slot in range(2):
                sp.wait_ge(r_stored[slot], 16 * 2 * STEPS * G // 2)

        def split_w_high(act, i):
            act.wait_ge(w_in[i % 2], 16 * (i // 2 + 1))
            nc.scalar.copy(w_piece(i)[0], w_raw[:, i % 2]).then_inc(w_hi_made, 1)

        @block.gpsimd
        def _(pool):
            for i in range(TOTAL):
                pool.wait_ge(w_hi_made, i + 1)
                low_part(nc.gpsimd, w_piece(i)[1], w_raw[:, i % 2], w_piece(i)[0]).then_inc(w_lo_made, 1)

        @block.scalar
        def _(act):
            for i in range(FIRST):
                split_w_high(act, i)
            act.wait_ge(consts_in, 32)

            def high_of_out(nth, ri, et):
                i = nth * 2 * DT + ri * DT + et
                act.wait_ge(transposed, i + 1)
                act.wait_ge(wo_done, nth * 2 * DT)
                nc.scalar.copy(ot_hi[:, ri, et], tr_ps[:, i % TR_BANKS if isinstance(i, int) else et % 2])\
                    .then_inc(ot_hi_made, 1)

            def step_body(pair, step):
                nth = pair * STEPS + step
                for ri in range(2):
                    for et in range(DT):
                        high_of_out(nth, ri, et)
                for ri in range(2):
                    for dt in range(DT):
                        i = nth * 2 * DT + ri * DT + dt
                        act.wait_ge(wo_done, i + 1)
                        act.wait_ge(ri_done, nth * G * RI)
                        nc.scalar.activation(at_hi[:, ri, dt], wo_ps[:, dt % WO_BANKS], ACT.Identity,
                                             bias=bo[:, ri, dt:dt + 1]).then_inc(at_hi_made, 1)
                for g in range(G):
                    i = nth * G + g
                    slot = g % 2
                    act.wait_ge(ri_done, i * RI + 1)
                    act.wait_ge(r_stored[slot], 16 * (nth * G // 2 + g // 2))
                    nc.scalar.copy(ri_out[:, slot, 0], ri_ps[:, (RI * g) % RI_BANKS]).then_inc(r1_out, 1)
                    act.wait_ge(ri_done, i * RI + 3)
                    nc.scalar.copy(ri_out[:, slot, 1], ri_ps[:, (RI * g + 2) % RI_BANKS]).then_inc(i_out, 1)
                    act.wait_ge(r_out, i + 1)
                    act.wait_ge(i_out, i + 1)
                    n, t = g // T, g % T
                    act.dma_start(r_dram[step * T + t, :, pair * NP + n], ri_out[:, slot]).then_inc(r_stored[slot], 16)

            with act.Fori(0, STEPS) as step:
                step_body(0, step)
            for i in range(FIRST, TOTAL):
                if i == FIRST:
                    act.wait_ge(ri_done, STEPS * G * RI)
                split_w_high(act, i)
            with act.Fori(0, STEPS) as step:
                step_body(1, step)

        @block.vector
        def _(dve):
            dve.wait_ge(consts_in, 32)
            with dve.Fori(0, 2 * STEPS) as nth:
                for ri in range(2):
                    for et in range(DT):
                        dve.wait_ge(ot_hi_made, nth * 2 * DT + ri * DT + et + 1)
                        low_part(nc.vector, ot_lo[:, ri, et], tr_ps[:, et % TR_BANKS],
                                 ot_hi[:, ri, et]).then_inc(ot_lo_made, 1)
                for ri in range(2):
                    for dt in range(DT):
                        dve.wait_ge(at_hi_made, nth * 2 * DT + ri * DT + dt + 1)
                        nc.vector.scalar_tensor_tensor(at_lo[:, ri, dt], wo_ps[:, dt % WO_BANKS],
                                                       bo[:, ri, dt:dt + 1], at_hi[:, ri, dt].bitcast(F32),
                                                       ALU.add, ALU.subtract).then_inc(at_lo_made, 1)
                for g in range(G):
                    i = nth * G + g
                    dve.wait_ge(r1_out, i + 1)
                    dve.wait_ge(ri_done, i * RI + 2)
                    nc.vector.tensor_tensor(ri_out[:, g % 2, 0], ri_out[:, g % 2, 0],
                                            ri_ps[:, (RI * g + 1) % RI_BANKS], ALU.subtract).then_inc(r_out, 1)

        @block.tensor
        def _(pe):
            pe.wait_ge(consts_in, 32)

            def step_body(nth):
                for t in range(T):
                    pe.wait_ge(o_in, 16 * (nth * T + T))
                for ri in range(2):
                    for et in range(DT):
                        i = nth * 2 * DT + ri * DT + et
                        bank = et % TR_BANKS
                        if not (isinstance(i, int) and i < TR_BANKS):
                            pe.wait_ge(ot_lo_made, i - TR_BANKS + 1)
                        for g in range(G):
                            n, t = g // T, g % T
                            tr = nc.tensor.transpose(tr_ps[:, bank, g * P:(g + 1) * P],
                                                     o_raw[:, t, n, ri, et * P:(et + 1) * P], ident[:])
                        tr.then_inc(transposed, 1)
                for ri in range(2):
                    for dt in range(DT):
                        i = nth * 2 * DT + ri * DT + dt
                        if not (isinstance(i, int) and i < WO_BANKS):
                            pe.wait_ge(at_lo_made, i - WO_BANKS + 1)
                        for et in range(DT):
                            if dt == 0:
                                pe.wait_ge(ot_lo_made, nth * 2 * DT + ri * DT + et + 1)
                            cols = slice(dt * P, (dt + 1) * P)
                            mm = mm3(nc, wo_ps[:, dt % WO_BANKS], (wo_hi[:, ri, et, cols], wo_lo[:, ri, et, cols]),
                                     (ot_hi[:, ri, et], ot_lo[:, ri, et]), et == 0, et == DT - 1)
                        mm.then_inc(wo_done, 1)
                pe.wait_ge(at_lo_made, (nth + 1) * 2 * DT)
                for g in range(G):
                    n = g // T
                    cols = slice(g * P, (g + 1) * P)
                    for q, terms in enumerate([[(0, 0)], [(1, 1)], [(0, 1), (1, 0)]]):
                        bank = (RI * g + q) % RI_BANKS
                        i = nth * G + g
                        if not (isinstance(nth, int) and RI * g + q < RI_BANKS):
                            before = RI * g + q - RI_BANKS
                            bg, bq = before // RI, before % RI
                            pe.wait_ge(i_out if bq == 2 else r_out, nth * G + bg + 1)
                        for x, (a, m) in enumerate(terms):
                            for dt in range(DT):
                                mm = mm3(nc, ri_ps[:, bank], (at_hi[:, a, dt, cols], at_lo[:, a, dt, cols]),
                                         (wi_hi[:, n, m, dt], wi_lo[:, n, m, dt]),
                                         x == 0 and dt == 0, x == len(terms) - 1 and dt == DT - 1)
                        mm.then_inc(ri_done, 1)

            pe.wait_ge(w_lo_made, FIRST)
            step_body(0)
            with pe.Fori(1, STEPS) as step:
                step_body(step)
            pe.wait_ge(w_lo_made, TOTAL)
            with pe.Fori(STEPS, 2 * STEPS) as step:
                step_body(step)


class Chain:

    def __init__(self, engine, semaphore, per_tile):
        self.engine, self.semaphore, self.per_tile, self.tile, self.n = engine, semaphore, per_tile, 0, 0

    def start(self, tile):
        self.tile, self.n = tile, 0

    def step(self, instruction):
        self.n += 1
        instruction.then_inc(self.semaphore, 1)
        self.engine.wait_ge(self.semaphore, self.tile * self.per_tile + self.n)

    def end(self):
        assert self.n == self.per_tile, self.n


def top_stage(nc, r_dram, t_dram, ids, tables, w_head, w_top2, head_rows, ident_dram, y_dram):
    MEAS_R, MEAS_I, POST, TOP1 = 0, DT, 2 * DT, 3 * DT
    WP = 4 * DT
    D2 = D // 2
    TINY = 2.0 ** -116

    with ExitStack() as ctx:
        def sb(name, shape, dt):
            return ctx.enter_context(nc.sbuf_tensor(name, shape, dt))

        def sem(name):
            return ctx.enter_context(nc.semaphore(name))

        w_hi, w_lo = sb("wh_hi", [P, WP, D], F32R), sb("wh_lo", [P, WP, D], F32R)
        w2_hi, w2_lo = sb("w2_hi", [P, DT, D2], F32R), sb("w2_lo", [P, DT, D2], F32R)
        rows = sb("rows", [P, 3 * D + 2 * D2], F32)
        post_b, post_g, post_be = (rows[:, i * D:(i + 1) * D] for i in range(3))
        b_top2, w_top3 = (rows[:, 3 * D + i * D2:3 * D + (i + 1) * D2] for i in range(2))
        ident = sb("top_ident", [P, P], F32)
        idx = sb("idx", [P, BT, N], mybir.dt.int32)
        strength = sb("strength", [P, BT, N * N], F32)
        r = sb("states", [P, 2, N, 2, D], F32)
        sq = sb("sq", [P, 2, 2, D], F32)
        inv = sb("inv", [P, N, D], F32)
        zero = sb("zero", [P, N, D], F32)
        unit = sb("unit", [P, N, 2, D], F32)
        pair = sb("pair", [P, 2, D], F32)
        cos = sb("cos", [P, D], F32)
        wt = sb("wt", [P, N, D], F32)
        sup = sb("sup", [P, 2, D], F32)
        supn = sb("supn", [P, 2, D], F32)
        st_hi, st_lo = sb("st_hi", [P, 3, DT, P], F32R), sb("st_lo", [P, 3, DT, P], F32R)
        xt_hi, xt_lo = sb("xt_hi", [P, DT, P], F32R), sb("xt_lo", [P, DT, P], F32R)
        tx = sb("tx", [P, 2, DT, P], F32)
        msq = sb("msq", [P, 2, D], F32)
        row_a, row_b = sb("row_a", [P, D], F32), sb("row_b", [P, D], F32)
        h2 = sb("h2", [P, D2], F32)
        mean = sb("mean", [P, 1], F32)
        ssq, rn, rs = sb("ssq", [P, 1], F32), sb("rn", [P, 1], F32), sb("rs", [P, 1], F32)
        eps_ln, eps_n = sb("eps_ln", [P, 1], F32), sb("eps_n", [P, 1], F32)
        y = sb("y_sb", [P, BT], F32)

        def bank(name):
            return ctx.enter_context(nc.psum_tensor(name, [P, D], F32))

        t_ps = [bank("t_ps_0"), bank("t_ps_1")]
        m_ps = [bank("mr_ps"), bank("mi_ps")]
        post_ps, top1_ps, top2_ps = bank("post_ps"), bank("top1_ps"), bank("top2_ps")

        consts_in, ids_in, gathered, eps_set = sem("top_consts_in"), sem("ids_in"), sem("gathered"), sem("eps_set")
        w_in, w_hi_made, w_lo_made = sem("top_w_in"), sem("top_w_hi_made"), sem("top_w_lo_made")
        r_in = [sem("r_in_0"), sem("r_in_1")]
        sq_made, abs2_made, abs_made, inv_made = sem("sq_made"), sem("abs2_made"), sem("abs_made"), sem("inv_made")
        unit_made, wz_made, sup_made = sem("unit_made"), sem("wz_made"), sem("sup_made")
        ssq_made, norm_made, supn_made = sem("ssq_made"), sem("norm_made"), sem("supn_made")
        sup_t, st_hi_made, st_lo_made = sem("sup_t"), sem("st_hi_made"), sem("st_lo_made")
        measured, msq_made, amp2_made, amp_made = sem("measured"), sem("msq_made"), sem("amp2_made"), sem("amp_made")
        row_t, xt_hi_made, xt_lo_made = sem("row_t"), sem("xt_hi_made"), sem("xt_lo_made")
        post_done, mean_made, var_made, std_made, ln_made, z_made = (
            sem("post_done"), sem("mean_made"), sem("var_made"), sem("top_std_made"), sem("ln_made"), sem("z_made"))
        top1_done, h1_made, top2_done, y_made = sem("top1_done"), sem("h1_made"), sem("top2_done"), sem("y_made")
        superposing, dense_steps = sem("superposing"), sem("dense_steps")
        SUPERPOSING, DENSE_STEPS = 2 * N + (N - 1) * N + 4 * (N * (N - 1) // 2), 8
        y_stored = sem("y_stored")

        PIECES = WP + 2
        flat = lambda t: t[:].rearrange("p a n -> p (a n)")

        def w_piece(part, i):
            if i < WP:
                return (w_hi, w_lo)[part][:, i]
            return flat((w2_hi, w2_lo)[part])[:, (i - WP) * D:(i - WP + 1) * D]

        def w_stage(i):
            return unit[:].rearrange("p n r d -> p (n r) d")[:, i % 8]

        block = ctx.enter_context(nc.Block())

        @block.sync
        def _(sp):
            sp.dma_start(idx[:], ids).then_inc(ids_in, 16)
            sp.dma_start(rows[:], head_rows.partition_broadcast(P)).then_inc(consts_in, 16)
            sp.dma_start(ident[:], ident_dram).then_inc(consts_in, 16)

            def load(i, slot, k):
                sp.dma_start(r[:, slot], r_dram[i]).then_inc(r_in[slot], 16)
                src = t_dram[:, :, bass.ds(i * P, P)].rearrange("t p b -> p t b")
                sp.dma_start(tx[:, slot], src).then_inc(r_in[slot], 16)

            for slot in range(2):
                load(slot, slot, 0)
            for c in range(0, PIECES, 8):
                n = min(8, PIECES - c)
                if c:
                    sp.wait_ge(w_lo_made, c)
                for i in range(c, c + n):
                    src = w_head[:, i] if i < WP else w_top2[:, 2 * (i - WP):2 * (i - WP) + 2].rearrange("p a n -> p (a n)")
                    sp.dma_start(w_stage(i), src).then_inc(w_in, 16)
            with sp.Fori(1, BT // 2) as i:
                for slot in range(2):
                    sp.wait_ge(wz_made, (2 * i + slot - 1) * N)
                    sp.wait_ge(top1_done, 2 * i + slot - 1)
                    load(2 * i + slot, slot, i)
            sp.wait_ge(y_made, BT)
            sp.dma_start(y_dram, y[:]).then_inc(y_stored, 16)
            sp.wait_ge(y_stored, 16)

        def in_steps(engine, step):
            step(0, 0, True, False)
            step(1, 1, True, True)
            with engine.Fori(1, BT // 2) as k:
                step(2 * k, 0, True, True)
                step(2 * k + 1, 1, True, True)
            step(BT, 0, False, True)

        @block.gpsimd
        def _(pool):
            nc.gpsimd.memset(eps_ln[:], LN_EPS).then_inc(eps_set, 1)
            nc.gpsimd.memset(eps_n[:], MAG_EPS).then_inc(eps_set, 1)
            pool.wait_ge(ids_in, 16)
            for t in range(BT):
                for f in range(N):
                    pool.indirect_dma_start(
                        out=strength[:, t, f * N:(f + 1) * N], out_offset=None, in_=tables[f],
                        in_offset=bass.IndirectOffsetOnAxis(ap=idx[:, t, f:f + 1].bitcast(U32), axis=0),
                    ).then_inc(gathered, 16)

            def units(i, slot):
                pool.wait_ge(sup_made, i)
                if isinstance(i, int) and i == 0:
                    pool.wait_ge(w_lo_made, PIECES)
                for n in range(N):
                    pool.wait_ge(inv_made, i * N + n + 1)
                    by = inv[:, n].unsqueeze(1).broadcast_to([P, 2, D])
                    nc.gpsimd.tensor_tensor(unit[:, n], r[:, slot, n], by, ALU.mult).then_inc(unit_made, 1)

            def weighted(i, slot):
                for n in range(N):
                    pool.wait_ge(superposing, (i + 1) * SUPERPOSING)
                    by = wt[:, n].unsqueeze(1).broadcast_to([P, 2, D])
                    nc.gpsimd.tensor_tensor(unit[:, n], r[:, slot, n], by, ALU.mult).then_inc(wz_made, 1)

            def step(i, slot, s, d):
                if s:
                    units(i, slot)
                    weighted(i, slot)

            in_steps(pool, step)

        @block.scalar
        def _(act):
            for i in range(PIECES):
                act.wait_ge(w_in, 16 * min((i // 8 + 1) * 8, PIECES))
                nc.scalar.copy(w_piece(0, i), w_stage(i)).then_inc(w_hi_made, 1)
            act.wait_ge(eps_set, 2)

            def squares(i, slot, n):
                if n == 0:
                    act.wait_ge(r_in[slot], 16 * (i - slot) + 32)
                if not (isinstance(i, int) and i * N + n < 2):
                    act.wait_ge(abs2_made, i * N + n - 1)
                nc.scalar.activation(sq[:, n % 2], r[:, slot, n], ACT.Square).then_inc(sq_made, 1)

            def root(i, slot, n):
                act.wait_ge(abs2_made, i * N + n + 1)
                nc.scalar.activation(inv[:, n], inv[:, n], ACT.Sqrt).then_inc(abs_made, 1)

            def norm(i, slot):
                act.wait_ge(sup_made, i + 1)
                act.wait_ge(amp2_made, i)
                nc.scalar.activation(msq[:].rearrange("p a n -> p (a n)"), sup[:].rearrange("p a n -> p (a n)"),
                                     ACT.Square, accum_out=ssq[:]).then_inc(ssq_made, 1)
                act.wait_ge(ssq_made, i + 1)
                nc.scalar.activation(rn[:], ssq[:], ACT.Sqrt, bias=eps_n[:]).then_inc(norm_made, 1)

            def sup_high(i, slot):
                act.wait_ge(measured, 2 * i)
                for a, (part, scale) in enumerate([(0, 1.0), (1, 1.0), (1, -1.0)]):
                    act.wait_ge(sup_t, 2 * i + part + 1)
                    nc.scalar.activation(st_hi[:, a].rearrange("p t b -> p (t b)"), t_ps[part][:], ACT.Identity,
                                         scale=scale).then_inc(st_hi_made, 1)

            def measure_squares(i, slot):
                for part in range(2):
                    act.wait_ge(measured, 2 * i + part + 1)
                    act.wait_ge(ssq_made, i + 1)
                    nc.scalar.activation(msq[:, part], m_ps[part][:], ACT.Square).then_inc(msq_made, 1)

            def amplitude(i, slot):
                act.wait_ge(amp2_made, i + 1)
                nc.scalar.activation(row_a[:], row_a[:], ACT.Sqrt).then_inc(amp_made, 1)

            def row_high(i, slot, nth):
                act.wait_ge(row_t, 3 * i + nth + 1)
                act.wait_ge((top2_done, post_done, top1_done)[nth], i if nth == 0 else i + 1)
                nc.scalar.copy(xt_hi[:].rearrange("p t b -> p (t b)"), t_ps[nth % 2][:]).then_inc(xt_hi_made, 1)

            def post_root(i, slot):
                act.wait_ge(mean_made, i + 1)
                nc.scalar.activation(row_a[:], row_b[:], ACT.Square, bias=mean[:], accum_out=rs[:]).then_inc(var_made, 1)
                act.wait_ge(var_made, i + 1)
                nc.scalar.activation(rs[:], rs[:], ACT.Sqrt, bias=eps_ln[:], scale=1.0 / D).then_inc(std_made, 1)

            def post_gelu(i, slot):
                act.wait_ge(ln_made, i + 1)
                nc.scalar.activation(row_a[:], row_b[:], ACT.Gelu).then_inc(z_made, 1)

            def top1_relu(i, slot):
                act.wait_ge(top1_done, i + 1)
                nc.scalar.activation(row_b[:], top1_ps[:], ACT.Relu).then_inc(h1_made, 1)

            def step(i, slot, s, d):
                if s:
                    squares(i, slot, 0)
                    squares(i, slot, 1)
                    root(i, slot, 0)
                    root(i, slot, 1)
                    squares(i, slot, 2)
                    squares(i, slot, 3)
                if d:
                    norm(i - 1, 1 - slot)
                if s:
                    root(i, slot, 2)
                    root(i, slot, 3)
                if d:
                    sup_high(i - 1, 1 - slot)
                    measure_squares(i - 1, 1 - slot)
                    amplitude(i - 1, 1 - slot)
                    row_high(i - 1, 1 - slot, 0)
                    post_root(i - 1, 1 - slot)
                    post_gelu(i - 1, 1 - slot)
                    row_high(i - 1, 1 - slot, 1)
                    top1_relu(i - 1, 1 - slot)
                    row_high(i - 1, 1 - slot, 2)

            in_steps(act, step)

        @block.vector
        def _(dve):
            for i in range(PIECES):
                dve.wait_ge(w_hi_made, i + 1)
                low_part(nc.vector, w_piece(1, i), w_stage(i), w_piece(0, i)).then_inc(w_lo_made, 1)
            dve.wait_ge(consts_in, 32)
            dve.wait_ge(gathered, 16 * BT * N)

            supers = Chain(dve, superposing, SUPERPOSING)
            layers = Chain(dve, dense_steps, DENSE_STEPS)

            def magnitudes(i, slot, n):
                if n == 0:
                    supers.start(i)
                dve.wait_ge(sq_made, i * N + n + 1)
                supers.step(nc.vector.tensor_tensor(inv[:, n], sq[:, n % 2, 0], sq[:, n % 2, 1], ALU.add))
                supers.step(nc.vector.tensor_scalar(zero[:, n], inv[:, n], TINY, None, ALU.is_le))
                nc.vector.tensor_tensor(inv[:, n], inv[:, n], zero[:, n], ALU.add).then_inc(abs2_made, 1)

            def inverse(i, slot, n):
                dve.wait_ge(abs_made, i * N + n + 1)
                nc.vector.reciprocal(inv[:, n], inv[:, n]).then_inc(inv_made, 1)

            def s_ij(i, a, b):
                return strength[:, i, a * N + b:a * N + b + 1] if isinstance(i, int) else strength[:].rearrange("p t s -> p (t s)")[:, bass.ds(i * N * N + a * N + b, 1)]

            def of_zeros(i, slot, j):
                others = [a for a in range(N) if a != j]
                supers.step(nc.vector.tensor_scalar(wt[:, j], zero[:, others[0]], s_ij(i, others[0], j),
                                                    s_ij(i, j, j), ALU.mult, ALU.add))
                for a in others[1:]:
                    supers.step(nc.vector.scalar_tensor_tensor(wt[:, j], zero[:, a], s_ij(i, a, j), wt[:, j],
                                                               ALU.mult, ALU.add))

            def of_pair(i, slot, a, b):
                dve.wait_ge(unit_made, i * N + max(a, b) + 1)
                supers.step(nc.vector.tensor_tensor(pair[:], unit[:, a], unit[:, b], ALU.mult))
                supers.step(nc.vector.tensor_tensor(cos[:], pair[:, 0], pair[:, 1], ALU.add))
                for x, z in ((a, b), (b, a)):
                    supers.step(nc.vector.scalar_tensor_tensor(wt[:, z], cos[:], s_ij(i, x, z), wt[:, z],
                                                               ALU.mult, ALU.add))
                if (a, b) == (N - 2, N - 1):
                    supers.end()

            def sum_states(i, slot):
                layers.start(i)
                dve.wait_ge(wz_made, (i + 1) * N)
                layers.step(nc.vector.tensor_tensor(sup[:], unit[:, 0], unit[:, 1], ALU.add))
                layers.step(nc.vector.tensor_tensor(sup[:], sup[:], unit[:, 2], ALU.add))
                nc.vector.tensor_tensor(sup[:], sup[:], unit[:, 3], ALU.add).then_inc(sup_made, 1)

            def normalise(i, slot):
                dve.wait_ge(norm_made, i + 1)
                layers.step(nc.vector.reciprocal(rn[:], rn[:]))
                nc.vector.tensor_scalar(supn[:], sup[:], rn[:, 0:1], None, ALU.mult).then_inc(supn_made, 1)

            def sup_low(i, slot):
                for a, part in enumerate((0, 1, 1)):
                    dve.wait_ge(st_hi_made, 3 * i + (1 if a == 0 else 3))
                    lo, hi = (t[:, a].rearrange("p t b -> p (t b)") for t in (st_lo, st_hi))
                    if a < 2:
                        low_part(nc.vector, lo, t_ps[part][:], hi).then_inc(st_lo_made, 1)
                    else:
                        nc.vector.scalar_tensor_tensor(lo, t_ps[part][:], -1.0, hi.bitcast(F32),
                                                       ALU.mult, ALU.subtract).then_inc(st_lo_made, 1)

            def amplitude2(i, slot):
                dve.wait_ge(msq_made, 2 * i + 2)
                nc.vector.tensor_tensor(row_a[:], msq[:, 0], msq[:, 1], ALU.add).then_inc(amp2_made, 1)

            def row_low(i, slot, nth):
                dve.wait_ge(xt_hi_made, 3 * i + nth + 1)
                lo, hi = (t[:].rearrange("p t b -> p (t b)") for t in (xt_lo, xt_hi))
                low_part(nc.vector, lo, t_ps[nth % 2][:], hi).then_inc(xt_lo_made, 1)

            def post_stats(i, slot):
                dve.wait_ge(post_done, i + 1)
                layers.step(nc.vector.scalar_tensor_tensor(row_b[:], post_ps[:], 0.0, post_b, ALU.add, ALU.add,
                                                           accum_out=mean[:]))
                nc.vector.tensor_scalar(mean[:], mean[:], -1.0 / D, None, ALU.mult).then_inc(mean_made, 1)

            def post_norm(i, slot):
                dve.wait_ge(std_made, i + 1)
                layers.step(nc.vector.reciprocal(rs[:], rs[:]))
                layers.step(nc.vector.tensor_scalar(row_b[:], row_b[:], mean[:, 0:1], rs[:, 0:1],
                                                    ALU.add, ALU.mult))
                layers.step(nc.vector.tensor_tensor(row_b[:], row_b[:], post_g, ALU.mult))
                nc.vector.tensor_tensor(row_b[:], row_b[:], post_be, ALU.add).then_inc(ln_made, 1)

            def last_layer(i, slot):
                dve.wait_ge(top2_done, i + 1)
                layers.step(nc.vector.tensor_tensor(h2[:], top2_ps[:, 0:D2], b_top2, ALU.add))
                nc.vector.scalar_tensor_tensor(h2[:], h2[:], 0.0, w_top3, ALU.max, ALU.mult,
                                               accum_out=y[:, bass.ds(i, 1)]).then_inc(y_made, 1)
                layers.end()

            def step(i, slot, s, d):
                if s:
                    magnitudes(i, slot, 0)
                    magnitudes(i, slot, 1)
                if d:
                    sum_states(i - 1, 1 - slot)
                if s:
                    inverse(i, slot, 0)
                    magnitudes(i, slot, 2)
                if d:
                    normalise(i - 1, 1 - slot)
                if s:
                    inverse(i, slot, 1)
                    magnitudes(i, slot, 3)
                    inverse(i, slot, 2)
                if d:
                    sup_low(i - 1, 1 - slot)
                if s:
                    inverse(i, slot, 3)
                    of_zeros(i, slot, 0)
                    of_zeros(i, slot, 1)
                if d:
                    amplitude2(i - 1, 1 - slot)
                if s:
                    of_zeros(i, slot, 2)
                    of_zeros(i, slot, 3)
                if d:
                    row_low(i - 1, 1 - slot, 0)
                if s:
                    of_pair(i, slot, 0, 1)
                if d:
                    post_stats(i - 1, 1 - slot)
                if s:
                    of_pair(i, slot, 0, 2)
                if d:
                    post_norm(i - 1, 1 - slot)
                if s:
                    of_pair(i, slot, 1, 2)
                if d:
                    row_low(i - 1, 1 - slot, 1)
                if s:
                    of_pair(i, slot, 0, 3)
                    of_pair(i, slot, 1, 3)
                if d:
                    row_low(i - 1, 1 - slot, 2)
                if s:
                    of_pair(i, slot, 2, 3)
                if d:
                    last_layer(i - 1, 1 - slot)

            in_steps(dve, step)

        @block.tensor
        def _(pe):
            pe.wait_ge(consts_in, 32)
            pe.wait_ge(w_lo_made, PIECES)

            def transposes(to, of):
                for t in range(DT):
                    tr = nc.tensor.transpose(to[:, t * P:(t + 1) * P], of[:, t * P:(t + 1) * P], ident[:])
                return tr

            def product(out, of, first, start=True, stop=True, **more):
                for t in range(DT):
                    mm = mm3(nc, out, (of[0][:, t], of[1][:, t]), (w_hi[:, first + t], w_lo[:, first + t]),
                             start and t == 0, stop and t == DT - 1, **more)
                return mm

            def tile(i, slot):
                st = [(st_hi[:, a], st_lo[:, a]) for a in range(3)]
                xt = (xt_hi[:], xt_lo[:])
                pe.wait_ge(supn_made, i + 1)
                pe.wait_ge(xt_lo_made, 3 * i)
                for part in range(2):
                    transposes(t_ps[part], supn[:, part]).then_inc(sup_t, 1)
                pe.wait_ge(st_lo_made, 3 * i + 3)
                pe.wait_ge(msq_made, 2 * i)
                for part, terms in enumerate([((0, MEAS_R), (2, MEAS_I)), ((0, MEAS_I), (1, MEAS_R))]):
                    for x, (a, first) in enumerate(terms):
                        mm = product(m_ps[part][:], st[a], first, start=x == 0, stop=x == 1)
                    mm.then_inc(measured, 1)
                pe.wait_ge(amp_made, i + 1)
                transposes(t_ps[0], row_a).then_inc(row_t, 1)
                pe.wait_ge(xt_lo_made, 3 * i + 1)
                pe.wait_ge(ln_made, i)
                product(post_ps[:], xt, POST).then_inc(post_done, 1)
                pe.wait_ge(z_made, i + 1)
                transposes(t_ps[1], row_a).then_inc(row_t, 1)
                pe.wait_ge(xt_lo_made, 3 * i + 2)
                pe.wait_ge(h1_made, i)
                product(top1_ps[:], xt, TOP1, skip_group_check=True)
                pe.wait_ge(r_in[slot], 16 * (i - slot) + 32)
                for t in range(DT):
                    mm = nc.tensor.matmul(top1_ps[:, t * P:(t + 1) * P], tx[:, slot, t], ident[:],
                                          start=False, stop=True, skip_group_check=True)
                mm.then_inc(top1_done, 1)
                pe.wait_ge(h1_made, i + 1)
                transposes(t_ps[0], row_b).then_inc(row_t, 1)
                pe.wait_ge(xt_lo_made, 3 * i + 3)
                pe.wait_ge(y_made, i)
                for t in range(DT):
                    mm = mm3(nc, top2_ps[:, 0:D2], (xt[0][:, t], xt[1][:, t]), (w2_hi[:, t], w2_lo[:, t]),
                             t == 0, t == DT - 1)
                mm.then_inc(top2_done, 1)

            with pe.Fori(0, BT // 2) as k:
                for slot in range(2):
                    tile(2 * k + slot, slot)


def recurrent_tower(nc, xT, w_enc, enc_vec, b_top1, w_qkv, b_qkv, w_o, b_o, w_int, ident, w_head, w_top2,
                    head_rows, ids, tbl_0, tbl_1, tbl_2, tbl_3, y):
    s = nc.dram_tensor("s_both", (2, FT, P, B), F32).ap()
    x_top = nc.dram_tensor("x_top", (DT, P, B), F32).ap()
    attended = nc.dram_tensor("attended", (BT, P, N, 2, D), F32).ap()
    mixed = nc.dram_tensor("mixed", (BT, P, N, 2, D), F32).ap()
    encoder_stage(nc, xT, w_enc, enc_vec, b_top1, s, x_top)
    attention_stage(nc, s, w_qkv, b_qkv, attended)
    mixing_stage(nc, attended, w_o, b_o, w_int, ident, mixed)
    top_stage(nc, mixed, x_top, ids, [tbl_0, tbl_1, tbl_2, tbl_3], w_head, w_top2, head_rows, ident, y)


def _layouts(inputs):
    given = {name.replace("L0_rec_", ""): np.asarray(a) for name, a in inputs.items()}

    def encoder_chunks(w):
        return w.reshape(FT, P, 2, FT // 2, P).transpose(0, 2, 4, 3, 1).reshape(2 * FT, P, FT // 2, P)

    w_top1 = given["W_top1"]
    top_chunks = w_top1[D:].reshape(2, FT // 2, P, DT, P).transpose(3, 0, 2, 1, 4).reshape(2 * DT, P, FT // 2, P)
    qkv = [np.stack([given[f"W{q}_{part}"].T.reshape(DT, P, HP, P) for q in "qkv"], axis=3) for part in "ri"]
    int_w = np.stack([given["int_Wr"], given["int_Wi"]], axis=1).transpose(3, 0, 1, 2).reshape(DT, P, N, 2, D)
    return {
        "xT": given["r_x"].reshape(HALVES, HB, FT, P).transpose(0, 3, 2, 1),
        "w_enc": np.concatenate([encoder_chunks(given["er_W1"]), top_chunks, encoder_chunks(given["ei_W1"]),
                                 encoder_chunks(given["er_W2"]), encoder_chunks(given["ei_W2"])]),
        "enc_vec": np.stack([given[e + v].reshape(FT, P).T for v in ("_b1", "_g1", "_be1", "_b2")
                             for e in ("er", "ei")], axis=1),
        "b_top1": given["b_top1"].reshape(DT, P).T,
        "w_qkv": np.stack([w.transpose(1, 0, 2, 3, 4) for w in qkv], axis=1).reshape(P, -1),
        "b_qkv": np.stack([np.stack([given[f"b{q}_{part}"].reshape(HP, P) for q in "qkv"], axis=1)
                           for part in "ri"]).reshape(-1),
        "w_o": np.stack([given["Wo_" + part].T.reshape(DT, P, D).transpose(1, 0, 2) for part in "ri"],
                        axis=1).reshape(P, 2 * DT, D),
        "b_o": np.stack([given["bo_" + part].reshape(DT, P).T for part in "ri"], axis=1),
        "w_int": int_w.transpose(1, 2, 3, 0, 4).reshape(P, N * 2 * DT, D),
        "ident": np.eye(P, dtype=np.float32),
        "w_head": np.concatenate([given["meas_Mr"].T, given["meas_Mi"].T, given["post_W"].T, w_top1[:D]])
                    .reshape(4 * DT, P, D).transpose(1, 0, 2),
        "w_top2": given["W_top2"].reshape(DT, P, D // 2).transpose(1, 0, 2),
        "head_rows": np.concatenate([given["post_b"], given["post_g"], given["post_be"], given["b_top2"],
                                     given["W_top3"][:, 0]]),
        "ids": given["ids"].reshape(BT, P, N).transpose(1, 0, 2),
        "tbl_0": given["tbl_0"], "tbl_1": given["tbl_1"], "tbl_2": given["tbl_2"], "tbl_3": given["tbl_3"],
    }


def kernel(**inputs):
    import concourse.bacc as _bacc
    from concourse.bass_utils import run_bass_kernel_spmd as _run

    nc = _bacc.Bacc("TRN2", target_bir_lowering=False, num_devices=1)
    arrays = {name: np.ascontiguousarray(a) for name, a in _layouts(inputs).items()}
    args = [nc.dram_tensor(name, a.shape, mybir.dt.from_np(a.dtype), kind="ExternalInput").ap()
            for name, a in arrays.items()]
    y = nc.dram_tensor("y", (P, BT), F32, kind="ExternalOutput").ap()
    recurrent_tower(nc, *args, y)
    results = _run(nc, [arrays], core_ids=[0])
    return results.results[0]["y"].T.reshape(B, 1)
```

```python
from contextlib import ExitStack

import concourse.bass as bass
import numpy as np
from concourse import mybir

ALU = mybir.AluOpType
ACT = mybir.ActivationFunctionType
AX_X = mybir.AxisListType.X
F32 = mybir.dt.float32
F32R = mybir.dt.float32r
U32 = mybir.dt.uint32

P = 128
B = 1024
HB = 512
HALVES = B // HB
BT = B // P
K = 2048
FT = K // P
D = 512
DT = D // P
N = 4
H = 8
HD = D // H
HP = H // 2
LN_EPS = 1e-5
MAG_EPS = 1e-8
VEC_B1, VEC_G, VEC_BE, VEC_B2 = 0, 2, 4, 6


def mm3(nc, out, w, x, start, stop, **more):
    (w_hi, w_lo), (x_hi, x_lo) = w, x
    nc.tensor.matmul(out, w_hi, x_hi, start=start, stop=False, **more)
    nc.tensor.matmul(out, w_hi, x_lo, start=False, stop=False, **more)
    return nc.tensor.matmul(out, w_lo, x_hi, start=False, stop=stop, **more)


def low_part(engine, lo, full, hi):
    return engine.tensor_tensor(lo, full, hi.bitcast(F32), ALU.subtract)


def encoder_stage(nc, xT, w_enc, enc_vec, b_top1, s_dram, t_dram):
    CK = 4
    CHUNKS = FT // CK
    L1_R, TOP, L1_I, L2_R, L2_I = range(5)
    TILES = [FT, DT, FT, FT, FT]
    START = [sum(TILES[:g]) for g in range(5)]
    HT = sum(TILES)
    HC = HT * CHUNKS
    ENC = {L1_R: 0, L1_I: 1, L2_R: 0, L2_I: 1}
    OUT_START = {TOP: 0, L2_R: DT, L2_I: DT + FT}
    OUT_TILES = DT + 2 * FT

    with ExitStack() as ctx:
        def sb(name, shape, dt):
            return ctx.enter_context(nc.sbuf_tensor(name, shape, dt))

        def sem(name):
            return ctx.enter_context(nc.semaphore(name))

        x_hi = sb("x_hi", [P, FT, HB], F32R)
        x_lo = sb("x_lo", [P, FT, HB], F32R)
        h_lo = sb("h_lo", [P, FT, HB], F32R)
        h_hi = sb("h_hi", [P, FT, HB], F32R)
        pre_r = nc.alloc_sbuf_tensor_at("pre_r", [P, FT, HB], F32, offset=nc.sbuf_base - FT * HB * 4)
        pre_i = sb("pre_i", [P, FT, HB], F32)
        w_raw = sb("w_raw", [P, CHUNKS, CK, P], F32)
        w_hi = sb("w_hi", [P, CHUNKS, CK, P], F32R)
        w_lo = sb("w_lo", [P, CHUNKS, CK, P], F32R)
        acc = sb("acc", [P, HB], F32)
        acc2 = sb("acc2", [P, HB], F32)
        rstd = sb("rstd", [P, HB], F32)
        norm = sb("norm", [P, 2, HB], F32)
        gelu = sb("gelu", [P, 2, HB], F32)
        s_out = sb("s_out", [P, 2, HB], F32)
        vec = sb("vec", [P, 8, FT], F32)
        vec_top = sb("vec_top", [P, DT], F32)
        ones = sb("ones", [P, P], F32)
        eps = sb("eps", [P, 1], F32)

        x_in = [sem(f"x_in_{group}") for group in range(FT // CK)]
        vec_in = sem("vec_in")
        w_in = [sem(f"w_in_{slot}") for slot in range(CHUNKS)]
        consts_set = sem("consts_set")
        x_hi_made, x_lo_made = sem("x_hi_made"), sem("x_lo_made")
        w_hi_made, w_lo_made, w_used = sem("w_hi_made"), sem("w_lo_made"), sem("w_used")
        tile_out = sem("tile_out")
        cleared, summed = sem("cleared"), sem("summed")
        centred, squared, sq_summed = sem("centred"), sem("squared"), sem("sq_summed")
        stats_done, std_made, rstd_made = sem("stats_done"), sem("std_made"), sem("rstd_made")
        normed, gelu_made = sem("normed"), sem("gelu_made")
        hid_hi_made, hid_lo_made = sem("hid_hi_made"), sem("hid_lo_made")
        stored = [sem("stored_0"), sem("stored_1")]

        START_AT_ONE = [w_lo_made, w_used, summed, sq_summed, *stored]
        START_AT_TWO = [tile_out, gelu_made, hid_lo_made]

        mm_ps = ctx.enter_context(nc.psum_tensor("enc_mm", [P, 2, HB], F32))
        st_ps = ctx.enter_context(nc.psum_tensor("enc_stats", [P, 2, HB], F32))
        moving = [(x_hi, x_lo), (x_hi, x_lo), (x_hi, x_lo), (h_hi, h_lo), (x_hi, x_lo)]
        pre = [pre_r, pre_i]
        hidden = [(h_hi, h_lo), (x_hi, x_lo)]
        BESIDE = [None, None, 0, 1, None]

        block = ctx.enter_context(nc.Block())

        @block.sync
        def _(sp):
            def load_x(h):
                for group, arrived in enumerate(x_in):
                    ks = slice(group * CK, (group + 1) * CK)
                    sp.dma_start(pre_i[:, ks, :], xT[h, :, ks, :]).then_inc(arrived, 16)

            def load_chunk(tile, source, ch):
                if not isinstance(tile, int) or tile > 0:
                    sp.wait_ge(w_lo_made, 1 + (tile - 1) * CHUNKS + ch + 1)
                k = (ch % 2) * CK
                sp.dma_start(w_raw[:, ch], w_enc[2 * source + ch // 2, :, k:k + CK]).then_inc(w_in[ch], 16)

            def load_tile(tile, source):
                for ch in range(CHUNKS):
                    load_chunk(tile, source, ch)

            sp.dma_start(vec[:], enc_vec).then_inc(vec_in, 16)
            sp.dma_start(vec_top[:], b_top1).then_inc(vec_in, 16)
            load_tile(0, 0)
            load_x(0)
            AHEAD = START[L2_I] + 2
            with sp.Fori(1, AHEAD) as tile:
                load_tile(tile, tile)
            sp.wait_ge(normed, 2 * FT)
            load_x(1)
            with sp.Fori(AHEAD, HT) as tile:
                load_tile(tile, tile)
            with sp.Fori(0, HT) as tile:
                load_tile(tile + HT, tile)
            load_tile(2 * HT, 0)

        @block.gpsimd
        def _(pool):
            nc.gpsimd.memset(ones[:], 1.0 / K).then_inc(consts_set, 1)
            nc.gpsimd.memset(eps[:], LN_EPS).then_inc(consts_set, 1)
            for semaphore in START_AT_ONE:
                pool.sem_inc(semaphore, 1)
            for semaphore in START_AT_TWO:
                pool.sem_inc(semaphore, 2)
            with pool.Fori(0, HALVES * HT + 1) as tile:
                for ch in range(CHUNKS):
                    pool.wait_ge(w_hi_made, tile * CHUNKS + ch + 1)
                    low_part(nc.gpsimd, w_lo[:, ch], w_raw[:, ch], w_hi[:, ch]).then_inc(w_lo_made, 1)

        @block.scalar
        def _(act):
            def high_of_chunk(tile, ch):
                act.wait_ge(w_in[ch], 16 * (tile + 1))
                if not isinstance(tile, int):
                    act.wait_ge(w_used, 1 + (tile - 1) * CHUNKS + ch + 1)
                nc.scalar.copy(w_hi[:, ch], w_raw[:, ch]).then_inc(w_hi_made, 1)

            def square(h, e, k):
                nth = (2 * h + e) * FT + k
                act.wait_ge(centred, nth + 1)
                act.wait_ge(sq_summed, 1 + nth)
                nc.scalar.activation(norm[:, 0], pre[e][:, k, :], ACT.Square).then_inc(squared, 1)

            def gelu_tile(h, e, k, slot):
                nth = (2 * h + e) * FT + k
                act.wait_ge(normed, nth + 1)
                act.wait_ge(hid_lo_made, 2 + nth - 1)
                nc.scalar.activation(gelu[:, slot], norm[:, slot], ACT.Gelu,
                                     bias=vec[:, VEC_BE + e, bass.ds(k, 1)],
                                     scale=vec[:, VEC_G + e, bass.ds(k, 1)]).then_inc(gelu_made, 1)
                act.wait_ge(gelu_made, 2 + nth + 1)
                nc.scalar.copy(hidden[e][0][:, k, :], gelu[:, slot]).then_inc(hid_hi_made, 1)

            def tile_to_sbuf(h, g, f, slot):
                nth = h * HT + START[g] + f
                act.wait_ge(w_used, 1 + CHUNKS * (nth + 1))
                if g in (L1_R, L1_I):
                    nc.scalar.activation(pre[ENC[g]][:, f, :], mm_ps[:, slot], ACT.Identity,
                                         bias=vec[:, VEC_B1 + ENC[g], bass.ds(f, 1)]).then_inc(tile_out, 1)
                    return
                act.wait_ge(stored[slot], 1 + 8 * (h * OUT_TILES + OUT_START[g] + f - slot))
                bias = vec_top[:, bass.ds(f, 1)] if g == TOP else vec[:, VEC_B2 + ENC[g], bass.ds(f, 1)]
                nc.scalar.activation(s_out[:, slot], mm_ps[:, slot], ACT.Identity, bias=bias).then_inc(tile_out, 1)
                act.wait_ge(tile_out, 2 + nth + 1)
                to = t_dram[f] if g == TOP else s_dram[ENC[g], f]
                act.dma_start(to[:, bass.ds(h * HB, HB)], s_out[:, slot]).then_inc(stored[slot], 16)

            act.wait_ge(vec_in, 32)
            for ch in range(CHUNKS):
                high_of_chunk(0, ch)
            with act.Fori(0, HALVES) as h:
                for k in range(FT):
                    act.wait_ge(x_in[k // CK], 16 * (h + 1))
                    act.wait_ge(w_used, 1 + h * HC)
                    nc.scalar.copy(x_hi[:, k, :], pre_i[:, k, :]).then_inc(x_hi_made, 1)
                for g in range(5):
                    e = BESIDE[g]
                    IT = TILES[g] // 2
                    for part in range(2):
                        if e is not None and part == 1:
                            act.wait_ge(stats_done, 4 * h + 2 * e + 2)
                            nc.scalar.activation(acc2[:], st_ps[:, 1], ACT.Sqrt, bias=eps[:]).then_inc(std_made, 1)
                        with act.Fori(part * IT // 2, (part + 1) * IT // 2) as it:
                            for j in range(2):
                                f = 2 * it + j
                                nth = h * HT + START[g] + f
                                for ch in range(CHUNKS):
                                    high_of_chunk(nth + 1, ch)
                                    second = ch // 2
                                    k = 2 * f + second - part * FT
                                    if ch % 2 == 0 or e is None:
                                        continue
                                    if part == 0:
                                        square(h, e, k)
                                    else:
                                        if j == 0 and second == 0 and g == L2_R:
                                            act.wait_ge(w_used, 1 + h * HC + CHUNKS * START[L2_R])
                                        gelu_tile(h, e, k, second)
                                tile_to_sbuf(h, g, f, j)
            for slot in range(2):
                act.wait_ge(stored[slot], 1 + 8 * HALVES * OUT_TILES)

        @block.vector
        def _(dve):
            dve.wait_ge(consts_set, 2)
            with dve.Fori(0, HALVES) as h:
                for k in range(FT):
                    dve.wait_ge(x_hi_made, h * FT + k + 1)
                    low_part(nc.vector, x_lo[:, k, :], pre_i[:, k, :], x_hi[:, k, :]).then_inc(x_lo_made, 1)
                for g in (L1_R, L1_I, L2_R):
                    e = BESIDE[g]
                    IT = TILES[g] // 2
                    if g == L1_R:
                        nc.vector.memset(acc[:], 0.0).then_inc(cleared, 1)
                    for part in range(2):
                        if e is not None and part == 0:
                            dve.wait_ge(stats_done, 4 * h + 2 * e + 1)
                            nc.vector.memset(acc[:], 0.0).then_inc(cleared, 1)
                            nc.vector.memset(acc2[:], 0.0).then_inc(cleared, 1)
                        if e is not None and part == 1:
                            dve.wait_ge(std_made, 2 * h + e + 1)
                            nc.vector.reciprocal(rstd[:], acc2[:]).then_inc(rstd_made, 1)
                        with dve.Fori(part * IT // 2, (part + 1) * IT // 2) as it:
                            for j in range(2):
                                f = 2 * it + j
                                for second in range(2):
                                    k = 2 * f + second - part * FT
                                    if e is None:
                                        continue
                                    nth = (2 * h + e) * FT + k
                                    if part == 0:
                                        nc.vector.tensor_tensor(pre[e][:, k, :], pre[e][:, k, :], st_ps[:, 0],
                                                                ALU.subtract).then_inc(centred, 1)
                                        dve.wait_ge(cleared, 5 * h + 1 + 2 * e + 2)
                                        dve.wait_ge(squared, nth + 1)
                                        nc.vector.tensor_tensor(acc2[:], acc2[:], norm[:, 0],
                                                                ALU.add).then_inc(sq_summed, 1)
                                    else:
                                        dve.wait_ge(gelu_made, 2 + nth - 1)
                                        dve.wait_ge(rstd_made, 2 * h + e + 1)
                                        nc.vector.tensor_tensor(norm[:, second], pre[e][:, k, :], rstd[:],
                                                                ALU.mult).then_inc(normed, 1)
                                        dve.wait_ge(hid_hi_made, nth + 1)
                                        low_part(nc.vector, hidden[e][1][:, k, :], gelu[:, second],
                                                 hidden[e][0][:, k, :]).then_inc(hid_lo_made, 1)
                                if g != L2_R:
                                    dve.wait_ge(tile_out, 2 + h * HT + START[g] + f + 1)
                                    if g == L1_R:
                                        dve.wait_ge(cleared, 5 * h + 1)
                                    dve.wait_ge(summed, 1 + (2 * h + ENC[g]) * FT + f)
                                    nc.vector.tensor_tensor(acc[:], acc[:], pre[ENC[g]][:, f, :],
                                                            ALU.add).then_inc(summed, 1)

        @block.tensor
        def _(pe):
            pe.wait_ge(consts_set, 2)

            def product_tile(h, g, f, slot, first=False):
                nth = h * HT + START[g] + f
                for ch in range(CHUNKS):
                    if g in (L2_R, L2_I) and ch == 0:
                        pe.wait_ge(hid_lo_made, 2 + (2 * h + ENC[g] + 1) * FT)
                    pe.wait_ge(w_lo_made, 1 + CHUNKS * nth + ch + 1)
                    if ch == 0:
                        pe.wait_ge(tile_out, 2 + nth - 1)
                    for kk in range(CK):
                        k = ch * CK + kk
                        if first:
                            pe.wait_ge(x_lo_made, h * FT + k + 1)
                        mm = mm3(nc, mm_ps[:, slot], (w_hi[:, ch, kk, :], w_lo[:, ch, kk, :]),
                                 (moving[g][0][:, k, :], moving[g][1][:, k, :]), k == 0, k == FT - 1)
                    mm.then_inc(w_used, 1)

            with pe.Fori(0, HALVES) as h:
                for g in range(5):
                    e = BESIDE[g]
                    IT = TILES[g] // 2
                    for part in range(2):
                        if e is not None:
                            pe.wait_ge(sq_summed if part else summed, 1 + (2 * h + e + 1) * FT)
                            nc.tensor.matmul(st_ps[:, part], ones[:], (acc2 if part else acc)[:],
                                             start=True, stop=True).then_inc(stats_done, 1)
                        start = part * IT // 2
                        if g == L1_R and part == 0:
                            for j in range(2):
                                product_tile(h, g, j, j, first=True)
                            start = 1
                        with pe.Fori(start, (part + 1) * IT // 2) as it:
                            for j in range(2):
                                product_tile(h, g, 2 * it + j, j)


def attention_stage(nc, s_dram, w_qkv, b_qkv, o_dram):
    W3 = 3 * P
    SL = 2 * N
    BANKS = 4

    with ExitStack() as ctx:
        def sb(name, shape, dt):
            return ctx.enter_context(nc.sbuf_tensor(name, shape, dt))

        def sem(name):
            return ctx.enter_context(nc.semaphore(name))

        wq_hi = sb("wq_hi", [P, HP, 2, DT, W3], F32R)
        wq_lo = sb("wq_lo", [P, HP, 2, DT, W3], F32R)
        bias = sb("bias", [P, 2, HP, W3], F32R)
        ones = sb("ones_r", [P, P], F32R)
        s_raw = sb("s_raw", [P, 4, DT, P], F32)
        s_hi = sb("s_hi", [P, SL, DT, P], F32R)
        s_lo = sb("s_lo", [P, SL, DT, P], F32R)
        qk = sb("qk", [P, 2, N, 2, 2 * P], F32)
        v = sb("v", [P, HP, N, 2, P], F32)
        qx = sb("qx", [P, 2, N, 2, P], F32)
        wv = sb("wv", [P, 2, N, P], F32)
        wv2 = sb("wv2", [P, N, 2, P], F32)
        out = sb("out_bd", [P, 2, N, 2, P], F32)
        ar = sb("ar", [P, N * N, 2], F32)
        ai = sb("ai", [P, N * N, 2], F32)
        mag = sb("mag", [P, N, N, 2], F32)
        top = sb("top", [P, N, 2], F32)
        ex = sb("ex", [P, N, N, 2], F32)
        tot = sb("tot", [P, N, 2], F32)
        wts = sb("wts", [P, 2, N, N, 2], F32)

        qkv_ps = ctx.enter_context(nc.psum_tensor("qkv_ps", [P, BANKS, 512], F32))

        GROUPS = N * N // 2
        prod = ctx.enter_context(nc.psum_tensor("prod", [P, 2, 8, P], F32))

        consts_set = sem("att_consts_set")
        b_in, b_split, b_set = sem("b_in"), sem("b_split"), sem("b_set")
        wq_in = [sem("wq_in_0"), sem("wq_in_1")]
        wq_hi_made, wq_lo_made = sem("wq_hi_made"), sem("wq_lo_made")
        s_in = [sem(f"s_in_{i}") for i in range(4)]
        s_hi_made, s_lo_made = sem("s_hi_made"), sem("s_lo_made")
        qkv_done, qk_out, v_out = sem("qkv_done"), sem("qk_out"), sem("v_out")
        qk_free, wv_free, wv_made, scores_made = sem("qk_free"), sem("wv_free"), sem("wv_made"), sem("scores_made")
        small = sem("small")
        sq_ready, mag_made, exp_ready, exp_made, wts_made = (
            sem("sq_ready"), sem("mag_made"), sem("exp_ready"), sem("exp_made"), sem("wts_made"))
        wv_mults = sem("wv_mults")
        o_stored = [sem("o_stored_0"), sem("o_stored_1")]


        PIECES = 2 * HP
        PN = DT * W3
        BN = 2 * HP * W3
        HALF_B = BN // 2

        def flat(t):
            return t[:].rearrange("p a b c d -> p (a b c d)")

        def piece(t, i):
            return flat(t)[:, i * PN:(i + 1) * PN]

        v_half = HP // 2 * N * 2 * P

        def w_stage(i):
            return flat(v)[:, v_half:v_half + PN] if i % 2 else flat(out)[:, 0:PN]

        b_raw = flat(v)[:, 0:BN]
        b_hi = flat(qx)[:, 0:HALF_B]
        bias_flat = bias[:].rearrange("p a b c -> p (a b c)")
        SMALLS = 5

        block = ctx.enter_context(nc.Block())

        @block.sync
        def _(sp):
            sp.dma_start(b_raw, b_qkv.partition_broadcast(P)).then_inc(b_in, 16)

            def load_w(i):
                if i == 1:
                    sp.wait_ge(b_split, 2)
                if i >= 2:
                    sp.wait_ge(wq_lo_made, i - 1)
                sp.dma_start(w_stage(i), w_qkv[:, i * PN:(i + 1) * PN]).then_inc(wq_in[i % 2], 16)

            def load_s(nth, bt, sl):
                if not isinstance(nth, int) or nth >= 4:
                    sp.wait_ge(s_lo_made, nth - 3)
                n, ri = sl // 2, sl % 2
                src = s_dram[ri, n * DT:(n + 1) * DT, :, bass.ds(bt * P, P)].rearrange("t p b -> p t b")
                sp.dma_start(s_raw[:, sl % 4], src).then_inc(s_in[sl % 4], 16)

            def store(bt, hp):
                sp.wait_ge(wv_free, (bt * HP + hp + 1) * SL + N)
                sp.dma_start(o_dram[bt, :, :, :, hp * P:(hp + 1) * P], out[:, hp % 2]).then_inc(o_stored[hp % 2], 16)

            def tile(bt, following):
                for sl in range(4):
                    load_s((bt + 1) * SL + sl, following, sl)
                store(bt, 0)
                for sl in range(4, SL):
                    load_s((bt + 1) * SL + sl, following, sl)
                for hp in range(1, HP):
                    store(bt, hp)

            load_w(0)
            for sl in range(2):
                load_s(sl, 0, sl)
            load_w(1)
            for sl in range(2, 4):
                load_s(sl, 0, sl)
            load_w(2)
            for sl in range(4, SL):
                load_s(sl, 0, sl)
            for i in range(3, PIECES):
                load_w(i)
            with sp.Fori(0, BT - 1) as bt:
                tile(bt, bt + 1)
            tile(BT - 1, 0)
            for slot in range(2):
                sp.wait_ge(o_stored[slot], 16 * BT * HP // 2)

        @block.scalar
        def _(act):
            act.wait_ge(b_in, 16)
            for half in range(2):
                part = slice(half * HALF_B, (half + 1) * HALF_B)
                if half:
                    act.wait_ge(b_split, 1)
                nc.scalar.copy(b_hi[0:64].bitcast(F32R), b_raw[0:64, part]).then_inc(b_set, 1)
                act.wait_ge(b_set, 2 * half + 1)
                act.wait_ge(consts_set, 2)
                nc.scalar.copy(bias_flat[0:1, part], b_hi[0:1]).then_inc(b_set, 1)

            def high_of_w(i):
                act.wait_ge(wq_in[i % 2], 16 * (i // 2 + 1))
                nc.scalar.copy(piece(wq_hi, i), w_stage(i)).then_inc(wq_hi_made, 1)

            def high_of_s(sl, nth_in_slot):
                act.wait_ge(s_in[sl % 4], 16 * nth_in_slot)
                nc.scalar.copy(s_hi[:, sl], s_raw[:, sl % 4]).then_inc(s_hi_made, 1)

            def copies(u, hp, next_bt=None):
                act.wait_ge(qk_free, u + 1)
                for sl in range(SL):
                    if isinstance(u, int) and sl + 3 < PIECES:
                        high_of_w(sl + 3)
                    act.wait_ge(qkv_done, u * SL + sl + 1)
                    n, ri = sl // 2, sl % 2
                    nc.scalar.copy(v[:, hp, n, ri, :], qkv_ps[:, sl % BANKS, 2 * P:W3]).then_inc(v_out, 1)
                    nc.scalar.mul(qx[:, hp % 2, n, 1 - ri, :], qkv_ps[:, sl % BANKS, 0:P], 1.0 if ri else -1.0)
                    nc.scalar.copy(qk[:, hp % 2, n, ri, :], qkv_ps[:, sl % BANKS, 0:2 * P]).then_inc(qk_out, 1)
                    if next_bt is not None:
                        high_of_s(sl, next_bt * 2 + sl // 4 + 1)

            high_of_w(0)
            for sl in range(2):
                high_of_s(sl, 1)
            high_of_w(1)
            for sl in range(2, 4):
                high_of_s(sl, 1)
            high_of_w(2)
            for sl in range(4, SL):
                high_of_s(sl, 2)
            copies(0, 0)
            with act.Fori(0, BT) as bt:
                for hp in range(HP):
                    u = bt * HP + hp
                    copies(u + 1, (hp + 1) % HP, bt + 1 if hp == HP - 2 else None)
                    act.wait_ge(sq_ready, u + 1)
                    nc.scalar.activation(mag[:], mag[:], ACT.Sqrt, scale=1.0 / HD).then_inc(mag_made, 1)
                    act.wait_ge(exp_ready, u + 1)
                    nc.scalar.activation(ex[:], ex[:], ACT.Exp).then_inc(exp_made, 1)

        @block.gpsimd
        def _(pool):
            nc.gpsimd.memset(bias[:].bitcast(F32), 0.0).then_inc(consts_set, 1)
            nc.gpsimd.memset(ones[:].bitcast(F32), 1.0).then_inc(consts_set, 1)

            def low_of_s(nth, sl):
                pool.wait_ge(s_hi_made, nth + 1)
                low_part(nc.gpsimd, s_lo[:, sl], s_raw[:, sl % 4], s_hi[:, sl]).then_inc(s_lo_made, 1)

            def weighted(u, hp, beside=None):
                pool.wait_ge(wts_made, u + 1)
                pool.wait_ge(v_out, (u + 1) * SL)
                for n in range(N):
                    for ri in range(2):
                        i = u * SL + 2 * n + ri
                        pool.wait_ge(wv_made, i + 1)
                        vv = v[:, hp, :, ri, :].rearrange("p m (h d) -> p m h d", h=2)
                        w = wts[:, hp % 2, n].unsqueeze(3).broadcast_to([P, N, 2, HD])
                        o = wv[:, ri].rearrange("p m (h d) -> p m h d", h=2)
                        nc.gpsimd.tensor_tensor(o, vv, w, ALU.mult).then_inc(wv_mults, 1)
                        if beside is not None:
                            low_of_s(beside + 2 * n + ri, 2 * n + ri)
                        pool.wait_ge(wv_mults, i + 1)
                        pool.wait_ge(wv_free, i + 1)
                        nc.gpsimd.tensor_tensor(wv2[:, (2 * n + ri) % N], wv[:, ri, 0:2], wv[:, ri, 2:4],
                                                ALU.add).then_inc(wv_made, 1)

            for sl in range(SL):
                low_of_s(sl, sl)
            with pool.Fori(0, BT) as bt:
                for hp in range(HP):
                    weighted(bt * HP + hp, hp, beside=(bt + 1) * SL if hp == 1 else None)

        @block.vector
        def _(dve):
            for half in range(2):
                part = slice(half * HALF_B, (half + 1) * HALF_B)
                dve.wait_ge(b_set, 2 * half + 2)
                low_part(nc.vector, bias_flat[32:33, part], b_raw[32:33, part], b_hi[32:33]).then_inc(b_split, 1)
            dve.sem_inc(qk_free, 2)
            dve.sem_inc(scores_made, 2)
            dve.sem_inc(wv_free, N)
            dve.sem_inc(wv_made, 2)
            for i in range(PIECES):
                dve.wait_ge(wq_hi_made, i + 1)
                low_part(nc.vector, piece(wq_lo, i), w_stage(i), piece(wq_hi, i)).then_inc(wq_lo_made, 1)

            def scores(u, hp, groups):
                dve.wait_ge(qk_out, (u + 1) * SL)
                for g in groups:
                    dve.wait_ge(scores_made, u * GROUPS + g + 1)
                    slot = 0
                    for nm in (2 * g, 2 * g + 1):
                        n, m = nm // N, nm % N
                        for h in range(2):
                            cols = slice(h * HD, (h + 1) * HD)
                            keys = qk[:, hp % 2, m, :, P + h * HD:P + (h + 1) * HD]
                            for q, total in ((qk[:, hp % 2, n, :, cols], ar), (qx[:, hp % 2, n, :, cols], ai)):
                                ins = nc.vector.scalar_tensor_tensor(
                                    prod[:, g % 2, slot].rearrange("p (r d) -> p r d", r=2), q, 1.0, keys,
                                    ALU.mult, ALU.mult, accum_out=total[:, nm, h:h + 1])
                                slot += 1
                    ins.then_inc(scores_made, 1)

            def chained(u, n, ins):
                ins.then_inc(small, 1)
                dve.wait_ge(small, u * SMALLS + n)

            def magnitude(u):
                m2 = mag[:].rearrange("p n m h -> p (n m) h")
                dve.wait_ge(scores_made, (u + 1) * GROUPS + 2)
                dve.sem_inc(qk_free, 1)
                nc.vector.tensor_tensor(ar[:], ar[:], ar[:], ALU.mult)
                chained(u, 1, nc.vector.tensor_tensor(ai[:], ai[:], ai[:], ALU.mult))
                chained(u, 2, nc.vector.tensor_tensor(m2, ar[:], ai[:], ALU.add))
                nc.vector.tensor_scalar(mag[:], mag[:], MAG_EPS, None, ALU.add).then_inc(sq_ready, 1)

            def less_top(u):
                dve.wait_ge(mag_made, u + 1)
                chained(u, 3, nc.vector.tensor_reduce(top[:], mag[:].rearrange("p n m h -> p n h m"), AX_X, ALU.max))
                nc.vector.tensor_tensor(ex[:], mag[:], top[:].unsqueeze(2).broadcast_to([P, N, N, 2]),
                                        ALU.subtract).then_inc(exp_ready, 1)

            def weights(u, hp):
                dve.wait_ge(exp_made, u + 1)
                chained(u, 4, nc.vector.tensor_reduce(tot[:], ex[:].rearrange("p n m h -> p n h m"), AX_X, ALU.add))
                chained(u, 5, nc.vector.reciprocal(tot[:], tot[:]))
                nc.vector.tensor_tensor(wts[:, hp % 2], ex[:], tot[:].unsqueeze(2).broadcast_to([P, N, N, 2]),
                                        ALU.mult).then_inc(wts_made, 1)

            def weighted_sums(u, hp, half, stored):
                if half == 0 and (not isinstance(stored, int) or stored > 0):
                    dve.wait_ge(o_stored[hp % 2], 16 * stored)
                for i in range(half * N, half * N + N):
                    n, ri = i // 2, i % 2
                    dve.wait_ge(wv_made, u * SL + i + 3)
                    nc.vector.tensor_tensor(out[:, hp % 2, n, ri, :], wv2[:, i % N, 0], wv2[:, i % N, 1],
                                            ALU.add).then_inc(wv_free, 1)

            def unit(bt, hp):
                u = bt * HP + hp
                begun = not isinstance(u, int)
                scores(u, hp, range(0, 2))
                if begun or u >= 1:
                    less_top(u - 1)
                if begun or u >= 2:
                    weighted_sums(u - 2, (hp - 2) % HP, 0, bt * 2 + hp // 2 - 1)
                scores(u, hp, range(2, 4))
                if begun or u >= 1:
                    weights(u - 1, (hp - 1) % HP)
                scores(u, hp, range(4, 7))
                if begun or u >= 2:
                    weighted_sums(u - 2, (hp - 2) % HP, 1, 0)
                scores(u, hp, range(7, GROUPS))
                magnitude(u)

            for hp in range(HP):
                unit(0, hp)
            with dve.Fori(1, BT) as bt:
                for hp in range(HP):
                    unit(bt, hp)
            last = BT * HP - 1
            less_top(last)
            weights(last, HP - 1)
            for unit_left, hp in ((last - 1, HP - 2), (last, HP - 1)):
                for half in range(2):
                    weighted_sums(unit_left, hp, half, 2 * BT - 1)

        @block.tensor
        def _(pe):
            pe.wait_ge(b_split, 2)
            pe.wait_ge(consts_set, 2)

            def unit(u, hp, bt):
                pe.wait_ge(wq_lo_made, 2 * hp + 1)
                for sl in range(SL):
                    if sl == 1:
                        pe.wait_ge(wq_lo_made, 2 * hp + 2)
                    n, ri = sl // 2, sl % 2
                    out_ps = qkv_ps[:, sl % BANKS, 0:W3]
                    if not (isinstance(u, int) and u == 0 and sl < BANKS):
                        pe.wait_ge(qk_out, u * SL + sl - BANKS + 1)
                    if hp == 0:
                        pe.wait_ge(s_lo_made, bt * SL + sl + 1)
                    nc.tensor.matmul(out_ps, ones[:], bias[:, ri, hp, :], start=True, stop=False)
                    for dt in range(DT):
                        mm = mm3(nc, out_ps, (s_hi[:, sl, dt, :], s_lo[:, sl, dt, :]),
                                 (wq_hi[:, hp, ri, dt, :], wq_lo[:, hp, ri, dt, :]), False, dt == DT - 1)
                    mm.then_inc(qkv_done, 1)

            unit(0, 0, 0)
            with pe.Fori(0, BT) as bt:
                for hp in range(HP):
                    unit(bt * HP + hp + 1, (hp + 1) % HP, bt + (hp + 1) // HP)


def mixing_stage(nc, o_dram, w_o, b_o, w_int, ident_dram, r_dram):
    T, NP = 2, 2
    STEPS = BT // T
    COLS = NP * T * P
    G = NP * T
    TR_BANKS, WO_BANKS, RI_BANKS = 2, 2, 4
    RAW = 8
    RI = 3

    with ExitStack() as ctx:
        def sb(name, shape, dt):
            return ctx.enter_context(nc.sbuf_tensor(name, shape, dt))

        def sem(name):
            return ctx.enter_context(nc.semaphore(name))

        wo_hi, wo_lo = sb("wo_hi", [P, 2, DT, D], F32R), sb("wo_lo", [P, 2, DT, D], F32R)
        wi_hi, wi_lo = sb("wi_hi", [P, NP, 2, DT, D], F32R), sb("wi_lo", [P, NP, 2, DT, D], F32R)
        w_raw = sb("mix_w_raw", [P, RAW, D], F32)
        bo = sb("bo", [P, 2, DT], F32)
        ident = sb("mix_ident", [P, P], F32)
        o_raw = sb("o_raw", [P, T, NP, 2, D], F32)
        ot_hi, ot_lo = sb("ot_hi", [P, 2, DT, COLS], F32R), sb("ot_lo", [P, 2, DT, COLS], F32R)
        at_hi, at_lo = sb("at_hi", [P, 2, DT, COLS], F32R), sb("at_lo", [P, 2, DT, COLS], F32R)
        ri_out = sb("ri_out", [P, 2, 2, D], F32)

        tr_ps = ctx.enter_context(nc.psum_tensor("tr_ps", [P, TR_BANKS, COLS], F32))
        wo_ps = ctx.enter_context(nc.psum_tensor("wo_ps", [P, WO_BANKS, COLS], F32))
        ri_ps = ctx.enter_context(nc.psum_tensor("ri_ps", [P, RI_BANKS, D], F32))

        consts_in = sem("mix_consts_in")
        w_in = [sem(f"mix_w_in_{slot}") for slot in range(RAW)]
        w_hi_made, w_lo_made = sem("mix_w_hi_made"), sem("mix_w_lo_made")
        o_in, transposed, ot_hi_made, ot_lo_made = (
            sem("o_in"), sem("transposed"), sem("ot_hi_made"), sem("ot_lo_made"))
        wo_done, at_hi_made, at_lo_made = sem("wo_done"), sem("at_hi_made"), sem("at_lo_made")
        ri_done, r1_out, r_out, i_out = sem("ri_done"), sem("r1_out"), sem("r_out"), sem("i_out")
        r_stored = [sem("r_stored_0"), sem("r_stored_1")]

        WO_PIECES, WI_PIECES = 2 * DT, NP * 2 * DT

        def w_piece(i):
            if i < WO_PIECES:
                return [t[:].rearrange("p a b n -> p (a b) n")[:, i] for t in (wo_hi, wo_lo)]
            return [t[:].rearrange("p a b c n -> p (a b c) n")[:, (i - WO_PIECES) % WI_PIECES]
                    for t in (wi_hi, wi_lo)]

        def w_source(i):
            if i < WO_PIECES:
                return w_o[:, i]
            return w_int[:, i - WO_PIECES]

        FIRST = WO_PIECES + WI_PIECES
        TOTAL = FIRST + WI_PIECES

        block = ctx.enter_context(nc.Block())

        @block.sync
        def _(sp):
            sp.dma_start(ident[:], ident_dram).then_inc(consts_in, 16)
            sp.dma_start(bo[:], b_o).then_inc(consts_in, 16)

            def load_o(pair, step, nth):
                if not isinstance(nth, int):
                    sp.wait_ge(transposed, nth * 2 * DT)
                for t in range(T):
                    sp.dma_start(o_raw[:, t], o_dram[step * T + t, :, pair * NP:(pair + 1) * NP]).then_inc(o_in, 16)

            def load_w(i):
                if i >= RAW:
                    sp.wait_ge(w_lo_made, i - RAW + 1)
                sp.dma_start(w_raw[:, i % RAW], w_source(i)).then_inc(w_in[i % RAW], 16)

            load_o(0, 0, 0)
            for i in range(FIRST):
                load_w(i)
            with sp.Fori(1, STEPS) as step:
                load_o(0, step, step)
            for i in range(FIRST, FIRST + RAW):
                load_w(i)
            sp.wait_ge(transposed, STEPS * 2 * DT)
            load_o(1, 0, STEPS)
            for i in range(FIRST + RAW, TOTAL):
                load_w(i)
            with sp.Fori(1, STEPS) as step:
                load_o(1, step, step + STEPS)
            for slot in range(2):
                sp.wait_ge(r_stored[slot], 16 * 2 * STEPS * G // 2)

        def split_w_high(act, i):
            act.wait_ge(w_in[i % RAW], 16 * (i // RAW + 1))
            if i >= FIRST:
                groups = (i - FIRST) // (2 * DT) * T + T
                act.wait_ge(ri_done, ((STEPS - 1) * G + groups) * RI)
            nc.scalar.copy(w_piece(i)[0], w_raw[:, i % RAW]).then_inc(w_hi_made, 1)

        @block.gpsimd
        def _(pool):
            for i in range(TOTAL):
                pool.wait_ge(w_hi_made, i + 1)
                low_part(nc.gpsimd, w_piece(i)[1], w_raw[:, i % RAW], w_piece(i)[0]).then_inc(w_lo_made, 1)

        @block.scalar
        def _(act):
            act.wait_ge(consts_in, 32)

            def high_of_out(nth, ri, et):
                i = nth * 2 * DT + ri * DT + et
                act.wait_ge(transposed, i + 1)
                if not isinstance(nth, int) or nth > 0:
                    act.wait_ge(wo_done, nth * 2 * DT)
                nc.scalar.copy(ot_hi[:, ri, et], tr_ps[:, i % TR_BANKS if isinstance(i, int) else et % 2])\
                    .then_inc(ot_hi_made, 1)

            def step_body(pair, step, pieces=()):
                nth = pair * STEPS + step
                half = len(pieces) // 2
                for ri in range(2):
                    for et in range(DT):
                        part = ri * DT + et
                        for i in pieces[part * half // 8:(part + 1) * half // 8]:
                            split_w_high(act, i)
                        high_of_out(nth, ri, et)
                for ri in range(2):
                    for dt in range(DT):
                        part = ri * DT + dt
                        for i in pieces[half + part * half // 8:half + (part + 1) * half // 8]:
                            split_w_high(act, i)
                        act.wait_ge(wo_done, nth * 2 * DT + part + 1)
                        if not isinstance(nth, int) or nth > 0:
                            act.wait_ge(ri_done, nth * G * RI)
                        nc.scalar.activation(at_hi[:, ri, dt], wo_ps[:, dt % WO_BANKS], ACT.Identity,
                                             bias=bo[:, ri, dt:dt + 1]).then_inc(at_hi_made, 1)
                for g in range(G):
                    i = nth * G + g
                    slot = g % 2
                    act.wait_ge(ri_done, i * RI + 1)
                    if not isinstance(nth, int) or nth * G + g >= 2:
                        act.wait_ge(r_stored[slot], 16 * (nth * G // 2 + g // 2))
                    nc.scalar.copy(ri_out[:, slot, 0], ri_ps[:, (RI * g) % RI_BANKS]).then_inc(r1_out, 1)
                    act.wait_ge(ri_done, i * RI + 3)
                    nc.scalar.copy(ri_out[:, slot, 1], ri_ps[:, (RI * g + 2) % RI_BANKS]).then_inc(i_out, 1)
                    act.wait_ge(r_out, i + 1)
                    act.wait_ge(i_out, i + 1)
                    n, t = g // T, g % T
                    act.dma_start(r_dram[step * T + t, :, pair * NP + n], ri_out[:, slot]).then_inc(r_stored[slot], 16)

            for i in range(WO_PIECES // 2):
                split_w_high(act, i)
            step_body(0, 0, range(WO_PIECES // 2, FIRST))
            with act.Fori(1, STEPS) as step:
                step_body(0, step)
            step_body(1, 0, range(FIRST, TOTAL))
            with act.Fori(1, STEPS) as step:
                step_body(1, step)

        @block.vector
        def _(dve):
            dve.wait_ge(consts_in, 32)
            with dve.Fori(0, 2 * STEPS) as nth:
                for ri in range(2):
                    for et in range(DT):
                        dve.wait_ge(ot_hi_made, nth * 2 * DT + ri * DT + et + 1)
                        low_part(nc.vector, ot_lo[:, ri, et], tr_ps[:, et % TR_BANKS],
                                 ot_hi[:, ri, et]).then_inc(ot_lo_made, 1)
                for ri in range(2):
                    for dt in range(DT):
                        dve.wait_ge(at_hi_made, nth * 2 * DT + ri * DT + dt + 1)
                        nc.vector.scalar_tensor_tensor(at_lo[:, ri, dt], wo_ps[:, dt % WO_BANKS],
                                                       bo[:, ri, dt:dt + 1], at_hi[:, ri, dt].bitcast(F32),
                                                       ALU.add, ALU.subtract).then_inc(at_lo_made, 1)
                for g in range(G):
                    i = nth * G + g
                    dve.wait_ge(r1_out, i + 1)
                    dve.wait_ge(ri_done, i * RI + 2)
                    nc.vector.tensor_tensor(ri_out[:, g % 2, 0], ri_out[:, g % 2, 0],
                                            ri_ps[:, (RI * g + 1) % RI_BANKS], ALU.subtract).then_inc(r_out, 1)

        @block.tensor
        def _(pe):
            pe.wait_ge(consts_in, 32)

            def step_body(nth, pair):
                for t in range(T):
                    pe.wait_ge(o_in, 16 * (nth * T + T))
                for ri in range(2):
                    for et in range(DT):
                        i = nth * 2 * DT + ri * DT + et
                        bank = et % TR_BANKS
                        if not (isinstance(i, int) and i < TR_BANKS):
                            pe.wait_ge(ot_lo_made, i - TR_BANKS + 1)
                        for g in range(G):
                            n, t = g // T, g % T
                            tr = nc.tensor.transpose(tr_ps[:, bank, g * P:(g + 1) * P],
                                                     o_raw[:, t, n, ri, et * P:(et + 1) * P], ident[:])
                        tr.then_inc(transposed, 1)
                for ri in range(2):
                    for dt in range(DT):
                        i = nth * 2 * DT + ri * DT + dt
                        if not (isinstance(i, int) and i < WO_BANKS):
                            pe.wait_ge(at_lo_made, i - WO_BANKS + 1)
                        for et in range(DT):
                            if dt == 0:
                                pe.wait_ge(ot_lo_made, nth * 2 * DT + ri * DT + et + 1)
                                pe.wait_ge(w_lo_made, ri * DT + et + 1)
                            cols = slice(dt * P, (dt + 1) * P)
                            mm = mm3(nc, wo_ps[:, dt % WO_BANKS], (wo_hi[:, ri, et, cols], wo_lo[:, ri, et, cols]),
                                     (ot_hi[:, ri, et], ot_lo[:, ri, et]), et == 0, et == DT - 1)
                        mm.then_inc(wo_done, 1)
                pe.wait_ge(at_lo_made, (nth + 1) * 2 * DT)
                for g in range(G):
                    n = g // T
                    cols = slice(g * P, (g + 1) * P)
                    for q, terms in enumerate([[(0, 0)], [(1, 1)], [(0, 1), (1, 0)]]):
                        bank = (RI * g + q) % RI_BANKS
                        i = nth * G + g
                        if not (isinstance(nth, int) and RI * g + q < RI_BANKS):
                            before = RI * g + q - RI_BANKS
                            bg, bq = before // RI, before % RI
                            pe.wait_ge(i_out if bq == 2 else r_out, nth * G + bg + 1)
                        for x, (a, m) in enumerate(terms):
                            for dt in range(DT):
                                if g % T == 0:
                                    pe.wait_ge(w_lo_made, WO_PIECES + pair * WI_PIECES + (n * 2 + m) * DT + dt + 1)
                                mm = mm3(nc, ri_ps[:, bank], (at_hi[:, a, dt, cols], at_lo[:, a, dt, cols]),
                                         (wi_hi[:, n, m, dt], wi_lo[:, n, m, dt]),
                                         x == 0 and dt == 0, x == len(terms) - 1 and dt == DT - 1)
                        mm.then_inc(ri_done, 1)

            step_body(0, 0)
            with pe.Fori(1, STEPS) as step:
                step_body(step, 0)
            with pe.Fori(STEPS, 2 * STEPS) as step:
                step_body(step, 1)


class Chain:

    def __init__(self, engine, semaphore, per_tile):
        self.engine, self.semaphore, self.per_tile, self.tile, self.n = engine, semaphore, per_tile, 0, 0

    def start(self, tile):
        self.tile, self.n = tile, 0

    def step(self, instruction):
        self.n += 1
        instruction.then_inc(self.semaphore, 1)
        self.engine.wait_ge(self.semaphore, self.tile * self.per_tile + self.n)

    def end(self):
        assert self.n == self.per_tile, self.n


def top_stage(nc, r_dram, t_dram, ids, tables, w_head, w_top2, head_rows, ident_dram, y_dram):
    MEAS_R, MEAS_I, POST, TOP1 = 0, DT, 2 * DT, 3 * DT
    WP = 4 * DT
    D2 = D // 2
    TINY = 2.0 ** -116

    with ExitStack() as ctx:
        def sb(name, shape, dt):
            return ctx.enter_context(nc.sbuf_tensor(name, shape, dt))

        def sem(name):
            return ctx.enter_context(nc.semaphore(name))

        w_hi, w_lo = sb("wh_hi", [P, WP, D], F32R), sb("wh_lo", [P, WP, D], F32R)
        w2_hi, w2_lo = sb("w2_hi", [P, DT, D2], F32R), sb("w2_lo", [P, DT, D2], F32R)
        rows = sb("rows", [P, 3 * D + 2 * D2], F32)
        post_b, post_g, post_be = (rows[:, i * D:(i + 1) * D] for i in range(3))
        b_top2, w_top3 = (rows[:, 3 * D + i * D2:3 * D + (i + 1) * D2] for i in range(2))
        ident = sb("top_ident", [P, P], F32)
        idx = sb("idx", [P, BT, N], mybir.dt.int32)
        strength = sb("strength", [P, BT, N * N], F32)
        r = sb("states", [P, 2, N, 2, D], F32)
        sq = sb("sq", [P, 2, 2, D], F32)
        inv = sb("inv", [P, N, D], F32)
        zero = sb("zero", [P, N, D], F32)
        unit = sb("unit", [P, N, 2, D], F32)
        pair = sb("pair", [P, 2, D], F32)
        cos = sb("cos", [P, D], F32)
        wt = sb("wt", [P, N, D], F32)
        sup = sb("sup", [P, 2, D], F32)
        supn = sb("supn", [P, 2, D], F32)
        st_hi, st_lo = sb("st_hi", [P, 3, DT, P], F32R), sb("st_lo", [P, 3, DT, P], F32R)
        xt_hi, xt_lo = sb("xt_hi", [P, DT, P], F32R), sb("xt_lo", [P, DT, P], F32R)
        tx = sb("tx", [P, 2, DT, P], F32)
        msq = sb("msq", [P, 2, D], F32)
        row_a, row_b = sb("row_a", [P, D], F32), sb("row_b", [P, D], F32)
        h2 = sb("h2", [P, D2], F32)
        mean = sb("mean", [P, 1], F32)
        ssq, rn, rs = sb("ssq", [P, 1], F32), sb("rn", [P, 1], F32), sb("rs", [P, 1], F32)
        eps_ln, eps_n = sb("eps_ln", [P, 1], F32), sb("eps_n", [P, 1], F32)
        y = sb("y_sb", [P, BT], F32)

        def bank(name):
            return ctx.enter_context(nc.psum_tensor(name, [P, D], F32))

        t_ps = [bank("t_ps_0"), bank("t_ps_1")]
        m_ps = [bank("mr_ps"), bank("mi_ps")]
        post_ps, top1_ps, top2_ps = bank("post_ps"), bank("top1_ps"), bank("top2_ps")

        consts_in, ids_in, gathered, eps_set = sem("top_consts_in"), sem("ids_in"), sem("gathered"), sem("eps_set")
        w_in, w_hi_made, w_lo_made = sem("top_w_in"), sem("top_w_hi_made"), sem("top_w_lo_made")
        r_in = [sem("r_in_0"), sem("r_in_1")]
        sq_made, abs2_made, abs_made, inv_made = sem("sq_made"), sem("abs2_made"), sem("abs_made"), sem("inv_made")
        unit_made, wz_made, sup_made = sem("unit_made"), sem("wz_made"), sem("sup_made")
        ssq_made, norm_made, supn_made = sem("ssq_made"), sem("norm_made"), sem("supn_made")
        sup_t, st_hi_made, st_lo_made = sem("sup_t"), sem("st_hi_made"), sem("st_lo_made")
        measured, msq_made, amp2_made, amp_made = sem("measured"), sem("msq_made"), sem("amp2_made"), sem("amp_made")
        row_t, xt_hi_made, xt_lo_made = sem("row_t"), sem("xt_hi_made"), sem("xt_lo_made")
        post_done, mean_made, var_made, std_made, ln_made, z_made = (
            sem("post_done"), sem("mean_made"), sem("var_made"), sem("top_std_made"), sem("ln_made"), sem("z_made"))
        top1_done, h1_made, top2_done, y_made = sem("top1_done"), sem("h1_made"), sem("top2_done"), sem("y_made")
        superposing, dense_steps = sem("superposing"), sem("dense_steps")
        SUPERPOSING, DENSE_STEPS = 2 * N + (N - 1) * N + 4 * (N * (N - 1) // 2), 8
        y_stored = sem("y_stored")

        PIECES = WP + 2
        flat = lambda t: t[:].rearrange("p a n -> p (a n)")

        def w_piece(part, i):
            if i < WP:
                return (w_hi, w_lo)[part][:, i]
            return flat((w2_hi, w2_lo)[part])[:, (i - WP) * D:(i - WP + 1) * D]

        def w_stage(i):
            return unit[:].rearrange("p n r d -> p (n r) d")[:, i % 8]

        block = ctx.enter_context(nc.Block())

        @block.sync
        def _(sp):
            sp.dma_start(idx[:], ids).then_inc(ids_in, 16)
            sp.dma_start(rows[:], head_rows.partition_broadcast(P)).then_inc(consts_in, 16)
            sp.dma_start(ident[:], ident_dram).then_inc(consts_in, 16)

            def load(i, slot, k):
                sp.dma_start(r[:, slot], r_dram[i]).then_inc(r_in[slot], 16)
                src = t_dram[:, :, bass.ds(i * P, P)].rearrange("t p b -> p t b")
                sp.dma_start(tx[:, slot], src).then_inc(r_in[slot], 16)

            for slot in range(2):
                load(slot, slot, 0)
            for c in range(0, PIECES, 8):
                n = min(8, PIECES - c)
                if c:
                    sp.wait_ge(w_lo_made, c)
                for i in range(c, c + n):
                    src = w_head[:, i] if i < WP else w_top2[:, 2 * (i - WP):2 * (i - WP) + 2].rearrange("p a n -> p (a n)")
                    sp.dma_start(w_stage(i), src).then_inc(w_in, 16)
            with sp.Fori(1, BT // 2) as i:
                for slot in range(2):
                    sp.wait_ge(wz_made, (2 * i + slot - 1) * N)
                    sp.wait_ge(top1_done, 2 * i + slot - 1)
                    load(2 * i + slot, slot, i)
            sp.wait_ge(y_made, BT)
            sp.dma_start(y_dram, y[:]).then_inc(y_stored, 16)
            sp.wait_ge(y_stored, 16)

        def in_steps(engine, step):
            step(0, 0, True, False)
            step(1, 1, True, True)
            with engine.Fori(1, BT // 2) as k:
                step(2 * k, 0, True, True)
                step(2 * k + 1, 1, True, True)
            step(BT, 0, False, True)

        @block.gpsimd
        def _(pool):
            nc.gpsimd.memset(eps_ln[:], LN_EPS).then_inc(eps_set, 1)
            nc.gpsimd.memset(eps_n[:], MAG_EPS).then_inc(eps_set, 1)
            pool.wait_ge(ids_in, 16)
            for t in range(BT):
                for f in range(N):
                    pool.indirect_dma_start(
                        out=strength[:, t, f * N:(f + 1) * N], out_offset=None, in_=tables[f],
                        in_offset=bass.IndirectOffsetOnAxis(ap=idx[:, t, f:f + 1].bitcast(U32), axis=0),
                    ).then_inc(gathered, 16)

            def units(i, slot):
                pool.wait_ge(sup_made, i)
                if isinstance(i, int) and i == 0:
                    pool.wait_ge(w_lo_made, PIECES)
                for n in range(N):
                    pool.wait_ge(inv_made, i * N + n + 1)
                    by = inv[:, n].unsqueeze(1).broadcast_to([P, 2, D])
                    nc.gpsimd.tensor_tensor(unit[:, n], r[:, slot, n], by, ALU.mult).then_inc(unit_made, 1)

            def weighted(i, slot):
                for n in range(N):
                    pool.wait_ge(superposing, (i + 1) * SUPERPOSING)
                    by = wt[:, n].unsqueeze(1).broadcast_to([P, 2, D])
                    nc.gpsimd.tensor_tensor(unit[:, n], r[:, slot, n], by, ALU.mult).then_inc(wz_made, 1)

            def step(i, slot, s, d):
                if s:
                    units(i, slot)
                    weighted(i, slot)

            in_steps(pool, step)

        @block.scalar
        def _(act):
            for i in range(PIECES):
                act.wait_ge(w_in, 16 * min((i // 8 + 1) * 8, PIECES))
                nc.scalar.copy(w_piece(0, i), w_stage(i)).then_inc(w_hi_made, 1)
            act.wait_ge(eps_set, 2)

            def squares(i, slot, n):
                if n == 0:
                    act.wait_ge(r_in[slot], 16 * (i - slot) + 32)
                if not (isinstance(i, int) and i * N + n < 2):
                    act.wait_ge(abs2_made, i * N + n - 1)
                nc.scalar.activation(sq[:, n % 2], r[:, slot, n], ACT.Square).then_inc(sq_made, 1)

            def root(i, slot, n):
                act.wait_ge(abs2_made, i * N + n + 1)
                nc.scalar.activation(inv[:, n], inv[:, n], ACT.Sqrt).then_inc(abs_made, 1)

            def norm(i, slot):
                act.wait_ge(sup_made, i + 1)
                act.wait_ge(amp2_made, i)
                nc.scalar.activation(msq[:].rearrange("p a n -> p (a n)"), sup[:].rearrange("p a n -> p (a n)"),
                                     ACT.Square, accum_out=ssq[:]).then_inc(ssq_made, 1)
                act.wait_ge(ssq_made, i + 1)
                nc.scalar.activation(rn[:], ssq[:], ACT.Sqrt, bias=eps_n[:]).then_inc(norm_made, 1)

            def sup_high(i, slot):
                act.wait_ge(measured, 2 * i)
                for a, (part, scale) in enumerate([(0, 1.0), (1, 1.0), (1, -1.0)]):
                    act.wait_ge(sup_t, 2 * i + part + 1)
                    nc.scalar.activation(st_hi[:, a].rearrange("p t b -> p (t b)"), t_ps[part][:], ACT.Identity,
                                         scale=scale).then_inc(st_hi_made, 1)

            def measure_squares(i, slot):
                for part in range(2):
                    act.wait_ge(measured, 2 * i + part + 1)
                    act.wait_ge(ssq_made, i + 1)
                    nc.scalar.activation(msq[:, part], m_ps[part][:], ACT.Square).then_inc(msq_made, 1)

            def amplitude(i, slot):
                act.wait_ge(amp2_made, i + 1)
                nc.scalar.activation(row_a[:], row_a[:], ACT.Sqrt).then_inc(amp_made, 1)

            def row_high(i, slot, nth):
                act.wait_ge(row_t, 3 * i + nth + 1)
                act.wait_ge((top2_done, post_done, top1_done)[nth], i if nth == 0 else i + 1)
                nc.scalar.copy(xt_hi[:].rearrange("p t b -> p (t b)"), t_ps[nth % 2][:]).then_inc(xt_hi_made, 1)

            def post_root(i, slot):
                act.wait_ge(mean_made, i + 1)
                nc.scalar.activation(row_a[:], row_b[:], ACT.Square, bias=mean[:], accum_out=rs[:]).then_inc(var_made, 1)
                act.wait_ge(var_made, i + 1)
                nc.scalar.activation(rs[:], rs[:], ACT.Sqrt, bias=eps_ln[:], scale=1.0 / D).then_inc(std_made, 1)

            def post_gelu(i, slot):
                act.wait_ge(ln_made, i + 1)
                nc.scalar.activation(row_a[:], row_b[:], ACT.Gelu).then_inc(z_made, 1)

            def top1_relu(i, slot):
                act.wait_ge(top1_done, i + 1)
                nc.scalar.activation(row_b[:], top1_ps[:], ACT.Relu).then_inc(h1_made, 1)

            def step(i, slot, s, d):
                if s:
                    squares(i, slot, 0)
                    squares(i, slot, 1)
                    root(i, slot, 0)
                    root(i, slot, 1)
                    squares(i, slot, 2)
                    squares(i, slot, 3)
                if d:
                    norm(i - 1, 1 - slot)
                if s:
                    root(i, slot, 2)
                    root(i, slot, 3)
                if d:
                    sup_high(i - 1, 1 - slot)
                    measure_squares(i - 1, 1 - slot)
                    amplitude(i - 1, 1 - slot)
                    row_high(i - 1, 1 - slot, 0)
                    post_root(i - 1, 1 - slot)
                    post_gelu(i - 1, 1 - slot)
                    row_high(i - 1, 1 - slot, 1)
                    top1_relu(i - 1, 1 - slot)
                    row_high(i - 1, 1 - slot, 2)

            in_steps(act, step)

        @block.vector
        def _(dve):
            for i in range(PIECES):
                dve.wait_ge(w_hi_made, i + 1)
                low_part(nc.vector, w_piece(1, i), w_stage(i), w_piece(0, i)).then_inc(w_lo_made, 1)
            dve.wait_ge(consts_in, 32)
            dve.wait_ge(gathered, 16 * BT * N)

            supers = Chain(dve, superposing, SUPERPOSING)
            layers = Chain(dve, dense_steps, DENSE_STEPS)

            def magnitudes(i, slot, n):
                if n == 0:
                    supers.start(i)
                dve.wait_ge(sq_made, i * N + n + 1)
                supers.step(nc.vector.tensor_tensor(inv[:, n], sq[:, n % 2, 0], sq[:, n % 2, 1], ALU.add))
                supers.step(nc.vector.tensor_scalar(zero[:, n], inv[:, n], TINY, None, ALU.is_le))
                nc.vector.tensor_tensor(inv[:, n], inv[:, n], zero[:, n], ALU.add).then_inc(abs2_made, 1)

            def inverse(i, slot, n):
                dve.wait_ge(abs_made, i * N + n + 1)
                nc.vector.reciprocal(inv[:, n], inv[:, n]).then_inc(inv_made, 1)

            def s_ij(i, a, b):
                return strength[:, i, a * N + b:a * N + b + 1] if isinstance(i, int) else strength[:].rearrange("p t s -> p (t s)")[:, bass.ds(i * N * N + a * N + b, 1)]

            def of_zeros(i, slot, j):
                others = [a for a in range(N) if a != j]
                supers.step(nc.vector.tensor_scalar(wt[:, j], zero[:, others[0]], s_ij(i, others[0], j),
                                                    s_ij(i, j, j), ALU.mult, ALU.add))
                for a in others[1:]:
                    supers.step(nc.vector.scalar_tensor_tensor(wt[:, j], zero[:, a], s_ij(i, a, j), wt[:, j],
                                                               ALU.mult, ALU.add))

            def of_pair(i, slot, a, b):
                dve.wait_ge(unit_made, i * N + max(a, b) + 1)
                supers.step(nc.vector.tensor_tensor(pair[:], unit[:, a], unit[:, b], ALU.mult))
                supers.step(nc.vector.tensor_tensor(cos[:], pair[:, 0], pair[:, 1], ALU.add))
                for x, z in ((a, b), (b, a)):
                    supers.step(nc.vector.scalar_tensor_tensor(wt[:, z], cos[:], s_ij(i, x, z), wt[:, z],
                                                               ALU.mult, ALU.add))
                if (a, b) == (N - 2, N - 1):
                    supers.end()

            def sum_states(i, slot):
                layers.start(i)
                dve.wait_ge(wz_made, (i + 1) * N)
                layers.step(nc.vector.tensor_tensor(sup[:], unit[:, 0], unit[:, 1], ALU.add))
                layers.step(nc.vector.tensor_tensor(sup[:], sup[:], unit[:, 2], ALU.add))
                nc.vector.tensor_tensor(sup[:], sup[:], unit[:, 3], ALU.add).then_inc(sup_made, 1)

            def normalise(i, slot):
                dve.wait_ge(norm_made, i + 1)
                layers.step(nc.vector.reciprocal(rn[:], rn[:]))
                nc.vector.tensor_scalar(supn[:], sup[:], rn[:, 0:1], None, ALU.mult).then_inc(supn_made, 1)

            def sup_low(i, slot):
                for a, part in enumerate((0, 1, 1)):
                    dve.wait_ge(st_hi_made, 3 * i + (1 if a == 0 else 3))
                    lo, hi = (t[:, a].rearrange("p t b -> p (t b)") for t in (st_lo, st_hi))
                    if a < 2:
                        low_part(nc.vector, lo, t_ps[part][:], hi).then_inc(st_lo_made, 1)
                    else:
                        nc.vector.scalar_tensor_tensor(lo, t_ps[part][:], -1.0, hi.bitcast(F32),
                                                       ALU.mult, ALU.subtract).then_inc(st_lo_made, 1)

            def amplitude2(i, slot):
                dve.wait_ge(msq_made, 2 * i + 2)
                nc.vector.tensor_tensor(row_a[:], msq[:, 0], msq[:, 1], ALU.add).then_inc(amp2_made, 1)

            def row_low(i, slot, nth):
                dve.wait_ge(xt_hi_made, 3 * i + nth + 1)
                lo, hi = (t[:].rearrange("p t b -> p (t b)") for t in (xt_lo, xt_hi))
                low_part(nc.vector, lo, t_ps[nth % 2][:], hi).then_inc(xt_lo_made, 1)

            def post_stats(i, slot):
                dve.wait_ge(post_done, i + 1)
                layers.step(nc.vector.scalar_tensor_tensor(row_b[:], post_ps[:], 0.0, post_b, ALU.add, ALU.add,
                                                           accum_out=mean[:]))
                nc.vector.tensor_scalar(mean[:], mean[:], -1.0 / D, None, ALU.mult).then_inc(mean_made, 1)

            def post_norm(i, slot):
                dve.wait_ge(std_made, i + 1)
                layers.step(nc.vector.reciprocal(rs[:], rs[:]))
                layers.step(nc.vector.tensor_scalar(row_b[:], row_b[:], mean[:, 0:1], rs[:, 0:1],
                                                    ALU.add, ALU.mult))
                layers.step(nc.vector.tensor_tensor(row_b[:], row_b[:], post_g, ALU.mult))
                nc.vector.tensor_tensor(row_b[:], row_b[:], post_be, ALU.add).then_inc(ln_made, 1)

            def last_layer(i, slot):
                dve.wait_ge(top2_done, i + 1)
                layers.step(nc.vector.tensor_tensor(h2[:], top2_ps[:, 0:D2], b_top2, ALU.add))
                nc.vector.scalar_tensor_tensor(h2[:], h2[:], 0.0, w_top3, ALU.max, ALU.mult,
                                               accum_out=y[:, bass.ds(i, 1)]).then_inc(y_made, 1)
                layers.end()

            def step(i, slot, s, d):
                if s:
                    magnitudes(i, slot, 0)
                    magnitudes(i, slot, 1)
                if d:
                    sum_states(i - 1, 1 - slot)
                if s:
                    inverse(i, slot, 0)
                    magnitudes(i, slot, 2)
                if d:
                    normalise(i - 1, 1 - slot)
                if s:
                    inverse(i, slot, 1)
                    magnitudes(i, slot, 3)
                    inverse(i, slot, 2)
                if d:
                    sup_low(i - 1, 1 - slot)
                if s:
                    inverse(i, slot, 3)
                    of_zeros(i, slot, 0)
                    of_zeros(i, slot, 1)
                if d:
                    amplitude2(i - 1, 1 - slot)
                if s:
                    of_zeros(i, slot, 2)
                    of_zeros(i, slot, 3)
                if d:
                    row_low(i - 1, 1 - slot, 0)
                if s:
                    of_pair(i, slot, 0, 1)
                if d:
                    post_stats(i - 1, 1 - slot)
                if s:
                    of_pair(i, slot, 0, 2)
                if d:
                    post_norm(i - 1, 1 - slot)
                if s:
                    of_pair(i, slot, 1, 2)
                if d:
                    row_low(i - 1, 1 - slot, 1)
                if s:
                    of_pair(i, slot, 0, 3)
                    of_pair(i, slot, 1, 3)
                if d:
                    row_low(i - 1, 1 - slot, 2)
                if s:
                    of_pair(i, slot, 2, 3)
                if d:
                    last_layer(i - 1, 1 - slot)

            in_steps(dve, step)

        @block.tensor
        def _(pe):
            pe.wait_ge(consts_in, 32)
            pe.wait_ge(w_lo_made, PIECES)

            def transposes(to, of):
                for t in range(DT):
                    tr = nc.tensor.transpose(to[:, t * P:(t + 1) * P], of[:, t * P:(t + 1) * P], ident[:])
                return tr

            def product(out, of, first, start=True, stop=True, **more):
                for t in range(DT):
                    mm = mm3(nc, out, (of[0][:, t], of[1][:, t]), (w_hi[:, first + t], w_lo[:, first + t]),
                             start and t == 0, stop and t == DT - 1, **more)
                return mm

            def tile(i, slot):
                st = [(st_hi[:, a], st_lo[:, a]) for a in range(3)]
                xt = (xt_hi[:], xt_lo[:])
                pe.wait_ge(supn_made, i + 1)
                pe.wait_ge(xt_lo_made, 3 * i)
                for part in range(2):
                    transposes(t_ps[part], supn[:, part]).then_inc(sup_t, 1)
                pe.wait_ge(st_lo_made, 3 * i + 3)
                pe.wait_ge(msq_made, 2 * i)
                for part, terms in enumerate([((0, MEAS_R), (2, MEAS_I)), ((0, MEAS_I), (1, MEAS_R))]):
                    for x, (a, first) in enumerate(terms):
                        mm = product(m_ps[part][:], st[a], first, start=x == 0, stop=x == 1)
                    mm.then_inc(measured, 1)
                pe.wait_ge(amp_made, i + 1)
                transposes(t_ps[0], row_a).then_inc(row_t, 1)
                pe.wait_ge(xt_lo_made, 3 * i + 1)
                pe.wait_ge(ln_made, i)
                product(post_ps[:], xt, POST).then_inc(post_done, 1)
                pe.wait_ge(z_made, i + 1)
                transposes(t_ps[1], row_a).then_inc(row_t, 1)
                pe.wait_ge(xt_lo_made, 3 * i + 2)
                pe.wait_ge(h1_made, i)
                product(top1_ps[:], xt, TOP1, skip_group_check=True)
                pe.wait_ge(r_in[slot], 16 * (i - slot) + 32)
                for t in range(DT):
                    mm = nc.tensor.matmul(top1_ps[:, t * P:(t + 1) * P], tx[:, slot, t], ident[:],
                                          start=False, stop=True, skip_group_check=True)
                mm.then_inc(top1_done, 1)
                pe.wait_ge(h1_made, i + 1)
                transposes(t_ps[0], row_b).then_inc(row_t, 1)
                pe.wait_ge(xt_lo_made, 3 * i + 3)
                pe.wait_ge(y_made, i)
                for t in range(DT):
                    mm = mm3(nc, top2_ps[:, 0:D2], (xt[0][:, t], xt[1][:, t]), (w2_hi[:, t], w2_lo[:, t]),
                             t == 0, t == DT - 1)
                mm.then_inc(top2_done, 1)

            with pe.Fori(0, BT // 2) as k:
                for slot in range(2):
                    tile(2 * k + slot, slot)


def recurrent_tower(nc, xT, w_enc, enc_vec, b_top1, w_qkv, b_qkv, w_o, b_o, w_int, ident, w_head, w_top2,
                    head_rows, ids, tbl_0, tbl_1, tbl_2, tbl_3, y):
    s = nc.dram_tensor("s_both", (2, FT, P, B), F32).ap()
    x_top = nc.dram_tensor("x_top", (DT, P, B), F32).ap()
    attended = nc.dram_tensor("attended", (BT, P, N, 2, D), F32).ap()
    mixed = nc.dram_tensor("mixed", (BT, P, N, 2, D), F32).ap()
    encoder_stage(nc, xT, w_enc, enc_vec, b_top1, s, x_top)
    attention_stage(nc, s, w_qkv, b_qkv, attended)
    mixing_stage(nc, attended, w_o, b_o, w_int, ident, mixed)
    top_stage(nc, mixed, x_top, ids, [tbl_0, tbl_1, tbl_2, tbl_3], w_head, w_top2, head_rows, ident, y)


def _layouts(inputs):
    given = {name.replace("L0_rec_", ""): np.asarray(a) for name, a in inputs.items()}

    def encoder_chunks(w):
        return w.reshape(FT, P, 2, FT // 2, P).transpose(0, 2, 4, 3, 1).reshape(2 * FT, P, FT // 2, P)

    w_top1 = given["W_top1"]
    top_chunks = w_top1[D:].reshape(2, FT // 2, P, DT, P).transpose(3, 0, 2, 1, 4).reshape(2 * DT, P, FT // 2, P)
    qkv = [np.stack([given[f"W{q}_{part}"].T.reshape(DT, P, HP, P) for q in "qkv"], axis=3) for part in "ri"]
    int_w = np.stack([given["int_Wr"], given["int_Wi"]], axis=1).transpose(3, 0, 1, 2).reshape(DT, P, N, 2, D)
    return {
        "xT": given["r_x"].reshape(HALVES, HB, FT, P).transpose(0, 3, 2, 1),
        "w_enc": np.concatenate([encoder_chunks(given["er_W1"]), top_chunks, encoder_chunks(given["ei_W1"]),
                                 encoder_chunks(given["er_W2"]), encoder_chunks(given["ei_W2"])]),
        "enc_vec": np.stack([given[e + v].reshape(FT, P).T for v in ("_b1", "_g1", "_be1", "_b2")
                             for e in ("er", "ei")], axis=1),
        "b_top1": given["b_top1"].reshape(DT, P).T,
        "w_qkv": np.stack(qkv, axis=2).reshape(DT, P, 2, HP, 3 * P).transpose(1, 3, 2, 0, 4).reshape(P, -1),
        "b_qkv": np.stack([np.stack([given[f"b{q}_{part}"].reshape(HP, P) for q in "qkv"], axis=1)
                           for part in "ri"]).reshape(-1),
        "w_o": np.stack([given["Wo_" + part].T.reshape(DT, P, D).transpose(1, 0, 2) for part in "ri"],
                        axis=1).reshape(P, 2 * DT, D),
        "b_o": np.stack([given["bo_" + part].reshape(DT, P).T for part in "ri"], axis=1),
        "w_int": int_w.transpose(1, 2, 3, 0, 4).reshape(P, N * 2 * DT, D),
        "ident": np.eye(P, dtype=np.float32),
        "w_head": np.concatenate([given["meas_Mr"].T, given["meas_Mi"].T, given["post_W"].T, w_top1[:D]])
                    .reshape(4 * DT, P, D).transpose(1, 0, 2),
        "w_top2": given["W_top2"].reshape(DT, P, D // 2).transpose(1, 0, 2),
        "head_rows": np.concatenate([given["post_b"], given["post_g"], given["post_be"], given["b_top2"],
                                     given["W_top3"][:, 0]]),
        "ids": given["ids"].reshape(BT, P, N).transpose(1, 0, 2),
        "tbl_0": given["tbl_0"], "tbl_1": given["tbl_1"], "tbl_2": given["tbl_2"], "tbl_3": given["tbl_3"],
    }


def kernel(**inputs):
    import concourse.bacc as _bacc
    from concourse.bass_utils import run_bass_kernel_spmd as _run

    nc = _bacc.Bacc("TRN2", target_bir_lowering=False, num_devices=1)
    arrays = {name: np.ascontiguousarray(a) for name, a in _layouts(inputs).items()}
    args = [nc.dram_tensor(name, a.shape, mybir.dt.from_np(a.dtype), kind="ExternalInput").ap()
            for name, a in arrays.items()]
    y = nc.dram_tensor("y", (P, BT), F32, kind="ExternalOutput").ap()
    recurrent_tower(nc, *args, y)
    results = _run(nc, [arrays], core_ids=[0])
    return results.results[0]["y"].T.reshape(B, 1)
```

```python
from contextlib import ExitStack

import concourse.bass as bass
import numpy as np
from concourse import mybir

ALU = mybir.AluOpType
ACT = mybir.ActivationFunctionType
AX_X = mybir.AxisListType.X
F32 = mybir.dt.float32
F32R = mybir.dt.float32r
BF16 = mybir.dt.bfloat16
U32 = mybir.dt.uint32

P = 128
B = 1024
HB = 512
HALVES = B // HB
BT = B // P
K = 2048
FT = K // P
D = 512
DT = D // P
N = 4
H = 8
HD = D // H
HP = H // 2
LN_EPS = 1e-5
MAG_EPS = 1e-8
VEC_B1, VEC_G, VEC_BE, VEC_B2 = 0, 2, 4, 6


def mm3(nc, out, w, x, start, stop, **more):
    (w_hi, w_lo), (x_hi, x_lo) = w, x
    nc.tensor.matmul(out, w_hi, x_hi, start=start, stop=False, **more)
    nc.tensor.matmul(out, w_hi, x_lo, start=False, stop=False, **more)
    return nc.tensor.matmul(out, w_lo, x_hi, start=False, stop=stop, **more)


def low_part(engine, lo, full, hi):
    return engine.tensor_tensor(lo, full, hi.bitcast(F32), ALU.subtract)


def encoder_stage(nc, xT, w_enc, enc_vec, b_top1, s_dram, t_dram):
    CK = 4
    CHUNKS = FT // CK
    L1_R, TOP, L1_I, L2_R, L2_I = range(5)
    TILES = [FT, DT, FT, FT, FT]
    START = [sum(TILES[:g]) for g in range(5)]
    HT = sum(TILES)
    HC = HT * CHUNKS
    ENC = {L1_R: 0, L1_I: 1, L2_R: 0, L2_I: 1}
    OUT_START = {TOP: 0, L2_R: DT, L2_I: DT + FT}
    OUT_TILES = DT + 2 * FT

    with ExitStack() as ctx:
        def sb(name, shape, dt):
            return ctx.enter_context(nc.sbuf_tensor(name, shape, dt))

        def sem(name):
            return ctx.enter_context(nc.semaphore(name))

        x_hi = sb("x_hi", [P, FT, HB], F32R)
        x_lo = sb("x_lo", [P, FT, HB], F32R)
        h_lo = sb("h_lo", [P, FT, HB], F32R)
        h_hi = sb("h_hi", [P, FT, HB], F32R)
        pre_r = nc.alloc_sbuf_tensor_at("pre_r", [P, FT, HB], F32, offset=nc.sbuf_base - FT * HB * 4)
        pre_i = sb("pre_i", [P, FT, HB], F32)
        w_raw = sb("w_raw", [P, CHUNKS, CK, P], F32)
        w_hi = sb("w_hi", [P, CHUNKS, CK, P], F32R)
        w_lo = sb("w_lo", [P, CHUNKS, CK, P], F32R)
        acc = sb("acc", [P, HB], F32)
        acc2 = sb("acc2", [P, HB], F32)
        rstd = sb("rstd", [P, HB], F32)
        norm = sb("norm", [P, 2, HB], F32)
        gelu = sb("gelu", [P, 2, HB], F32)
        s_out = sb("s_out", [P, 2, HB], F32)
        vec = sb("vec", [P, 8, FT], F32)
        vec_top = sb("vec_top", [P, DT], F32)
        ones = sb("ones", [P, P], F32)
        eps = sb("eps", [P, 1], F32)

        x_in = [sem(f"x_in_{group}") for group in range(FT // CK)]
        vec_in = sem("vec_in")
        w_in = [sem(f"w_in_{slot}") for slot in range(CHUNKS)]
        consts_set = sem("consts_set")
        x_hi_made, x_lo_made = sem("x_hi_made"), sem("x_lo_made")
        w_hi_made, w_lo_made, w_used = sem("w_hi_made"), sem("w_lo_made"), sem("w_used")
        tile_out = sem("tile_out")
        cleared, summed = sem("cleared"), sem("summed")
        centred, squared, sq_summed = sem("centred"), sem("squared"), sem("sq_summed")
        stats_done, std_made, rstd_made = sem("stats_done"), sem("std_made"), sem("rstd_made")
        normed, gelu_made = sem("normed"), sem("gelu_made")
        hid_hi_made, hid_lo_made = sem("hid_hi_made"), sem("hid_lo_made")
        stored = [sem("stored_0"), sem("stored_1")]

        START_AT_ONE = [w_lo_made, w_used, summed, sq_summed, *stored]
        START_AT_TWO = [tile_out, gelu_made, hid_lo_made]

        mm_ps = ctx.enter_context(nc.psum_tensor("enc_mm", [P, 2, HB], F32))
        st_ps = ctx.enter_context(nc.psum_tensor("enc_stats", [P, 2, HB], F32))
        moving = [(x_hi, x_lo), (x_hi, x_lo), (x_hi, x_lo), (h_hi, h_lo), (x_hi, x_lo)]
        pre = [pre_r, pre_i]
        hidden = [(h_hi, h_lo), (x_hi, x_lo)]
        BESIDE = [None, None, 0, 1, None]

        block = ctx.enter_context(nc.Block())

        @block.sync
        def _(sp):
            def load_x(h):
                for group, arrived in enumerate(x_in):
                    ks = slice(group * CK, (group + 1) * CK)
                    sp.dma_start(pre_i[:, ks, :], xT[h, :, ks, :]).then_inc(arrived, 16)

            def load_chunk(tile, source, ch):
                if not isinstance(tile, int) or tile > 0:
                    sp.wait_ge(w_lo_made, 1 + (tile - 1) * CHUNKS + ch + 1)
                k = (ch % 2) * CK
                sp.dma_start(w_raw[:, ch], w_enc[2 * source + ch // 2, :, k:k + CK]).then_inc(w_in[ch], 16)

            def load_tile(tile, source):
                for ch in range(CHUNKS):
                    load_chunk(tile, source, ch)

            sp.dma_start(vec[:], enc_vec).then_inc(vec_in, 16)
            sp.dma_start(vec_top[:], b_top1).then_inc(vec_in, 16)
            load_tile(0, 0)
            load_x(0)
            AHEAD = START[L2_I] + 2
            with sp.Fori(1, AHEAD) as tile:
                load_tile(tile, tile)
            sp.wait_ge(normed, 2 * FT)
            load_x(1)
            with sp.Fori(AHEAD, HT) as tile:
                load_tile(tile, tile)
            with sp.Fori(0, HT) as tile:
                load_tile(tile + HT, tile)
            load_tile(2 * HT, 0)

        @block.gpsimd
        def _(pool):
            nc.gpsimd.memset(ones[:], 1.0 / K).then_inc(consts_set, 1)
            nc.gpsimd.memset(eps[:], LN_EPS).then_inc(consts_set, 1)
            for semaphore in START_AT_ONE:
                pool.sem_inc(semaphore, 1)
            for semaphore in START_AT_TWO:
                pool.sem_inc(semaphore, 2)
            with pool.Fori(0, HALVES * HT + 1) as tile:
                for ch in range(CHUNKS):
                    pool.wait_ge(w_hi_made, tile * CHUNKS + ch + 1)
                    low_part(nc.gpsimd, w_lo[:, ch], w_raw[:, ch], w_hi[:, ch]).then_inc(w_lo_made, 1)

        @block.scalar
        def _(act):
            def high_of_chunk(tile, ch):
                act.wait_ge(w_in[ch], 16 * (tile + 1))
                if not isinstance(tile, int):
                    act.wait_ge(w_used, 1 + (tile - 1) * CHUNKS + ch + 1)
                nc.scalar.copy(w_hi[:, ch], w_raw[:, ch]).then_inc(w_hi_made, 1)

            def square(h, e, k):
                nth = (2 * h + e) * FT + k
                act.wait_ge(centred, nth + 1)
                act.wait_ge(sq_summed, 1 + nth)
                nc.scalar.activation(norm[:, 0], pre[e][:, k, :], ACT.Square).then_inc(squared, 1)

            def gelu_tile(h, e, k, slot):
                nth = (2 * h + e) * FT + k
                act.wait_ge(normed, nth + 1)
                act.wait_ge(hid_lo_made, 2 + nth - 1)
                nc.scalar.activation(gelu[:, slot], norm[:, slot], ACT.Gelu,
                                     bias=vec[:, VEC_BE + e, bass.ds(k, 1)],
                                     scale=vec[:, VEC_G + e, bass.ds(k, 1)]).then_inc(gelu_made, 1)
                act.wait_ge(gelu_made, 2 + nth + 1)
                nc.scalar.copy(hidden[e][0][:, k, :], gelu[:, slot]).then_inc(hid_hi_made, 1)

            def tile_to_sbuf(h, g, f, slot):
                nth = h * HT + START[g] + f
                act.wait_ge(w_used, 1 + CHUNKS * (nth + 1))
                if g in (L1_R, L1_I):
                    nc.scalar.activation(pre[ENC[g]][:, f, :], mm_ps[:, slot], ACT.Identity,
                                         bias=vec[:, VEC_B1 + ENC[g], bass.ds(f, 1)]).then_inc(tile_out, 1)
                    return
                act.wait_ge(stored[slot], 1 + 8 * (h * OUT_TILES + OUT_START[g] + f - slot))
                bias = vec_top[:, bass.ds(f, 1)] if g == TOP else vec[:, VEC_B2 + ENC[g], bass.ds(f, 1)]
                nc.scalar.activation(s_out[:, slot], mm_ps[:, slot], ACT.Identity, bias=bias).then_inc(tile_out, 1)
                act.wait_ge(tile_out, 2 + nth + 1)
                to = t_dram[f] if g == TOP else s_dram[ENC[g], f]
                act.dma_start(to[:, bass.ds(h * HB, HB)], s_out[:, slot]).then_inc(stored[slot], 16)

            act.wait_ge(vec_in, 32)
            for ch in range(CHUNKS):
                high_of_chunk(0, ch)
            with act.Fori(0, HALVES) as h:
                for k in range(FT):
                    act.wait_ge(x_in[k // CK], 16 * (h + 1))
                    act.wait_ge(w_used, 1 + h * HC)
                    nc.scalar.copy(x_hi[:, k, :], pre_i[:, k, :]).then_inc(x_hi_made, 1)
                for g in range(5):
                    e = BESIDE[g]
                    IT = TILES[g] // 2
                    for part in range(2):
                        if e is not None and part == 1:
                            act.wait_ge(stats_done, 4 * h + 2 * e + 2)
                            nc.scalar.activation(acc2[:], st_ps[:, 1], ACT.Sqrt, bias=eps[:]).then_inc(std_made, 1)
                        with act.Fori(part * IT // 2, (part + 1) * IT // 2) as it:
                            for j in range(2):
                                f = 2 * it + j
                                nth = h * HT + START[g] + f
                                for ch in range(CHUNKS):
                                    high_of_chunk(nth + 1, ch)
                                    second = ch // 2
                                    k = 2 * f + second - part * FT
                                    if ch % 2 == 0 or e is None:
                                        continue
                                    if part == 0:
                                        square(h, e, k)
                                    else:
                                        if j == 0 and second == 0 and g == L2_R:
                                            act.wait_ge(w_used, 1 + h * HC + CHUNKS * START[L2_R])
                                        gelu_tile(h, e, k, second)
                                tile_to_sbuf(h, g, f, j)
            for slot in range(2):
                act.wait_ge(stored[slot], 1 + 8 * HALVES * OUT_TILES)

        @block.vector
        def _(dve):
            dve.wait_ge(consts_set, 2)
            with dve.Fori(0, HALVES) as h:
                for k in range(FT):
                    dve.wait_ge(x_hi_made, h * FT + k + 1)
                    low_part(nc.vector, x_lo[:, k, :], pre_i[:, k, :], x_hi[:, k, :]).then_inc(x_lo_made, 1)
                for g in (L1_R, L1_I, L2_R):
                    e = BESIDE[g]
                    IT = TILES[g] // 2
                    if g == L1_R:
                        nc.vector.memset(acc[:], 0.0).then_inc(cleared, 1)
                    for part in range(2):
                        if e is not None and part == 0:
                            dve.wait_ge(stats_done, 4 * h + 2 * e + 1)
                            nc.vector.memset(acc[:], 0.0).then_inc(cleared, 1)
                            nc.vector.memset(acc2[:], 0.0).then_inc(cleared, 1)
                        if e is not None and part == 1:
                            dve.wait_ge(std_made, 2 * h + e + 1)
                            nc.vector.reciprocal(rstd[:], acc2[:]).then_inc(rstd_made, 1)
                        with dve.Fori(part * IT // 2, (part + 1) * IT // 2) as it:
                            for j in range(2):
                                f = 2 * it + j
                                for second in range(2):
                                    k = 2 * f + second - part * FT
                                    if e is None:
                                        continue
                                    nth = (2 * h + e) * FT + k
                                    if part == 0:
                                        nc.vector.tensor_tensor(pre[e][:, k, :], pre[e][:, k, :], st_ps[:, 0],
                                                                ALU.subtract).then_inc(centred, 1)
                                        dve.wait_ge(cleared, 5 * h + 1 + 2 * e + 2)
                                        dve.wait_ge(squared, nth + 1)
                                        nc.vector.tensor_tensor(acc2[:], acc2[:], norm[:, 0],
                                                                ALU.add).then_inc(sq_summed, 1)
                                    else:
                                        dve.wait_ge(gelu_made, 2 + nth - 1)
                                        dve.wait_ge(rstd_made, 2 * h + e + 1)
                                        nc.vector.tensor_tensor(norm[:, second], pre[e][:, k, :], rstd[:],
                                                                ALU.mult).then_inc(normed, 1)
                                        dve.wait_ge(hid_hi_made, nth + 1)
                                        low_part(nc.vector, hidden[e][1][:, k, :], gelu[:, second],
                                                 hidden[e][0][:, k, :]).then_inc(hid_lo_made, 1)
                                if g != L2_R:
                                    dve.wait_ge(tile_out, 2 + h * HT + START[g] + f + 1)
                                    if g == L1_R:
                                        dve.wait_ge(cleared, 5 * h + 1)
                                    dve.wait_ge(summed, 1 + (2 * h + ENC[g]) * FT + f)
                                    nc.vector.tensor_tensor(acc[:], acc[:], pre[ENC[g]][:, f, :],
                                                            ALU.add).then_inc(summed, 1)

        @block.tensor
        def _(pe):
            pe.wait_ge(consts_set, 2)

            def mean_of(h, e, part):
                pe.wait_ge(sq_summed if part else summed, 1 + (2 * h + e + 1) * FT)
                nc.tensor.matmul(st_ps[:, part], ones[:], (acc2 if part else acc)[:],
                                 start=True, stop=True).then_inc(stats_done, 1)

            def product_tile(h, g, f, slot, first=False, mean=None):
                nth = h * HT + START[g] + f
                for ch in range(CHUNKS):
                    if g in (L2_R, L2_I):
                        pe.wait_ge(hid_lo_made, 2 + (2 * h + ENC[g]) * FT + (ch + 1) * CK)
                    pe.wait_ge(w_lo_made, 1 + CHUNKS * nth + ch + 1)
                    if ch == 0:
                        pe.wait_ge(tile_out, 2 + nth - 1)
                    for kk in range(CK):
                        k = ch * CK + kk
                        if first:
                            pe.wait_ge(x_lo_made, h * FT + k + 1)
                        mm = mm3(nc, mm_ps[:, slot], (w_hi[:, ch, kk, :], w_lo[:, ch, kk, :]),
                                 (moving[g][0][:, k, :], moving[g][1][:, k, :]), k == 0, k == FT - 1)
                    mm.then_inc(w_used, 1)
                    if mean is not None and ch == 0:
                        mean_of(h, BESIDE[g], mean)

            with pe.Fori(0, HALVES) as h:
                for g in range(5):
                    IT = TILES[g] // 2
                    for part in range(2):
                        start = part * IT // 2
                        if BESIDE[g] is not None or (g == L1_R and part == 0):
                            for j in range(2):
                                product_tile(h, g, 2 * start + j, j, first=g == L1_R,
                                             mean=part if BESIDE[g] is not None and j == 0 else None)
                            start += 1
                        with pe.Fori(start, (part + 1) * IT // 2) as it:
                            for j in range(2):
                                product_tile(h, g, 2 * it + j, j)


def attention_stage(nc, s_dram, w_qkv, b_qkv, o_dram):
    W3 = 3 * P
    SL = 2 * N
    BANKS = 4

    with ExitStack() as ctx:
        def sb(name, shape, dt):
            return ctx.enter_context(nc.sbuf_tensor(name, shape, dt))

        def sem(name):
            return ctx.enter_context(nc.semaphore(name))

        wq_hi = sb("wq_hi", [P, HP, 2, DT, W3], F32R)
        wq_lo = sb("wq_lo", [P, HP, 2, DT, W3], F32R)
        bias = sb("bias", [P, 2, HP, W3], F32R)
        ones = sb("ones_r", [P, P], F32R)
        s_raw = sb("s_raw", [P, 4, DT, P], F32)
        s_hi = sb("s_hi", [P, SL, DT, P], F32R)
        s_lo = sb("s_lo", [P, SL, DT, P], F32R)
        qk = sb("qk", [P, 2, N, 2, 2 * P], F32)
        v = sb("v", [P, HP, N, 2, P], F32)
        qx = sb("qx", [P, 2, N, 2, P], F32)
        wv = sb("wv", [P, 2, N, P], F32)
        wv2 = sb("wv2", [P, N, 2, P], F32)
        out = sb("out_bd", [P, 2, N, 2, P], F32)
        ar = sb("ar", [P, N * N, 2], F32)
        ai = sb("ai", [P, N * N, 2], F32)
        mag = sb("mag", [P, N, N, 2], F32)
        top = sb("top", [P, N, 2], F32)
        ex = sb("ex", [P, N, N, 2], F32)
        tot = sb("tot", [P, N, 2], F32)
        wts = sb("wts", [P, 2, N, N, 2], F32)

        qkv_ps = ctx.enter_context(nc.psum_tensor("qkv_ps", [P, BANKS, 512], F32))

        GROUPS = N * N // 2
        prod = ctx.enter_context(nc.psum_tensor("prod", [P, 2, 8, P], F32))

        consts_set = sem("att_consts_set")
        b_in, b_split, b_set = sem("b_in"), sem("b_split"), sem("b_set")
        wq_in = [sem("wq_in_0"), sem("wq_in_1")]
        wq_hi_made, wq_lo_made = sem("wq_hi_made"), sem("wq_lo_made")
        s_in = [sem(f"s_in_{i}") for i in range(4)]
        s_hi_made, s_lo_made = sem("s_hi_made"), sem("s_lo_made")
        qkv_done, qk_out, v_out = sem("qkv_done"), sem("qk_out"), sem("v_out")
        qk_free, wv_free, wv_made, scores_made = sem("qk_free"), sem("wv_free"), sem("wv_made"), sem("scores_made")
        small = sem("small")
        sq_ready, mag_made, exp_ready, exp_made, wts_made = (
            sem("sq_ready"), sem("mag_made"), sem("exp_ready"), sem("exp_made"), sem("wts_made"))
        wv_mults, last_made = sem("wv_mults"), sem("last_made")
        o_stored = [sem("o_stored_0"), sem("o_stored_1")]

        PIECES = 2 * HP
        PN = DT * W3
        BN = 2 * HP * W3

        def flat(t):
            return t[:].rearrange("p a b c d -> p (a b c d)")

        def piece(t, i):
            return flat(t)[:, i * PN:(i + 1) * PN]

        v_half = HP // 2 * N * 2 * P

        def w_stage(i):
            return flat(v)[:, v_half:v_half + PN] if i % 2 else flat(out)[:, 0:PN]

        b_raw = flat(v)[:, 0:BN]
        b_hi = flat(qk)[:, 0:BN]
        bias_flat = bias[:].rearrange("p a b c -> p (a b c)")
        SMALLS = 5

        block = ctx.enter_context(nc.Block())

        @block.sync
        def _(sp):
            for row in (0, 32):
                sp.dma_start(b_raw[row:row + 1], b_qkv.unsqueeze(0)).then_inc(b_in, 16)

            def load_w(i):
                if i == 1:
                    sp.wait_ge(b_split, 1)
                if i >= 2:
                    sp.wait_ge(wq_lo_made, i - 1)
                sp.dma_start(w_stage(i), w_qkv[:, i * PN:(i + 1) * PN]).then_inc(wq_in[i % 2], 16)

            def load_s(nth, bt, sl):
                if not isinstance(nth, int) or nth >= 4:
                    sp.wait_ge(s_lo_made, nth - 3)
                n, ri = sl // 2, sl % 2
                src = s_dram[ri, n * DT:(n + 1) * DT, :, bass.ds(bt * P, P)].rearrange("t p b -> p t b")
                sp.dma_start(s_raw[:, sl % 4], src).then_inc(s_in[sl % 4], 16)

            def store(bt, hp):
                sp.wait_ge(wv_free, (bt * HP + hp + 1) * SL + N)
                sp.dma_start(o_dram[bt, :, :, :, hp * P:(hp + 1) * P], out[:, hp % 2]).then_inc(o_stored[hp % 2], 16)

            def tile(bt, following):
                for sl in range(4):
                    load_s((bt + 1) * SL + sl, following, sl)
                store(bt, 0)
                for sl in range(4, SL):
                    load_s((bt + 1) * SL + sl, following, sl)
                for hp in range(1, HP):
                    store(bt, hp)

            load_w(0)
            for sl in range(2):
                load_s(sl, 0, sl)
            load_w(1)
            for sl in range(2, 4):
                load_s(sl, 0, sl)
            load_w(2)
            for sl in range(4, SL):
                load_s(sl, 0, sl)
            for i in range(3, PIECES):
                load_w(i)
            with sp.Fori(0, BT - 1) as bt:
                tile(bt, bt + 1)
            for hp in range(HP):
                store(BT - 1, hp)
            for slot in range(2):
                sp.wait_ge(o_stored[slot], 16 * BT * HP // 2)

        @block.scalar
        def _(act):
            act.wait_ge(b_in, 32)
            nc.scalar.copy(b_hi[32:33].bitcast(F32R), b_raw[32:33]).then_inc(b_set, 1)
            act.wait_ge(consts_set, 2)
            nc.scalar.copy(bias_flat[0:1], b_raw[0:1]).then_inc(b_set, 1)

            def high_of_w(i):
                act.wait_ge(wq_in[i % 2], 16 * (i // 2 + 1))
                nc.scalar.copy(piece(wq_hi, i), w_stage(i)).then_inc(wq_hi_made, 1)

            def high_of_s(sl, nth_in_slot):
                act.wait_ge(s_in[sl % 4], 16 * nth_in_slot)
                nc.scalar.copy(s_hi[:, sl], s_raw[:, sl % 4]).then_inc(s_hi_made, 1)

            def copies(u, hp, next_bt=None):
                act.wait_ge(qk_free, u + 1)
                for sl in range(SL):
                    if isinstance(u, int) and u == 0 and sl + 3 < PIECES:
                        high_of_w(sl + 3)
                    act.wait_ge(qkv_done, u * SL + sl + 1)
                    n, ri = sl // 2, sl % 2
                    nc.scalar.copy(v[:, hp, n, ri, :], qkv_ps[:, sl % BANKS, 2 * P:W3]).then_inc(v_out, 1)
                    nc.scalar.mul(qx[:, hp % 2, n, 1 - ri, :], qkv_ps[:, sl % BANKS, 0:P], 1.0 if ri else -1.0)
                    nc.scalar.copy(qk[:, hp % 2, n, ri, :], qkv_ps[:, sl % BANKS, 0:2 * P]).then_inc(qk_out, 1)
                    if next_bt is not None:
                        high_of_s(sl, next_bt * 2 + sl // 4 + 1)

            high_of_w(0)
            for sl in range(2):
                high_of_s(sl, 1)
            high_of_w(1)
            for sl in range(2, 4):
                high_of_s(sl, 1)
            high_of_w(2)
            for sl in range(4, SL):
                high_of_s(sl, 2)
            copies(0, 0)

            def softmax(u):
                act.wait_ge(sq_ready, u + 1)
                nc.scalar.activation(mag[:], mag[:], ACT.Sqrt, scale=1.0 / HD).then_inc(mag_made, 1)
                act.wait_ge(exp_ready, u + 1)
                nc.scalar.activation(ex[:], ex[:], ACT.Exp).then_inc(exp_made, 1)

            with act.Fori(0, BT - 1) as bt:
                for hp in range(HP):
                    copies(bt * HP + hp + 1, (hp + 1) % HP, bt + 1 if hp == HP - 2 else None)
                    softmax(bt * HP + hp)
            for hp in range(HP):
                u = (BT - 1) * HP + hp
                if hp < HP - 1:
                    copies(u + 1, hp + 1)
                softmax(u)

        @block.gpsimd
        def _(pool):
            nc.gpsimd.memset(bias[:].bitcast(F32), 0.0).then_inc(consts_set, 1)
            nc.gpsimd.memset(ones[:].bitcast(F32), 1.0).then_inc(consts_set, 1)

            def low_of_s(nth, sl):
                pool.wait_ge(s_hi_made, nth + 1)
                low_part(nc.gpsimd, s_lo[:, sl], s_raw[:, sl % 4], s_hi[:, sl]).then_inc(s_lo_made, 1)

            WITH_WEIGHTED = [1, 2, 2, 1, 2, 0, 0, 0]

            def weighted(u, hp, beside=None):
                pool.wait_ge(wts_made, u + 1)
                pool.wait_ge(v_out, (u + 1) * SL)
                for n in range(N):
                    for ri in range(2):
                        i = u * SL + 2 * n + ri
                        pool.wait_ge(wv_made, i + 1)
                        vv = v[:, hp, :, ri, :].rearrange("p m (h d) -> p m h d", h=2)
                        w = wts[:, hp % 2, n].unsqueeze(3).broadcast_to([P, N, 2, HD])
                        o = wv[:, ri].rearrange("p m (h d) -> p m h d", h=2)
                        nc.gpsimd.tensor_tensor(o, vv, w, ALU.mult).then_inc(wv_mults, 1)
                        if beside is not None:
                            first = sum(WITH_WEIGHTED[:2 * n + ri])
                            for sl in range(first, first + WITH_WEIGHTED[2 * n + ri]):
                                low_of_s(beside + sl, sl)
                        pool.wait_ge(wv_mults, i + 1)
                        pool.wait_ge(wv_free, i + 1)
                        nc.gpsimd.tensor_tensor(wv2[:, (2 * n + ri) % N], wv[:, ri, 0:2], wv[:, ri, 2:4],
                                                ALU.add).then_inc(wv_made, 1)

            for sl in range(SL):
                low_of_s(sl, sl)
            with pool.Fori(0, BT - 1) as bt:
                for hp in range(HP):
                    weighted(bt * HP + hp, hp, beside=(bt + 1) * SL if hp == 1 else None)
            for hp in range(HP - 1):
                weighted((BT - 1) * HP + hp, hp)

        @block.vector
        def _(dve):
            dve.wait_ge(b_set, 2)
            low_part(nc.vector, bias_flat[32:33], b_raw[32:33], b_hi[32:33]).then_inc(b_split, 1)
            dve.sem_inc(qk_free, 2)
            dve.sem_inc(scores_made, 2)
            dve.sem_inc(wv_free, N)
            dve.sem_inc(wv_made, 2)
            for i in range(PIECES):
                dve.wait_ge(wq_hi_made, i + 1)
                low_part(nc.vector, piece(wq_lo, i), w_stage(i), piece(wq_hi, i)).then_inc(wq_lo_made, 1)

            def scores(u, hp, groups):
                dve.wait_ge(qk_out, (u + 1) * SL)
                for g in groups:
                    dve.wait_ge(scores_made, u * GROUPS + g + 1)
                    slot = 0
                    for nm in (2 * g, 2 * g + 1):
                        n, m = nm // N, nm % N
                        for h in range(2):
                            cols = slice(h * HD, (h + 1) * HD)
                            keys = qk[:, hp % 2, m, :, P + h * HD:P + (h + 1) * HD]
                            for q, total in ((qk[:, hp % 2, n, :, cols], ar), (qx[:, hp % 2, n, :, cols], ai)):
                                ins = nc.vector.scalar_tensor_tensor(
                                    prod[:, g % 2, slot].rearrange("p (r d) -> p r d", r=2), q, 1.0, keys,
                                    ALU.mult, ALU.mult, accum_out=total[:, nm, h:h + 1])
                                slot += 1
                    ins.then_inc(scores_made, 1)

            def chained(u, n, ins):
                ins.then_inc(small, 1)
                dve.wait_ge(small, u * SMALLS + n)

            def magnitude(u):
                m2 = mag[:].rearrange("p n m h -> p (n m) h")
                dve.wait_ge(scores_made, (u + 1) * GROUPS + 2)
                dve.sem_inc(qk_free, 1)
                nc.vector.tensor_tensor(ar[:], ar[:], ar[:], ALU.mult)
                chained(u, 1, nc.vector.tensor_tensor(ai[:], ai[:], ai[:], ALU.mult))
                chained(u, 2, nc.vector.tensor_tensor(m2, ar[:], ai[:], ALU.add))
                nc.vector.tensor_scalar(mag[:], mag[:], MAG_EPS, None, ALU.add).then_inc(sq_ready, 1)

            def less_top(u):
                dve.wait_ge(mag_made, u + 1)
                chained(u, 3, nc.vector.tensor_reduce(top[:], mag[:].rearrange("p n m h -> p n h m"), AX_X, ALU.max))
                nc.vector.tensor_tensor(ex[:], mag[:], top[:].unsqueeze(2).broadcast_to([P, N, N, 2]),
                                        ALU.subtract).then_inc(exp_ready, 1)

            def weights(u, hp):
                dve.wait_ge(exp_made, u + 1)
                chained(u, 4, nc.vector.tensor_reduce(tot[:], ex[:].rearrange("p n m h -> p n h m"), AX_X, ALU.add))
                chained(u, 5, nc.vector.reciprocal(tot[:], tot[:]))
                nc.vector.tensor_tensor(wts[:, hp % 2], ex[:], tot[:].unsqueeze(2).broadcast_to([P, N, N, 2]),
                                        ALU.mult).then_inc(wts_made, 1)

            def weighted_sums(u, hp, half, stored):
                if half == 0 and (not isinstance(stored, int) or stored > 0):
                    dve.wait_ge(o_stored[hp % 2], 16 * stored)
                for i in range(half * N, half * N + N):
                    n, ri = i // 2, i % 2
                    dve.wait_ge(wv_made, u * SL + i + 3)
                    nc.vector.tensor_tensor(out[:, hp % 2, n, ri, :], wv2[:, i % N, 0], wv2[:, i % N, 1],
                                            ALU.add).then_inc(wv_free, 1)

            def unit(bt, hp):
                u = bt * HP + hp
                begun = not isinstance(u, int)
                scores(u, hp, range(0, 2))
                if begun or u >= 1:
                    less_top(u - 1)
                if begun or u >= 2:
                    weighted_sums(u - 2, (hp - 2) % HP, 0, bt * 2 + hp // 2 - 1)
                scores(u, hp, range(2, 4))
                if begun or u >= 1:
                    weights(u - 1, (hp - 1) % HP)
                scores(u, hp, range(4, 7))
                if begun or u >= 2:
                    weighted_sums(u - 2, (hp - 2) % HP, 1, 0)
                scores(u, hp, range(7, GROUPS))
                magnitude(u)

            for hp in range(HP):
                unit(0, hp)
            with dve.Fori(1, BT) as bt:
                for hp in range(HP):
                    unit(bt, hp)
            last = BT * HP - 1
            less_top(last)
            weights(last, HP - 1)
            products = flat(qk).rearrange("p (i m h d) -> p i m h d", i=SL, m=N, h=2)
            dve.wait_ge(wts_made, last + 1)
            for i in range(SL):
                n, ri = i // 2, i % 2
                vv = v[:, HP - 1, :, ri, :].rearrange("p m (h d) -> p m h d", h=2)
                w = wts[:, (HP - 1) % 2, n].unsqueeze(3).broadcast_to([P, N, 2, HD])
                nc.vector.tensor_tensor(products[:, i], vv, w, ALU.mult).then_inc(last_made, 1)
            for half in range(2):
                weighted_sums(last - 1, HP - 2, half, 2 * BT - 1)
            dve.wait_ge(o_stored[(HP - 1) % 2], 16 * (2 * BT - 1))
            summed = flat(qk).rearrange("p (i m c) -> p i m c", i=SL, m=N)
            for i in range(SL):
                dve.wait_ge(last_made, i + 1)
                nc.vector.tensor_tensor(summed[:, i, 0:2], summed[:, i, 0:2], summed[:, i, 2:4],
                                        ALU.add).then_inc(last_made, 1)
            for i in range(SL):
                dve.wait_ge(last_made, SL + i + 1)
                nc.vector.tensor_tensor(out[:, (HP - 1) % 2, i // 2, i % 2, :], summed[:, i, 0], summed[:, i, 1],
                                        ALU.add).then_inc(wv_free, 1)

        @block.tensor
        def _(pe):
            pe.wait_ge(b_split, 1)
            pe.wait_ge(consts_set, 2)

            def unit(u, hp, bt):
                pe.wait_ge(wq_lo_made, 2 * hp + 1)
                for sl in range(SL):
                    if sl == 1:
                        pe.wait_ge(wq_lo_made, 2 * hp + 2)
                    n, ri = sl // 2, sl % 2
                    out_ps = qkv_ps[:, sl % BANKS, 0:W3]
                    if not (isinstance(u, int) and u == 0 and sl < BANKS):
                        pe.wait_ge(qk_out, u * SL + sl - BANKS + 1)
                    if hp == 0:
                        pe.wait_ge(s_lo_made, bt * SL + sl + 1)
                    nc.tensor.matmul(out_ps, ones[:], bias[:, ri, hp, :], start=True, stop=False)
                    for dt in range(DT):
                        mm = mm3(nc, out_ps, (s_hi[:, sl, dt, :], s_lo[:, sl, dt, :]),
                                 (wq_hi[:, hp, ri, dt, :], wq_lo[:, hp, ri, dt, :]), False, dt == DT - 1)
                    mm.then_inc(qkv_done, 1)

            unit(0, 0, 0)
            with pe.Fori(0, BT - 1) as bt:
                for hp in range(HP):
                    unit(bt * HP + hp + 1, (hp + 1) % HP, bt + (hp + 1) // HP)
            for hp in range(1, HP):
                unit((BT - 1) * HP + hp, hp, BT - 1)


def mixing_stage(nc, o_dram, w_o, b_o, w_int, ident_dram, r_dram, ids, tables, idx, strength):
    T, NP = 2, 2
    STEPS = BT // T
    COLS = NP * T * P
    G = NP * T
    TR_BANKS, WO_BANKS, RI_BANKS = 2, 2, 4
    RAW = 8
    RI = 3

    with ExitStack() as ctx:
        def sb(name, shape, dt):
            return ctx.enter_context(nc.sbuf_tensor(name, shape, dt))

        def sem(name):
            return ctx.enter_context(nc.semaphore(name))

        wo_hi, wo_lo = sb("wo_hi", [P, 2, DT, D], F32R), sb("wo_lo", [P, 2, DT, D], F32R)
        wi_hi, wi_lo = sb("wi_hi", [P, NP, 2, DT, D], F32R), sb("wi_lo", [P, NP, 2, DT, D], F32R)
        w_raw = sb("mix_w_raw", [P, RAW, D], F32)
        bo = sb("bo", [P, 2, DT], F32)
        ident = sb("mix_ident", [P, P], F32)
        o_raw = sb("o_raw", [P, T, NP, 2, D], F32)
        ot_hi, ot_lo = sb("ot_hi", [P, 2, DT, COLS], F32R), sb("ot_lo", [P, 2, DT, COLS], F32R)
        at_hi, at_lo = sb("at_hi", [P, 2, DT, COLS], F32R), sb("at_lo", [P, 2, DT, COLS], F32R)
        ri_out = sb("ri_out", [P, 2, 2, D], F32)

        tr_ps = ctx.enter_context(nc.psum_tensor("tr_ps", [P, TR_BANKS, COLS], F32))
        wo_ps = ctx.enter_context(nc.psum_tensor("wo_ps", [P, WO_BANKS, COLS], F32))
        ri_ps = ctx.enter_context(nc.psum_tensor("ri_ps", [P, RI_BANKS, D], F32))

        consts_in = sem("mix_consts_in")
        w_in = [sem(f"mix_w_in_{slot}") for slot in range(RAW)]
        ids_in, gathered = sem("ids_in"), sem("gathered")
        w_hi_made, w_lo_made = sem("mix_w_hi_made"), sem("mix_w_lo_made")
        o_in, transposed, ot_hi_made, ot_lo_made = (
            sem("o_in"), sem("transposed"), sem("ot_hi_made"), sem("ot_lo_made"))
        wo_done, at_hi_made, at_lo_made = sem("wo_done"), sem("at_hi_made"), sem("at_lo_made")
        ri_done, r1_out, r_out, i_out = sem("ri_done"), sem("r1_out"), sem("r_out"), sem("i_out")
        r_stored = [sem("r_stored_0"), sem("r_stored_1")]

        WO_PIECES, WI_PIECES = 2 * DT, NP * 2 * DT

        def w_piece(i):
            if i < WO_PIECES:
                return [t[:].rearrange("p a b n -> p (a b) n")[:, i] for t in (wo_hi, wo_lo)]
            return [t[:].rearrange("p a b c n -> p (a b c) n")[:, (i - WO_PIECES) % WI_PIECES]
                    for t in (wi_hi, wi_lo)]

        def w_source(i):
            if i < WO_PIECES:
                return w_o[:, i]
            return w_int[:, i - WO_PIECES]

        FIRST = WO_PIECES + WI_PIECES
        TOTAL = FIRST + WI_PIECES

        block = ctx.enter_context(nc.Block())

        @block.sync
        def _(sp):
            sp.dma_start(ident[:], ident_dram).then_inc(consts_in, 16)
            sp.dma_start(bo[:], b_o).then_inc(consts_in, 16)

            def load_o(pair, step, nth):
                if not isinstance(nth, int):
                    sp.wait_ge(transposed, nth * 2 * DT)
                for t in range(T):
                    sp.dma_start(o_raw[:, t], o_dram[step * T + t, :, pair * NP:(pair + 1) * NP]).then_inc(o_in, 16)

            def load_w(i):
                if i >= RAW:
                    sp.wait_ge(w_lo_made, i - RAW + 1)
                sp.dma_start(w_raw[:, i % RAW], w_source(i)).then_inc(w_in[i % RAW], 16)

            load_o(0, 0, 0)
            for i in range(FIRST):
                load_w(i)
            sp.dma_start(idx[:], ids).then_inc(ids_in, 16)
            with sp.Fori(1, STEPS) as step:
                load_o(0, step, step)
            for i in range(FIRST, FIRST + RAW):
                load_w(i)
            sp.wait_ge(transposed, STEPS * 2 * DT)
            load_o(1, 0, STEPS)
            for i in range(FIRST + RAW, TOTAL):
                load_w(i)
            with sp.Fori(1, STEPS) as step:
                load_o(1, step, step + STEPS)
            for slot in range(2):
                sp.wait_ge(r_stored[slot], 16 * 2 * STEPS * G // 2)

        def split_w_high(act, i):
            act.wait_ge(w_in[i % RAW], 16 * (i // RAW + 1))
            if i >= FIRST:
                groups = (i - FIRST) // (2 * DT) * T + T
                act.wait_ge(ri_done, ((STEPS - 1) * G + groups) * RI)
            nc.scalar.copy(w_piece(i)[0], w_raw[:, i % RAW]).then_inc(w_hi_made, 1)

        @block.gpsimd
        def _(pool):
            for i in range(TOTAL):
                if i == FIRST:
                    pool.wait_ge(ids_in, 16)
                    for t in range(BT):
                        for f in range(N):
                            pool.indirect_dma_start(
                                out=strength[:, t, f * N:(f + 1) * N], out_offset=None, in_=tables[f],
                                in_offset=bass.IndirectOffsetOnAxis(ap=idx[:, t, f:f + 1].bitcast(U32), axis=0),
                            ).then_inc(gathered, 16)
                pool.wait_ge(w_hi_made, i + 1)
                low_part(nc.gpsimd, w_piece(i)[1], w_raw[:, i % RAW], w_piece(i)[0]).then_inc(w_lo_made, 1)
            pool.wait_ge(gathered, 16 * BT * N)

        @block.scalar
        def _(act):
            act.wait_ge(consts_in, 32)

            def high_of_out(nth, part):
                ri, et = part // DT, part % DT
                act.wait_ge(transposed, nth * 2 * DT + part + 1)
                if not isinstance(nth, int) or nth > 0:
                    act.wait_ge(wo_done, nth * 2 * DT)
                nc.scalar.copy(ot_hi[:, ri, et], tr_ps[:, part % TR_BANKS]).then_inc(ot_hi_made, 1)

            def step_body(pair, step, pieces=(), following=True):
                nth = pair * STEPS + step
                for ri in range(2):
                    for dt in range(DT):
                        part = ri * DT + dt
                        for i in pieces[part * len(pieces) // 8:(part + 1) * len(pieces) // 8]:
                            split_w_high(act, i)
                        act.wait_ge(wo_done, nth * 2 * DT + part + 1)
                        if not isinstance(nth, int) or nth > 0:
                            act.wait_ge(ri_done, nth * G * RI)
                        nc.scalar.activation(at_hi[:, ri, dt], wo_ps[:, dt % WO_BANKS], ACT.Identity,
                                             bias=bo[:, ri, dt:dt + 1]).then_inc(at_hi_made, 1)
                for g in range(G):
                    if following:
                        high_of_out(nth + 1, 2 * g)
                        high_of_out(nth + 1, 2 * g + 1)
                    i = nth * G + g
                    slot = g % 2
                    act.wait_ge(ri_done, i * RI + 1)
                    if not isinstance(nth, int) or nth * G + g >= 2:
                        act.wait_ge(r_stored[slot], 16 * (nth * G // 2 + g // 2))
                    nc.scalar.copy(ri_out[:, slot, 0], ri_ps[:, (RI * g) % RI_BANKS]).then_inc(r1_out, 1)
                    act.wait_ge(ri_done, i * RI + 3)
                    nc.scalar.copy(ri_out[:, slot, 1], ri_ps[:, (RI * g + 2) % RI_BANKS]).then_inc(i_out, 1)
                    act.wait_ge(r_out, i + 1)
                    act.wait_ge(i_out, i + 1)
                    n, t = g // T, g % T
                    act.dma_start(r_dram[step * T + t, :, pair * NP + n], ri_out[:, slot]).then_inc(r_stored[slot], 16)

            for part in range(2 * DT):
                split_w_high(act, part)
                high_of_out(0, part)
            step_body(0, 0, range(WO_PIECES, FIRST))
            with act.Fori(1, STEPS) as step:
                step_body(0, step)
            step_body(1, 0, range(FIRST, TOTAL))
            with act.Fori(1, STEPS - 1) as step:
                step_body(1, step)
            step_body(1, STEPS - 1, following=False)

        @block.vector
        def _(dve):
            dve.wait_ge(consts_in, 32)

            def low_of_out(nth, part):
                ri, et = part // DT, part % DT
                dve.wait_ge(ot_hi_made, nth * 2 * DT + part + 1)
                low_part(nc.vector, ot_lo[:, ri, et], tr_ps[:, part % TR_BANKS], ot_hi[:, ri, et]).then_inc(ot_lo_made, 1)

            def step_body(nth, following=True):
                for ri in range(2):
                    for dt in range(DT):
                        dve.wait_ge(at_hi_made, nth * 2 * DT + ri * DT + dt + 1)
                        nc.vector.scalar_tensor_tensor(at_lo[:, ri, dt], wo_ps[:, dt % WO_BANKS],
                                                       bo[:, ri, dt:dt + 1], at_hi[:, ri, dt].bitcast(F32),
                                                       ALU.add, ALU.subtract).then_inc(at_lo_made, 1)
                for g in range(G):
                    if following:
                        low_of_out(nth + 1, 2 * g)
                        low_of_out(nth + 1, 2 * g + 1)
                    i = nth * G + g
                    dve.wait_ge(r1_out, i + 1)
                    dve.wait_ge(ri_done, i * RI + 2)
                    nc.vector.tensor_tensor(ri_out[:, g % 2, 0], ri_out[:, g % 2, 0],
                                            ri_ps[:, (RI * g + 1) % RI_BANKS], ALU.subtract).then_inc(r_out, 1)

            for part in range(2 * DT):
                low_of_out(0, part)
            with dve.Fori(0, 2 * STEPS - 1) as nth:
                step_body(nth)
            step_body(2 * STEPS - 1, following=False)

        @block.tensor
        def _(pe):
            pe.wait_ge(consts_in, 32)

            def transpose_out(nth, part):
                ri, et = part // DT, part % DT
                if part == 0:
                    for t in range(T):
                        pe.wait_ge(o_in, 16 * (nth * T + T))
                if not isinstance(nth, int) or nth * 2 * DT + part >= TR_BANKS:
                    pe.wait_ge(ot_lo_made, nth * 2 * DT + part - TR_BANKS + 1)
                for g in range(G):
                    n, t = g // T, g % T
                    tr = nc.tensor.transpose(tr_ps[:, part % TR_BANKS, g * P:(g + 1) * P],
                                             o_raw[:, t, n, ri, et * P:(et + 1) * P], ident[:])
                tr.then_inc(transposed, 1)

            def step_body(nth, pair, following=True):
                for ri in range(2):
                    for dt in range(DT):
                        i = nth * 2 * DT + ri * DT + dt
                        if not (isinstance(i, int) and i < WO_BANKS):
                            pe.wait_ge(at_lo_made, i - WO_BANKS + 1)
                        for et in range(DT):
                            if dt == 0:
                                pe.wait_ge(ot_lo_made, nth * 2 * DT + ri * DT + et + 1)
                                pe.wait_ge(w_lo_made, ri * DT + et + 1)
                            cols = slice(dt * P, (dt + 1) * P)
                            mm = mm3(nc, wo_ps[:, dt % WO_BANKS], (wo_hi[:, ri, et, cols], wo_lo[:, ri, et, cols]),
                                     (ot_hi[:, ri, et], ot_lo[:, ri, et]), et == 0, et == DT - 1)
                        mm.then_inc(wo_done, 1)
                pe.wait_ge(at_lo_made, (nth + 1) * 2 * DT)
                for g in range(G):
                    if following:
                        transpose_out(nth + 1, 2 * g)
                        transpose_out(nth + 1, 2 * g + 1)
                    n = g // T
                    cols = slice(g * P, (g + 1) * P)
                    for q, terms in enumerate([[(0, 0)], [(1, 1)], [(0, 1), (1, 0)]]):
                        bank = (RI * g + q) % RI_BANKS
                        i = nth * G + g
                        if not (isinstance(nth, int) and RI * g + q < RI_BANKS):
                            before = RI * g + q - RI_BANKS
                            bg, bq = before // RI, before % RI
                            pe.wait_ge(i_out if bq == 2 else r_out, nth * G + bg + 1)
                        for x, (a, m) in enumerate(terms):
                            for dt in range(DT):
                                if g % T == 0:
                                    pe.wait_ge(w_lo_made, WO_PIECES + pair * WI_PIECES + (n * 2 + m) * DT + dt + 1)
                                mm = mm3(nc, ri_ps[:, bank], (at_hi[:, a, dt, cols], at_lo[:, a, dt, cols]),
                                         (wi_hi[:, n, m, dt], wi_lo[:, n, m, dt]),
                                         x == 0 and dt == 0, x == len(terms) - 1 and dt == DT - 1)
                        mm.then_inc(ri_done, 1)

            for part in range(2 * DT):
                transpose_out(0, part)
            step_body(0, 0)
            with pe.Fori(1, STEPS) as step:
                step_body(step, 0)
            with pe.Fori(STEPS, 2 * STEPS - 1) as step:
                step_body(step, 1)
            step_body(2 * STEPS - 1, 1, following=False)


class Chain:

    def __init__(self, engine, semaphore, per_tile):
        self.engine, self.semaphore, self.per_tile, self.tile, self.n = engine, semaphore, per_tile, 0, 0

    def start(self, tile):
        self.tile, self.n = tile, 0

    def step(self, instruction):
        self.n += 1
        instruction.then_inc(self.semaphore, 1)
        self.engine.wait_ge(self.semaphore, self.tile * self.per_tile + self.n)


def top_stage(nc, r_dram, t_dram, strength, w_head, w_top2, head_rows, ident_dram, y_dram):
    MEAS_R, MEAS_I, POST, TOP1 = 0, DT, 2 * DT, 3 * DT
    WP = 4 * DT
    D2 = D // 2
    TINY = 2.0 ** -116
    PAIRS = [(0, 1), (0, 2), (1, 2), (0, 3), (1, 3), (2, 3)]
    NP = len(PAIRS)
    FACTORS = 3

    with ExitStack() as ctx:
        def sb(name, shape, dt):
            return ctx.enter_context(nc.sbuf_tensor(name, shape, dt))

        def sem(name):
            return ctx.enter_context(nc.semaphore(name))

        w_hi, w_lo = sb("wh_hi", [P, WP, D], F32R), sb("wh_lo", [P, WP, D], F32R)
        w2_hi, w2_lo = sb("w2_hi", [P, DT, D2], F32R), sb("w2_lo", [P, DT, D2], F32R)
        rows = sb("rows", [P, 3 * D + 2 * D2], F32)
        post_b, post_g, post_be = (rows[:, i * D:(i + 1) * D] for i in range(3))
        b_top2, w_top3 = (rows[:, 3 * D + i * D2:3 * D + (i + 1) * D2] for i in range(2))
        ident = sb("top_ident", [P, P], F32)
        diag = sb("diag", [P, 2 * NP, P], F32)
        r = sb("states", [P, 2, N, 2, D], F32)
        sq = sb("sq", [P, 2, 2, D], F32)
        inv = sb("inv", [P, N, D], F32)
        zero = sb("zero", [P, N, D], BF16)
        zeros = sb("zeros", [P, 2, D], BF16)
        unit = sb("unit", [P, N, 2, D], F32)
        pair = sb("pair", [P, 2, D], F32)
        cos = sb("cos", [P, 2, D], F32)
        factor = sb("factor", [P, FACTORS, D], F32)
        wt = sb("wt", [P, N, D], F32)
        sup = sb("sup", [P, 2, D], F32)
        st_hi, st_lo = sb("st_hi", [P, 3, DT, P], F32R), sb("st_lo", [P, 3, DT, P], F32R)
        xt_hi, xt_lo = sb("xt_hi", [P, DT, P], F32R), sb("xt_lo", [P, DT, P], F32R)
        tx = sb("tx", [P, DT, P], F32)
        msq = sb("msq", [P, 2, D], F32)
        row = sb("row", [P, D], F32)
        neg_mean = sb("neg_mean", [P, 1], F32)
        ssq, rn, rs = sb("ssq", [P, 1], F32), sb("rn", [P, 1], F32), sb("rs", [P, 1], F32)
        eps_ln = sb("eps_ln", [P, 1], F32)
        y = sb("y_sb", [P, BT], F32)

        def bank(name):
            return ctx.enter_context(nc.psum_tensor(name, [P, D], F32))

        m_ps = [bank("mr_ps"), bank("mi_ps")]
        wt_ps = [bank(f"wt_ps_{j}") for j in range(N)]
        t_ps, layer_ps = bank("t_ps"), bank("layer_ps")

        ident_in, rows_in = sem("top_ident_in"), sem("rows_in")
        eps_set = sem("eps_set")
        w_in = [sem(f"top_w_in_{stage}") for stage in range(4)]
        w_hi_made, w_lo_made = sem("top_w_hi_made"), sem("top_w_lo_made")
        r_in, tx_in = [sem("r_in_0"), sem("r_in_1")], sem("tx_in")
        sq_made, abs2_made, safe_made, abs_made, inv_made = (
            sem("sq_made"), sem("abs2_made"), sem("safe_made"), sem("abs_made"), sem("inv_made"))
        unit_made, cos_made, factor_made, wt_added = (
            sem("unit_made"), sem("cos_made"), sem("factor_made"), sem("wt_added"))
        diag_made, wt_made, wz_made, sup_made = sem("diag_made"), sem("wt_made"), sem("wz_made"), sem("sup_made")
        ssq_made, rn_made = sem("ssq_made"), sem("rn_made")
        sup_t, st_hi_made, st_lo_made = sem("sup_t"), sem("st_hi_made"), sem("st_lo_made")
        measured, msq_made, amp2_made, amp_made = sem("measured"), sem("msq_made"), sem("amp2_made"), sem("amp_made")
        row_t, xt_hi_made, xt_lo_made = sem("row_t"), sem("xt_hi_made"), sem("xt_lo_made")
        post_done, mean_made, var_made, std_made, ln_made, z_made = (
            sem("post_done"), sem("mean_made"), sem("var_made"), sem("top_std_made"), sem("ln_made"), sem("z_made"))
        top1_done, h1_made, top2_done, y_made = sem("top1_done"), sem("h1_made"), sem("top2_done"), sem("y_made")
        inverse_steps, weigh_steps, adding_steps, measure_steps, layer_steps = (
            sem("inverse_steps"), sem("weigh_steps"), sem("adding_steps"), sem("measure_steps"), sem("layer_steps"))
        y_stored = sem("y_stored")

        PIECES = WP + 2
        STAGES = 4

        def w_piece(part, i):
            if i < WP:
                return (w_hi, w_lo)[part][:, i]
            return (w2_hi, w2_lo)[part][:].rearrange("p a n -> p (a n)")[:, (i - WP) * D:(i - WP + 1) * D]

        def w_stage(i):
            return (sup, msq)[i % STAGES // 2][:, i % 2]

        def some(tile, count):
            return not isinstance(tile, int) or count > 0

        def in_steps(engine, step):
            for s in range(4):
                step(s, s % 2, True, s >= 1, s >= 2, s >= 3)
            with engine.Fori(2, BT // 2) as k:
                for slot in range(2):
                    step(2 * k + slot, slot, True, True, True, True)
            for s in range(BT, BT + 3):
                step(s, s % 2, False, s < BT + 1, s < BT + 2, True)

        block = ctx.enter_context(nc.Block())

        @block.sync
        def _(sp):
            def load_r(i, slot):
                sp.dma_start(r[:, slot], r_dram[i]).then_inc(r_in[slot], 16)

            def load_tx(i):
                if some(i, i):
                    sp.wait_ge(top1_done, i)
                src = t_dram[:, :, bass.ds(i * P, P)].rearrange("t p b -> p t b")
                sp.dma_start(tx[:], src).then_inc(tx_in, 16)

            load_r(0, 0)
            sp.dma_start(ident[:], ident_dram).then_inc(ident_in, 16)
            load_r(1, 1)
            for i in range(PIECES):
                if i >= STAGES:
                    sp.wait_ge(w_lo_made, i - STAGES + 1)
                src = w_head[:, i] if i < WP else w_top2[:, 2 * (i - WP):2 * (i - WP) + 2].rearrange("p a n -> p (a n)")
                sp.dma_start(w_stage(i), src).then_inc(w_in[i % STAGES], 16)
            sp.dma_start(rows[:], head_rows.partition_broadcast(P)).then_inc(rows_in, 16)
            load_tx(0)
            sp.wait_ge(wz_made, N)
            load_r(2, 0)
            sp.wait_ge(wz_made, 2 * N)
            load_r(3, 1)
            with sp.Fori(2, BT // 2) as k:
                for slot in range(2):
                    i = 2 * k + slot
                    sp.wait_ge(wz_made, (i - 1) * N)
                    load_r(i, slot)
                    load_tx(i - 3)
            for i in range(BT - 3, BT):
                load_tx(i)
            sp.wait_ge(y_made, BT)
            sp.dma_start(y_dram, y[:]).then_inc(y_stored, 16)
            sp.wait_ge(y_stored, 16)

        @block.gpsimd
        def _(pool):
            nc.gpsimd.memset(eps_ln[:], LN_EPS).then_inc(eps_set, 1)

            def unit_vector(i, slot, n):
                if some(i, i):
                    if n < 3:
                        pool.wait_ge(adding_steps, 2 * i - (1 if n < 2 else 0))
                    else:
                        pool.wait_ge(sup_made, i)
                pool.wait_ge(inv_made, i * N + n + 1)
                by = inv[:, n].unsqueeze(1).broadcast_to([P, 2, D])
                nc.gpsimd.tensor_tensor(unit[:, n], r[:, slot, n], by, ALU.mult).then_inc(unit_made, 1)

            def add_cosine(i, p):
                nth = i * NP + p
                if some(i, nth - FACTORS + 1):
                    pool.wait_ge(wt_added, nth - FACTORS + 1)
                pool.wait_ge(cos_made, nth + 1)
                nc.gpsimd.tensor_tensor(factor[:, p % FACTORS], zeros[:, p % 2], cos[:, p % 2],
                                        ALU.add).then_inc(factor_made, 1)

            def squares_sum(i, n):
                if some(i, i):
                    pool.wait_ge(unit_made, i * N)
                pool.wait_ge(sq_made, i * N + n + 1)
                nc.gpsimd.tensor_tensor(inv[:, n], sq[:, n % 2, 0], sq[:, n % 2, 1], ALU.add).then_inc(abs2_made, 1)

            def weighted(i, slot):
                for n in range(N):
                    pool.wait_ge(wt_made, i * N + n + 1)
                    pool.wait_ge(cos_made, (i + 1) * NP)
                    by = wt[:, n].unsqueeze(1).broadcast_to([P, 2, D])
                    nc.gpsimd.tensor_tensor(unit[:, n], r[:, slot, n], by, ALU.mult).then_inc(wz_made, 1)

            def step(s, slot, i, w, m, l):
                if w:
                    for n in range(N):
                        unit_vector(s - 1, 1 - slot, n)
                    for p in range(4):
                        add_cosine(s - 1, p)
                if i:
                    squares_sum(s, 0)
                    squares_sum(s, 1)
                if w:
                    for p in range(4, NP):
                        add_cosine(s - 1, p)
                if i:
                    squares_sum(s, 2)
                    squares_sum(s, 3)
                if w:
                    weighted(s - 1, 1 - slot)

            in_steps(pool, step)

        @block.scalar
        def _(act):
            def s_ij(i, a, b):
                return strength[:].rearrange("p t s -> p (t s)")[:, bass.ds(i * N * N + a * N + b, 1)]

            def high_of_w(pieces):
                for i in pieces:
                    act.wait_ge(w_in[i % STAGES], 16 * (i // STAGES + 1))
                    nc.scalar.copy(w_piece(0, i), w_stage(i)).then_inc(w_hi_made, 1)

            def squares(i, slot, n):
                if n == 0:
                    act.wait_ge(r_in[slot], 8 * (i - slot) + 16)
                if some(i, i * N + n - 1):
                    act.wait_ge(abs2_made, i * N + n - 1)
                nc.scalar.activation(sq[:, n % 2], r[:, slot, n], ACT.Square).then_inc(sq_made, 1)

            def root(i, n):
                act.wait_ge(safe_made, i * N + n + 1)
                nc.scalar.activation(inv[:, n], inv[:, n], ACT.Sqrt).then_inc(abs_made, 1)

            def diagonals(i):
                act.wait_ge(ident_in, 16)
                if some(i, i):
                    act.wait_ge(wt_added, i * NP)
                for p, (a, b) in enumerate(PAIRS):
                    nc.scalar.activation(diag[:, 2 * p], ident[:], ACT.Copy, scale=s_ij(i, a, b))
                    nc.scalar.activation(diag[:, 2 * p + 1], ident[:], ACT.Copy,
                                         scale=s_ij(i, b, a)).then_inc(diag_made, 1)

            def weights(i):
                act.wait_ge(wt_added, (i + 1) * NP)
                if some(i, i):
                    act.wait_ge(wz_made, i * N)
                for j in range(N):
                    nc.scalar.activation(wt[:, j], wt_ps[j][:], ACT.Identity,
                                         bias=s_ij(i, j, j)).then_inc(wt_made, 1)

            def norm(i):
                act.wait_ge(sup_made, i + 1)
                if some(i, i):
                    act.wait_ge(row_t, 3 * i - 2)
                nc.scalar.activation(msq[:].rearrange("p a n -> p (a n)"), sup[:].rearrange("p a n -> p (a n)"),
                                     ACT.Square, accum_out=ssq[:]).then_inc(ssq_made, 1)

            def sup_high(i):
                if some(i, i):
                    act.wait_ge(measured, 2 * i)
                for a, (part, scale) in enumerate([(0, 1.0), (1, 1.0), (1, -1.0)]):
                    act.wait_ge(sup_t, 2 * i + part + 1)
                    nc.scalar.activation(st_hi[:, a].rearrange("p t b -> p (t b)"), m_ps[part][:], ACT.Copy,
                                         scale=scale).then_inc(st_hi_made, 1)

            def measure_squares(i):
                for part in range(2):
                    act.wait_ge(measured, 2 * i + part + 1)
                    act.wait_ge(ssq_made, i + 1)
                    nc.scalar.activation(msq[:, part], m_ps[part][:], ACT.Square).then_inc(msq_made, 1)

            def amplitude(i):
                act.wait_ge(amp2_made, i + 1)
                act.wait_ge(rn_made, i + 1)
                nc.scalar.activation(msq[:, 0], msq[:, 0], ACT.Sqrt, scale=rn[:]).then_inc(amp_made, 1)

            def row_high(i, nth):
                act.wait_ge(row_t, 3 * i + nth + 1)
                if some(i, i + nth):
                    act.wait_ge((top2_done, post_done, top1_done)[nth], i if nth == 0 else i + 1)
                nc.scalar.copy(xt_hi[:].rearrange("p t b -> p (t b)"), t_ps[:]).then_inc(xt_hi_made, 1)

            def post_root(i):
                act.wait_ge(mean_made, i + 1)
                nc.scalar.activation(t_ps[:], row[:], ACT.Square, bias=neg_mean[:], accum_out=rs[:]).then_inc(var_made, 1)
                act.wait_ge(var_made, i + 1)
                nc.scalar.activation(rs[:], rs[:], ACT.Sqrt, bias=eps_ln[:], scale=1.0 / D).then_inc(std_made, 1)

            def post_gelu(i):
                act.wait_ge(ln_made, i + 1)
                nc.scalar.activation(row[:], row[:], ACT.Gelu).then_inc(z_made, 1)

            def top1_relu(i):
                act.wait_ge(top1_done, i + 1)
                nc.scalar.activation(row[:], layer_ps[:], ACT.Relu).then_inc(h1_made, 1)

            def step(s, slot, i, w, m, l):
                if m:
                    norm(s - 2)
                    sup_high(s - 2)
                if w:
                    diagonals(s - 1)
                if isinstance(s, int) and s == 1:
                    high_of_w(range(PIECES // 2))
                if i:
                    squares(s, slot, 0)
                    squares(s, slot, 1)
                if l:
                    post_root(s - 3)
                    post_gelu(s - 3)
                    row_high(s - 3, 1)
                if i:
                    squares(s, slot, 2)
                    squares(s, slot, 3)
                if m:
                    measure_squares(s - 2)
                    amplitude(s - 2)
                if isinstance(s, int) and s == 1:
                    high_of_w(range(PIECES // 2, PIECES))
                if i:
                    root(s, 0)
                    root(s, 1)
                if w:
                    weights(s - 1)
                if l:
                    top1_relu(s - 3)
                    row_high(s - 3, 2)
                if i:
                    root(s, 2)
                    root(s, 3)
                if m:
                    row_high(s - 2, 0)

            act.wait_ge(eps_set, 1)
            in_steps(act, step)

        @block.vector
        def _(dve):
            inverse = Chain(dve, inverse_steps, N)
            weigh = Chain(dve, weigh_steps, NP)
            adding = Chain(dve, adding_steps, 2)
            measure = Chain(dve, measure_steps, 1)
            layers = Chain(dve, layer_steps, 5)

            def low_of_w(pieces):
                for i in pieces:
                    dve.wait_ge(w_hi_made, i + 1)
                    low_part(nc.vector, w_piece(1, i), w_stage(i), w_piece(0, i)).then_inc(w_lo_made, 1)

            def safe(i, n):
                if n == 0:
                    inverse.start(i)
                    if some(i, i):
                        dve.wait_ge(factor_made, i * NP)
                dve.wait_ge(abs2_made, i * N + n + 1)
                inverse.step(nc.vector.tensor_scalar(zero[:, n], inv[:, n], TINY, None, ALU.is_le))
                nc.vector.tensor_tensor(inv[:, n], inv[:, n], zero[:, n], ALU.add).then_inc(safe_made, 1)

            def reciprocal(i, n):
                dve.wait_ge(abs_made, i * N + n + 1)
                nc.vector.reciprocal(inv[:, n], inv[:, n]).then_inc(inv_made, 1)

            def cosine(i, p):
                if p == 0:
                    weigh.start(i)
                a, b = PAIRS[p]
                nth = i * NP + p
                if some(i, nth - 1):
                    dve.wait_ge(factor_made, nth - 1)
                nc.vector.tensor_tensor(zeros[:, p % 2], zero[:, a], zero[:, b], ALU.add)
                dve.wait_ge(unit_made, i * N + b + 1)
                if some(i, nth):
                    dve.wait_ge(cos_made, nth)
                weigh.step(nc.vector.tensor_tensor(pair[:], unit[:, a], unit[:, b], ALU.mult))
                nc.vector.tensor_tensor(cos[:, p % 2], pair[:, 0], pair[:, 1], ALU.add).then_inc(cos_made, 1)

            def sum_states(i):
                adding.start(i)
                dve.wait_ge(wz_made, i * N + 2)
                if some(i, i):
                    dve.wait_ge(sup_t, 2 * i)
                    dve.wait_ge(ssq_made, i)
                adding.step(nc.vector.tensor_tensor(sup[:], unit[:, 0], unit[:, 1], ALU.add))

            def sum_rest(i):
                dve.wait_ge(wz_made, i * N + 3)
                adding.step(nc.vector.tensor_tensor(sup[:], sup[:], unit[:, 2], ALU.add))
                dve.wait_ge(wz_made, i * N + 4)
                nc.vector.tensor_tensor(sup[:], sup[:], unit[:, 3], ALU.add).then_inc(sup_made, 1)

            def norm_inverse(i):
                measure.start(i)
                dve.wait_ge(ssq_made, i + 1)
                if some(i, i):
                    dve.wait_ge(amp_made, i)
                measure.step(nc.vector.tensor_scalar(rn[:], ssq[:], MAG_EPS, None, ALU.add))
                nc.vector.reciprocal(rn[:], rn[:]).then_inc(rn_made, 1)

            def sup_low(i):
                for a, part in enumerate((0, 1, 1)):
                    dve.wait_ge(st_hi_made, 3 * i + (1 if a == 0 else 3))
                    lo, hi = (t[:, a].rearrange("p t b -> p (t b)") for t in (st_lo, st_hi))
                    if a < 2:
                        low_part(nc.vector, lo, m_ps[part][:], hi).then_inc(st_lo_made, 1)
                    else:
                        nc.vector.scalar_tensor_tensor(lo, m_ps[part][:], -1.0, hi.bitcast(F32),
                                                       ALU.mult, ALU.subtract).then_inc(st_lo_made, 1)

            def amplitude2(i):
                dve.wait_ge(msq_made, 2 * i + 2)
                nc.vector.tensor_tensor(msq[:, 0], msq[:, 0], msq[:, 1], ALU.add).then_inc(amp2_made, 1)

            def row_low(i, nth):
                dve.wait_ge(xt_hi_made, 3 * i + nth + 1)
                lo, hi = (t[:].rearrange("p t b -> p (t b)") for t in (xt_lo, xt_hi))
                low_part(nc.vector, lo, t_ps[:], hi).then_inc(xt_lo_made, 1)

            def post_stats(i):
                layers.start(i)
                dve.wait_ge(rows_in, 16)
                dve.wait_ge(post_done, i + 1)
                layers.step(nc.vector.scalar_tensor_tensor(row[:], layer_ps[:], 0.0, post_b, ALU.add, ALU.add,
                                                           accum_out=neg_mean[:]))
                nc.vector.tensor_scalar(neg_mean[:], neg_mean[:], -1.0 / D, None, ALU.mult).then_inc(mean_made, 1)

            def post_norm(i):
                dve.wait_ge(std_made, i + 1)
                layers.step(nc.vector.reciprocal(rs[:], rs[:]))
                layers.step(nc.vector.tensor_scalar(row[:], row[:], neg_mean[:, 0:1], rs[:, 0:1],
                                                    ALU.add, ALU.mult))
                layers.step(nc.vector.tensor_tensor(row[:], row[:], post_g, ALU.mult))
                nc.vector.tensor_tensor(row[:], row[:], post_be, ALU.add).then_inc(ln_made, 1)

            def last_layer(i):
                dve.wait_ge(top2_done, i + 1)
                h2 = row[:, 0:D2]
                layers.step(nc.vector.tensor_tensor(h2, layer_ps[:, 0:D2], b_top2, ALU.add))
                nc.vector.scalar_tensor_tensor(h2, h2, 0.0, w_top3, ALU.max, ALU.mult,
                                               accum_out=y[:, bass.ds(i, 1)]).then_inc(y_made, 1)

            def step(s, slot, i, w, m, l):
                if m:
                    norm_inverse(s - 2)
                    sup_low(s - 2)
                if w:
                    cosine(s - 1, 0)
                    cosine(s - 1, 1)
                if l:
                    post_stats(s - 3)
                if w:
                    cosine(s - 1, 2)
                    cosine(s - 1, 3)
                if l:
                    post_norm(s - 3)
                if isinstance(s, int) and s == 1:
                    low_of_w(range(PIECES // 2))
                if w:
                    cosine(s - 1, 4)
                    cosine(s - 1, 5)
                if l:
                    row_low(s - 3, 1)
                if isinstance(s, int) and s == 1:
                    low_of_w(range(PIECES // 2, PIECES))
                if m:
                    amplitude2(s - 2)
                if i:
                    for n in range(N):
                        safe(s, n)
                    reciprocal(s, 0)
                    reciprocal(s, 1)
                if l:
                    row_low(s - 3, 2)
                if w:
                    sum_states(s - 1)
                if i:
                    reciprocal(s, 2)
                if l:
                    last_layer(s - 3)
                if m:
                    row_low(s - 2, 0)
                if w:
                    sum_rest(s - 1)
                if i:
                    reciprocal(s, 3)

            in_steps(dve, step)

        @block.tensor
        def _(pe):
            pe.wait_ge(ident_in, 16)
            xt = (xt_hi[:], xt_lo[:])

            def transposes(to, of):
                for t in range(DT):
                    tr = nc.tensor.transpose(to[:, t * P:(t + 1) * P], of[:, t * P:(t + 1) * P], ident[:])
                return tr

            def product(out, of, first, start=True, stop=True, **more):
                for t in range(DT):
                    mm = mm3(nc, out, (of[0][:, t], of[1][:, t]), (w_hi[:, first + t], w_lo[:, first + t]),
                             start and t == 0, stop and t == DT - 1, **more)
                return mm

            def row_transposed(i, nth):
                pe.wait_ge((amp_made, z_made, h1_made)[nth], i + 1)
                if some(i, 3 * i + nth):
                    pe.wait_ge(xt_lo_made, 3 * i + nth)
                transposes(t_ps, msq[:, 0] if nth == 0 else row).then_inc(row_t, 1)

            def add_weights(i, p):
                pe.wait_ge(diag_made, i * NP + p + 1)
                if p == 0 and some(i, i):
                    pe.wait_ge(wt_made, i * N)
                pe.wait_ge(factor_made, i * NP + p + 1)
                a, b = PAIRS[p]
                for d, j in ((2 * p, b), (2 * p + 1, a)):
                    with_j = [q for q in range(NP) if j in PAIRS[q]]
                    mm = nc.tensor.matmul(wt_ps[j][:], diag[:, d], factor[:, p % FACTORS],
                                          start=p == with_j[0], stop=p == with_j[-1])
                mm.then_inc(wt_added, 1)

            def sup_transposed(i):
                pe.wait_ge(sup_made, i + 1)
                if some(i, i):
                    pe.wait_ge(msq_made, 2 * i)
                for part in range(2):
                    transposes(m_ps[part], sup[:, part]).then_inc(sup_t, 1)

            def measurement(i, part):
                pe.wait_ge(w_lo_made, PIECES)
                pe.wait_ge(st_lo_made, 3 * i + 3)
                terms = (((0, MEAS_R), (2, MEAS_I)), ((0, MEAS_I), (1, MEAS_R)))[part]
                for x, (a, first) in enumerate(terms):
                    mm = product(m_ps[part][:], (st_hi[:, a], st_lo[:, a]), first, start=x == 0, stop=x == 1)
                mm.then_inc(measured, 1)

            def post(i):
                pe.wait_ge(xt_lo_made, 3 * i + 1)
                if some(i, i):
                    pe.wait_ge(y_made, i)
                product(layer_ps[:], xt, POST).then_inc(post_done, 1)

            def top1(i):
                pe.wait_ge(xt_lo_made, 3 * i + 2)
                pe.wait_ge(mean_made, i + 1)
                product(layer_ps[:], xt, TOP1, skip_group_check=True)
                pe.wait_ge(tx_in, 16 * (i + 1))
                for t in range(DT):
                    mm = nc.tensor.matmul(layer_ps[:, t * P:(t + 1) * P], tx[:, t], ident[:],
                                          start=False, stop=True, skip_group_check=True)
                mm.then_inc(top1_done, 1)

            def top2(i):
                pe.wait_ge(xt_lo_made, 3 * i + 3)
                pe.wait_ge(h1_made, i + 1)
                for t in range(DT):
                    mm = mm3(nc, layer_ps[:, 0:D2], (xt[0][:, t], xt[1][:, t]), (w2_hi[:, t], w2_lo[:, t]),
                             t == 0, t == DT - 1)
                mm.then_inc(top2_done, 1)

            def step(s, slot, i, w, m, l):
                if m:
                    sup_transposed(s - 2)
                    measurement(s - 2, 0)
                if w:
                    add_weights(s - 1, 0)
                if m:
                    measurement(s - 2, 1)
                if l:
                    row_transposed(s - 3, 1)
                if w:
                    add_weights(s - 1, 1)
                    add_weights(s - 1, 2)
                    add_weights(s - 1, 3)
                    add_weights(s - 1, 4)
                    add_weights(s - 1, 5)
                if l:
                    top1(s - 3)
                    row_transposed(s - 3, 2)
                    top2(s - 3)
                if m:
                    row_transposed(s - 2, 0)
                    post(s - 2)

            in_steps(pe, step)


def recurrent_tower(nc, xT, w_enc, enc_vec, b_top1, w_qkv, b_qkv, w_o, b_o, w_int, ident, w_head, w_top2,
                    head_rows, ids, tbl_0, tbl_1, tbl_2, tbl_3, y):
    s = nc.dram_tensor("s_both", (2, FT, P, B), F32).ap()
    x_top = nc.dram_tensor("x_top", (DT, P, B), F32).ap()
    attended = nc.dram_tensor("attended", (BT, P, N, 2, D), F32).ap()
    mixed = nc.dram_tensor("mixed", (BT, P, N, 2, D), F32).ap()
    encoder_stage(nc, xT, w_enc, enc_vec, b_top1, s, x_top)
    attention_stage(nc, s, w_qkv, b_qkv, attended)
    with (nc.sbuf_tensor("idx", [P, BT, N], mybir.dt.int32) as idx,
          nc.sbuf_tensor("strength", [P, BT, N * N], F32) as strength):
        mixing_stage(nc, attended, w_o, b_o, w_int, ident, mixed, ids, [tbl_0, tbl_1, tbl_2, tbl_3], idx, strength)
        top_stage(nc, mixed, x_top, strength, w_head, w_top2, head_rows, ident, y)


def _layouts(inputs):
    given = {name.replace("L0_rec_", ""): np.asarray(a) for name, a in inputs.items()}

    def encoder_chunks(w):
        return w.reshape(FT, P, 2, FT // 2, P).transpose(0, 2, 4, 3, 1).reshape(2 * FT, P, FT // 2, P)

    w_top1 = given["W_top1"]
    top_chunks = w_top1[D:].reshape(2, FT // 2, P, DT, P).transpose(3, 0, 2, 1, 4).reshape(2 * DT, P, FT // 2, P)
    qkv = [np.stack([given[f"W{q}_{part}"].T.reshape(DT, P, HP, P) for q in "qkv"], axis=3) for part in "ri"]
    int_w = np.stack([given["int_Wr"], given["int_Wi"]], axis=1).transpose(3, 0, 1, 2).reshape(DT, P, N, 2, D)
    return {
        "xT": given["r_x"].reshape(HALVES, HB, FT, P).transpose(0, 3, 2, 1),
        "w_enc": np.concatenate([encoder_chunks(given["er_W1"]), top_chunks, encoder_chunks(given["ei_W1"]),
                                 encoder_chunks(given["er_W2"]), encoder_chunks(given["ei_W2"])]),
        "enc_vec": np.stack([given[e + v].reshape(FT, P).T for v in ("_b1", "_g1", "_be1", "_b2")
                             for e in ("er", "ei")], axis=1),
        "b_top1": given["b_top1"].reshape(DT, P).T,
        "w_qkv": np.stack(qkv, axis=2).reshape(DT, P, 2, HP, 3 * P).transpose(1, 3, 2, 0, 4).reshape(P, -1),
        "b_qkv": np.stack([np.stack([given[f"b{q}_{part}"].reshape(HP, P) for q in "qkv"], axis=1)
                           for part in "ri"]).reshape(-1),
        "w_o": np.stack([given["Wo_" + part].T.reshape(DT, P, D).transpose(1, 0, 2) for part in "ri"],
                        axis=1).reshape(P, 2 * DT, D),
        "b_o": np.stack([given["bo_" + part].reshape(DT, P).T for part in "ri"], axis=1),
        "w_int": int_w.transpose(1, 2, 3, 0, 4).reshape(P, N * 2 * DT, D),
        "ident": np.eye(P, dtype=np.float32),
        "w_head": np.concatenate([given["meas_Mr"].T, given["meas_Mi"].T, given["post_W"].T, w_top1[:D]])
                    .reshape(4 * DT, P, D).transpose(1, 0, 2),
        "w_top2": given["W_top2"].reshape(DT, P, D // 2).transpose(1, 0, 2),
        "head_rows": np.concatenate([given["post_b"], given["post_g"], given["post_be"], given["b_top2"],
                                     given["W_top3"][:, 0]]),
        "ids": given["ids"].reshape(BT, P, N).transpose(1, 0, 2),
        "tbl_0": given["tbl_0"], "tbl_1": given["tbl_1"], "tbl_2": given["tbl_2"], "tbl_3": given["tbl_3"],
    }


def kernel(**inputs):
    import concourse.bacc as _bacc
    from concourse.bass_utils import run_bass_kernel_spmd as _run

    nc = _bacc.Bacc("TRN2", target_bir_lowering=False, num_devices=1)
    arrays = {name: np.ascontiguousarray(a) for name, a in _layouts(inputs).items()}
    args = [nc.dram_tensor(name, a.shape, mybir.dt.from_np(a.dtype), kind="ExternalInput").ap()
            for name, a in arrays.items()]
    y = nc.dram_tensor("y", (P, BT), F32, kind="ExternalOutput").ap()
    recurrent_tower(nc, *args, y)
    results = _run(nc, [arrays], core_ids=[0])
    return results.results[0]["y"].T.reshape(B, 1)
```
